# Optimizing a Trainium2 kernel written in Bass

```python
import numpy as np
import jax
import jax.numpy as jnp

def _softmax(x, axis=-1):
    return jax.nn.softmax(x, axis=axis)

def _gelu(x):
    return jax.nn.gelu(x, approximate=True)

def _silu(x):
    return jax.nn.silu(x)

def _sigmoid(x):
    return jax.nn.sigmoid(x)

def _layernorm(x, axis=-1, eps=1e-05):
    m = jnp.mean(x, axis=axis, keepdims=True)
    v = jnp.var(x, axis=axis, keepdims=True)
    return (x - m) / jnp.sqrt(v + eps)

def _scatter_add(tgt, idx, src, axis=0):
    return tgt.at[idx].add(src)

def _segment_sum(src, seg, n):
    return jax.ops.segment_sum(src, seg, n)
kernel_name = 'mk_prb_d4_jaxref_r8_0833a0'

def setup_inputs(seed: int=0):
    np.random.seed(seed)
    _w = jnp.asarray

    def _L0_attn_setup():
        import jax, jax.numpy as jnp
        import numpy as np
        N_HEADS = 16
        key = jax.random.key(seed)
        ks = jax.random.split(key, 9)
        B, S, D = (2, 256, 256)
        s = 0.02
        return {'X': jax.random.normal(ks[0], (B, S, D), jnp.float32), 'Wq': jax.random.normal(ks[1], (D, D), jnp.float32) * s, 'bq': jax.random.normal(ks[2], (D,), jnp.float32) * s, 'Wk': jax.random.normal(ks[3], (D, D), jnp.float32) * s, 'bk': jax.random.normal(ks[4], (D,), jnp.float32) * s, 'Wv': jax.random.normal(ks[5], (D, D), jnp.float32) * s, 'bv': jax.random.normal(ks[6], (D,), jnp.float32) * s, 'Wo': jax.random.normal(ks[7], (D, D), jnp.float32) * s, 'bo': jax.random.normal(ks[8], (D,), jnp.float32) * s}
    _L0_attn_in = _L0_attn_setup()

    def _L0_ffn_setup():
        import jax, jax.numpy as jnp
        import numpy as np
        DIM = 256
        INTER = 176
        E = 16
        TOPK = 4
        G = 4
        TOPK_G = 2
        N_SHARED = 2
        SHARED_INTER = N_SHARED * INTER
        ROUTE_SCALE = 1.0

        def _moe_forward(x, Wg, W1, W3, W2, Ws1, Ws3, Ws2):
            B, S, D = x.shape
            xt = x.reshape(-1, D)
            T = xt.shape[0]
            scores = jax.nn.softmax(xt @ Wg.T, axis=-1)
            sg = scores.reshape(T, G, E // G)
            group_scores = sg.max(axis=-1)
            gidx = jax.lax.top_k(group_scores, TOPK_G)[1]
            gmask = jax.nn.one_hot(gidx, G, dtype=jnp.float32).sum(axis=1) > 0
            masked = jnp.where(gmask[:, :, None], sg, -jnp.inf).reshape(T, E)
            topi = jax.lax.top_k(masked, TOPK)[1]
            weights = jnp.take_along_axis(scores, topi, axis=1) * ROUTE_SCALE
            combine = jnp.zeros((T, E), xt.dtype).at[jnp.arange(T)[:, None], topi].add(weights)
            h = jax.nn.silu(jnp.einsum('td,eid->eti', xt, W1)) * jnp.einsum('td,eid->eti', xt, W3)
            expert_out = jnp.einsum('eti,edi->etd', h, W2)
            y = jnp.einsum('etd,te->td', expert_out, combine)
            z = jax.nn.silu(xt @ Ws1.T) * (xt @ Ws3.T) @ Ws2.T
            return (y + z).reshape(B, S, D)
        key = jax.random.key(seed)
        ks = jax.random.split(key, 8)
        s = 0.02
        x = jax.random.normal(ks[0], (1, 256, DIM), dtype=jnp.float32)
        Wg = jax.random.normal(ks[1], (E, DIM), dtype=jnp.float32) * s
        W1 = jax.random.normal(ks[2], (E, INTER, DIM), dtype=jnp.float32) * s
        W3 = jax.random.normal(ks[3], (E, INTER, DIM), dtype=jnp.float32) * s
        W2 = jax.random.normal(ks[4], (E, DIM, INTER), dtype=jnp.float32) * s
        Ws1 = jax.random.normal(ks[5], (SHARED_INTER, DIM), dtype=jnp.float32) * s
        Ws3 = jax.random.normal(ks[6], (SHARED_INTER, DIM), dtype=jnp.float32) * s
        Ws2 = jax.random.normal(ks[7], (DIM, SHARED_INTER), dtype=jnp.float32) * s
        return {'x': x, 'Wg': Wg, 'W1': W1, 'W3': W3, 'W2': W2, 'Ws1': Ws1, 'Ws3': Ws3, 'Ws2': Ws2}
    _L0_ffn_in = _L0_ffn_setup()

    def _L1_attn_setup():
        import jax, jax.numpy as jnp
        import numpy as np
        HID, H, KV, D = (256, 16, 4, 128)
        ROPE_THETA = 10000.0
        GATE_NORM = 16.0

        def _rope_cos_sin(n, d, dtype=jnp.float32):
            inv_freq = 1.0 / ROPE_THETA ** (jnp.arange(0, d, 2, dtype=jnp.float32) / d)
            freqs = jnp.arange(n, dtype=jnp.float32)[:, None] * inv_freq[None, :]
            cos = jnp.cos(freqs).astype(dtype)[None, :, None, :]
            sin = jnp.sin(freqs).astype(dtype)[None, :, None, :]
            return (cos, sin)

        def _apply_rotary(x, cos, sin):
            x1, x2 = jnp.split(x, 2, axis=-1)
            return jnp.concatenate([x1 * cos - x2 * sin, x2 * cos + x1 * sin], axis=-1)

        def _forward(hidden_states, Wq, Wk, Wv, Wo):
            b, n, _ = hidden_states.shape
            groups = H // KV
            q = hidden_states @ Wq
            k = hidden_states @ Wk
            v = hidden_states @ Wv
            g = k
            q = q.reshape(b, n, H, D)
            k = k.reshape(b, n, KV, D)
            v = v.reshape(b, n, KV, D)
            g = g.reshape(b, n, KV, D)
            k = jnp.repeat(k, groups, axis=2)
            v = jnp.repeat(v, groups, axis=2)
            g = jnp.repeat(g, groups, axis=2)
            sq, sk, sv = (q, k, v)
            qs = jax.nn.softmax(q.astype(jnp.float32), axis=-1)
            ks = jax.nn.softmax(k.astype(jnp.float32), axis=-1)
            gl = jax.nn.log_sigmoid(g.astype(jnp.float32)) / GATE_NORM
            cos, sin = _rope_cos_sin(n, D)
            sq = _apply_rotary(sq, cos, sin)
            sk = _apply_rotary(sk, cos, sin)

            def step(S, inp):
                q_t, k_t, v_t, g_t = inp
                S = S * jnp.exp(g_t)[..., None] + k_t[..., None] * v_t[..., None, :]
                o_t = jnp.einsum('bhk,bhkv->bhv', q_t, S)
                return (S, o_t)
            xs = tuple((jnp.moveaxis(a, 1, 0) for a in (qs, ks, v, gl)))
            S0 = jnp.zeros((b, H, D, D), dtype=jnp.float32)
            _, o_gla = jax.lax.scan(step, S0, xs)
            o_gla = jnp.moveaxis(o_gla, 0, 1)
            scale = D ** (-0.5)
            scores = jnp.einsum('bqhd,bkhd->bhqk', sq, sk) * scale
            causal = jnp.tril(jnp.ones((n, n), dtype=bool))
            scores = jnp.where(causal[None, None], scores, jnp.finfo(scores.dtype).min)
            attn = jax.nn.softmax(scores, axis=-1)
            y = jnp.einsum('bhqk,bkhd->bqhd', attn, sv)
            o = 0.5 * y + 0.5 * o_gla
            o = o.reshape(b, n, H * D).astype(hidden_states.dtype)
            return o @ Wo
        key = jax.random.key(seed)
        k1, k2, k3, k4, k5 = jax.random.split(key, 5)
        s = 0.02
        return {'hidden_states': jax.random.normal(k1, (1, 256, HID), dtype=jnp.float32), 'Wq': jax.random.normal(k2, (HID, H * D), dtype=jnp.float32) * s, 'Wk': jax.random.normal(k3, (HID, KV * D), dtype=jnp.float32) * s, 'Wv': jax.random.normal(k4, (HID, KV * D), dtype=jnp.float32) * s, 'Wo': jax.random.normal(k5, (H * D, HID), dtype=jnp.float32) * s}
    _L1_attn_in = _L1_attn_setup()

    def _L1_ffn_setup():
        import jax, jax.numpy as jnp
        import numpy as np
        HIDDEN = 256
        INTER = 1024
        BATCH, LOCAL_SEQ = (2, 512)
        key = jax.random.key(seed)
        k1, k2, k3 = jax.random.split(key, 3)
        h_shard = jax.random.normal(k1, (BATCH, LOCAL_SEQ, HIDDEN), dtype=jnp.float32)
        w_gate_up = jax.random.normal(k2, (2 * INTER, HIDDEN), dtype=jnp.float32) * 0.02
        w_down = jax.random.normal(k3, (HIDDEN, INTER), dtype=jnp.float32) * 0.02
        return {'h_shard': h_shard, 'w_gate_up': w_gate_up, 'w_down': w_down}
    _L1_ffn_in = _L1_ffn_setup()

    def _L2_attn_setup():
        import jax, jax.numpy as jnp
        import numpy as np
        from jax import lax
        B, N, D = (4, 512, 256)
        E = 128
        H = D // E
        CHUNK = 64
        EPS = 1e-06

        def rmsnorm(x, w):
            var = jnp.mean(jnp.square(x), axis=-1, keepdims=True)
            return x * lax.rsqrt(var + EPS) * w

        def chunked_gla(q, v, log_f):
            b, n, h, e = q.shape
            nc = n // CHUNK
            k = 1.0 - jnp.exp(log_f)

            def to_chunks(t):
                return t.reshape(b, nc, CHUNK, h, e).transpose(1, 0, 2, 3, 4)
            qs, ks_, vs, lfs = map(to_chunks, (q, k, v, log_f))
            A = jnp.cumsum(lfs, axis=2)
            mask = jnp.tril(jnp.ones((CHUNK, CHUNK), dtype=bool))

            def step(S, xs):
                qc, kc, vc, Ac = xs
                q_dec = qc * jnp.exp(Ac)
                k_dec = kc * jnp.exp(-Ac)
                scores = jnp.einsum('bthe,bshe->bhts', q_dec, k_dec)
                scores = jnp.where(mask[None, None], scores, 0.0)
                o_intra = jnp.einsum('bhts,bshe->bthe', scores, vc)
                o_inter = jnp.einsum('bthe,bhef->bthf', q_dec, S)
                A_last = Ac[:, -1]
                k_rem = kc * jnp.exp(A_last[:, None] - Ac)
                S_new = jnp.exp(A_last)[..., None] * S + jnp.einsum('bthe,bthf->bhef', k_rem, vc)
                return (S_new, o_intra + o_inter)
            S0 = jnp.zeros((b, h, e, e), dtype=q.dtype)
            _, o = lax.scan(step, S0, (qs, ks_, vs, A))
            return o.transpose(1, 0, 2, 3, 4).reshape(b, n, h, e)
        key = jax.random.key(seed)
        ks = jax.random.split(key, 6)
        std = 0.02
        x = jax.random.normal(ks[0], (B, N, D), dtype=jnp.float32)
        Wq = jax.random.normal(ks[1], (D, D), dtype=jnp.float32) * std
        Wk = jax.random.normal(ks[2], (D, D), dtype=jnp.float32) * std
        Wv = jax.random.normal(ks[3], (D, D), dtype=jnp.float32) * std
        Wo = jax.random.normal(ks[4], (D, D), dtype=jnp.float32) * std
        norm_w = jnp.ones((D,), dtype=jnp.float32)
        return {'x': x, 'Wq': Wq, 'Wk': Wk, 'Wv': Wv, 'Wo': Wo, 'norm_w': norm_w}
    _L2_attn_in = _L2_attn_setup()

    def _L2_ffn_setup():
        import jax, jax.numpy as jnp
        import numpy as np
        H = 256
        I = 128
        E = 32
        K = 4
        N_SHARED = 1
        EPS = 1e-06

        def _rmsnorm(x, w, eps=EPS):
            var = jnp.mean(jnp.square(x), axis=-1, keepdims=True)
            return x * jax.lax.rsqrt(var + eps) * w

        def _moe_core(x, gate_w, w13, w2):
            T = x.shape[0]
            N = T * K
            C = 2 * N // E
            logits = jnp.einsum('th,eh->te', x.astype(jnp.float32), gate_w.astype(jnp.float32))
            scores = jax.nn.softmax(logits, axis=-1)
            topk_w, topk_ids = jax.lax.top_k(scores, K)
            topk_w = topk_w / jnp.sum(topk_w, axis=-1, keepdims=True)
            flat_ids = topk_ids.reshape(-1)
            flat_w = topk_w.reshape(-1)
            order = jnp.argsort(flat_ids)
            sorted_eid = flat_ids[order]
            tok = order // K
            counts = jnp.zeros((E,), jnp.int32).at[flat_ids].add(1)
            starts = jnp.cumsum(counts) - counts
            pos = jnp.arange(N) - starts[sorted_eid]
            buf = jnp.zeros((E, C, x.shape[1]), x.dtype).at[sorted_eid, pos].set(x[tok], mode='drop')
            gu = jnp.einsum('ech,ehf->ecf', buf, w13)
            g, u = jnp.split(gu, 2, axis=-1)
            act = jax.nn.silu(g) * u
            eo = jnp.einsum('eci,eih->ech', act, w2)
            out_slots = eo[sorted_eid, pos]
            routed = jnp.zeros_like(x).at[tok].add(out_slots * flat_w[order][:, None])
            return routed
        key = jax.random.key(seed)
        ks = jax.random.split(key, 8)
        s = 1.0 / np.sqrt(H)
        si = 1.0 / np.sqrt(I)
        return {'hidden_states': jax.random.normal(ks[0], (1, 512, H), jnp.float32), 'norm_w': jnp.ones((H,), jnp.float32), 'gate_w': jax.random.normal(ks[1], (E, H), jnp.float32) * s, 'w13': jax.random.normal(ks[2], (E, H, 2 * I), jnp.float32) * s, 'w2': jax.random.normal(ks[3], (E, I, H), jnp.float32) * si, 'shared_gate_w': jax.random.normal(ks[4], (H, I * N_SHARED), jnp.float32) * s, 'shared_up_w': jax.random.normal(ks[5], (H, I * N_SHARED), jnp.float32) * s, 'shared_down_w': jax.random.normal(ks[6], (I * N_SHARED, H), jnp.float32) * si}
    _L2_ffn_in = _L2_ffn_setup()

    def _L3_attn_setup():
        import jax, jax.numpy as jnp
        import numpy as np
        B, S, D, H = (4, 256, 256, 16)
        DK = D // H
        key = jax.random.key(seed)
        ks = jax.random.split(key, 9)

        def xavier(k, shape):
            fan_in, fan_out = (shape[1], shape[0])
            limit = (6.0 / (fan_in + fan_out)) ** 0.5
            return jax.random.uniform(k, shape, jnp.float32, -limit, limit)
        return {'x': jax.random.normal(ks[0], (B, S, D), jnp.float32), 'Wq': xavier(ks[1], (D, D)), 'bq': jnp.zeros((D,), jnp.float32), 'Wk': xavier(ks[2], (D, D)), 'bk': jnp.zeros((D,), jnp.float32), 'Wv': xavier(ks[3], (D, D)), 'bv': jnp.zeros((D,), jnp.float32), 'Wo': xavier(ks[4], (D, D)), 'bo': jnp.zeros((D,), jnp.float32)}
    _L3_attn_in = _L3_attn_setup()

    def _L3_ffn_setup():
        import jax, jax.numpy as jnp
        import numpy as np
        B, T, D = (1, 256, 256)
        E, K, F = (64, 4, 64)
        S, SF = (2, 64 * 4)
        CAP = 32

        def _moe_forward(x, router_w, router_bias, gate_w, up_w, down_w, sh_gate_w, sh_up_w, sh_down_w):
            b, t, d = x.shape
            flat = x.reshape(b * t, d)
            N = flat.shape[0]
            logits = flat @ router_w.T
            scores = jax.nn.softmax(logits, axis=-1)
            _, topk_idx = jax.lax.top_k(logits + router_bias, K)
            topk_w = jnp.take_along_axis(scores, topk_idx, axis=-1)
            topk_w = topk_w / topk_w.sum(axis=-1, keepdims=True)
            P = N * K
            e_flat = topk_idx.reshape(-1)
            t_flat = jnp.repeat(jnp.arange(N), K)
            w_flat = topk_w.reshape(-1)
            order = jnp.argsort(e_flat)
            e_s, t_s, w_s = (e_flat[order], t_flat[order], w_flat[order])
            counts = jnp.bincount(e_s, length=E)
            starts = jnp.concatenate([jnp.zeros((1,), counts.dtype), jnp.cumsum(counts)[:-1]])
            pos = jnp.arange(P) - starts[e_s]
            slot = jnp.where(pos < CAP, pos, CAP)
            tok_table = jnp.zeros((E, CAP + 1), jnp.int32).at[e_s, slot].set(t_s)[:, :CAP]
            w_table = jnp.zeros((E, CAP + 1), w_s.dtype).at[e_s, slot].set(w_s)[:, :CAP]
            xg = flat[tok_table]
            g = jnp.einsum('ecd,efd->ecf', xg, gate_w)
            u = jnp.einsum('ecd,efd->ecf', xg, up_w)
            y = jnp.einsum('ecf,edf->ecd', jax.nn.silu(g) * u, down_w)
            out = jnp.zeros_like(flat).at[tok_table.reshape(-1)].add((y * w_table[..., None]).reshape(-1, d))
            sg = jnp.einsum('nd,sfd->nsf', flat, sh_gate_w)
            su = jnp.einsum('nd,sfd->nsf', flat, sh_up_w)
            out = out + jnp.einsum('nsf,sdf->nd', jax.nn.silu(sg) * su, sh_down_w)
            return out.reshape(b, t, d)
        key = jax.random.key(seed)
        ks = jax.random.split(key, 9)
        s = 0.02
        return {'x': jax.random.normal(ks[0], (B, T, D), jnp.float32), 'router_w': jax.random.normal(ks[1], (E, D), jnp.float32) * s, 'router_bias': jnp.zeros((E,), jnp.float32), 'gate_w': jax.random.normal(ks[2], (E, F, D), jnp.float32) * s, 'up_w': jax.random.normal(ks[3], (E, F, D), jnp.float32) * s, 'down_w': jax.random.normal(ks[4], (E, D, F), jnp.float32) * s, 'sh_gate_w': jax.random.normal(ks[5], (S, SF, D), jnp.float32) * s, 'sh_up_w': jax.random.normal(ks[6], (S, SF, D), jnp.float32) * s, 'sh_down_w': jax.random.normal(ks[7], (S, D, SF), jnp.float32) * s}
    _L3_ffn_in = _L3_ffn_setup()
    _d = {'L0_attn_X': _L0_attn_in['X'], 'L0_attn_Wq': _L0_attn_in['Wq'], 'L0_attn_bq': _L0_attn_in['bq'], 'L0_attn_Wk': _L0_attn_in['Wk'], 'L0_attn_bk': _L0_attn_in['bk'], 'L0_attn_Wv': _L0_attn_in['Wv'], 'L0_attn_bv': _L0_attn_in['bv'], 'L0_attn_Wo': _L0_attn_in['Wo'], 'L0_attn_bo': _L0_attn_in['bo'], 'L0_ffn_Wg': _L0_ffn_in['Wg'], 'L0_ffn_W1': _L0_ffn_in['W1'], 'L0_ffn_W3': _L0_ffn_in['W3'], 'L0_ffn_W2': _L0_ffn_in['W2'], 'L0_ffn_Ws1': _L0_ffn_in['Ws1'], 'L0_ffn_Ws3': _L0_ffn_in['Ws3'], 'L0_ffn_Ws2': _L0_ffn_in['Ws2'], 'L1_attn_Wq': _L1_attn_in['Wq'], 'L1_attn_Wk': _L1_attn_in['Wk'], 'L1_attn_Wv': _L1_attn_in['Wv'], 'L1_attn_Wo': _L1_attn_in['Wo'], 'L1_ffn_w_gate_up': _L1_ffn_in['w_gate_up'], 'L1_ffn_w_down': _L1_ffn_in['w_down'], 'L2_attn_Wq': _L2_attn_in['Wq'], 'L2_attn_Wk': _L2_attn_in['Wk'], 'L2_attn_Wv': _L2_attn_in['Wv'], 'L2_attn_Wo': _L2_attn_in['Wo'], 'L2_attn_norm_w': _L2_attn_in['norm_w'], 'L2_ffn_norm_w': _L2_ffn_in['norm_w'], 'L2_ffn_gate_w': _L2_ffn_in['gate_w'], 'L2_ffn_w13': _L2_ffn_in['w13'], 'L2_ffn_w2': _L2_ffn_in['w2'], 'L2_ffn_shared_gate_w': _L2_ffn_in['shared_gate_w'], 'L2_ffn_shared_up_w': _L2_ffn_in['shared_up_w'], 'L2_ffn_shared_down_w': _L2_ffn_in['shared_down_w'], 'L3_attn_Wq': _L3_attn_in['Wq'], 'L3_attn_bq': _L3_attn_in['bq'], 'L3_attn_Wk': _L3_attn_in['Wk'], 'L3_attn_bk': _L3_attn_in['bk'], 'L3_attn_Wv': _L3_attn_in['Wv'], 'L3_attn_bv': _L3_attn_in['bv'], 'L3_attn_Wo': _L3_attn_in['Wo'], 'L3_attn_bo': _L3_attn_in['bo'], 'L3_ffn_router_w': _L3_ffn_in['router_w'], 'L3_ffn_router_bias': _L3_ffn_in['router_bias'], 'L3_ffn_gate_w': _L3_ffn_in['gate_w'], 'L3_ffn_up_w': _L3_ffn_in['up_w'], 'L3_ffn_down_w': _L3_ffn_in['down_w'], 'L3_ffn_sh_gate_w': _L3_ffn_in['sh_gate_w'], 'L3_ffn_sh_up_w': _L3_ffn_in['sh_up_w'], 'L3_ffn_sh_down_w': _L3_ffn_in['sh_down_w']}
    _x0 = _d['L0_attn_X']
    _d['L0_attn_X'] = jax.random.normal(jax.random.fold_in(jax.random.key(seed), 1), (8, 256, 256), dtype=_x0.dtype)
    del _x0
    return _d

def reference(L0_attn_X, L0_attn_Wq, L0_attn_bq, L0_attn_Wk, L0_attn_bk, L0_attn_Wv, L0_attn_bv, L0_attn_Wo, L0_attn_bo, L0_ffn_Wg, L0_ffn_W1, L0_ffn_W3, L0_ffn_W2, L0_ffn_Ws1, L0_ffn_Ws3, L0_ffn_Ws2, L1_attn_Wq, L1_attn_Wk, L1_attn_Wv, L1_attn_Wo, L1_ffn_w_gate_up, L1_ffn_w_down, L2_attn_Wq, L2_attn_Wk, L2_attn_Wv, L2_attn_Wo, L2_attn_norm_w, L2_ffn_norm_w, L2_ffn_gate_w, L2_ffn_w13, L2_ffn_w2, L2_ffn_shared_gate_w, L2_ffn_shared_up_w, L2_ffn_shared_down_w, L3_attn_Wq, L3_attn_bq, L3_attn_Wk, L3_attn_bk, L3_attn_Wv, L3_attn_bv, L3_attn_Wo, L3_attn_bo, L3_ffn_router_w, L3_ffn_router_bias, L3_ffn_gate_w, L3_ffn_up_w, L3_ffn_down_w, L3_ffn_sh_gate_w, L3_ffn_sh_up_w, L3_ffn_sh_down_w):

    def _L0_attn_ref(X, Wq, bq, Wk, bk, Wv, bv, Wo, bo):
        import jax, jax.numpy as jnp
        import numpy as np
        N_HEADS = 16
        B, S, D = X.shape
        H = N_HEADS
        d_head = D // H
        scale = jnp.asarray(1.0 / np.sqrt(np.sqrt(d_head)), X.dtype)
        Q = (X @ Wq.T + bq).reshape(B, S, H, d_head) * scale
        K = (X @ Wk.T + bk).reshape(B, S, H, d_head) * scale
        V = (X @ Wv.T + bv).reshape(B, S, H, d_head)
        scores = jnp.einsum('bqhd,bkhd->bhqk', Q, K)
        causal = jnp.tril(jnp.ones((S, S), bool))
        scores = jnp.where(causal[None, None], scores, -jnp.inf)
        attn = jax.nn.softmax(scores.astype(jnp.float32), axis=-1).astype(X.dtype)
        out = jnp.einsum('bhqk,bkhd->bqhd', attn, V).reshape(B, S, D)
        return out @ Wo.T + bo

    def _L0_ffn_ref(x, Wg, W1, W3, W2, Ws1, Ws3, Ws2):
        import jax, jax.numpy as jnp
        import numpy as np
        DIM = 256
        INTER = 176
        E = 16
        TOPK = 4
        G = 4
        TOPK_G = 2
        N_SHARED = 2
        SHARED_INTER = N_SHARED * INTER
        ROUTE_SCALE = 1.0

        def _moe_forward(x, Wg, W1, W3, W2, Ws1, Ws3, Ws2):
            B, S, D = x.shape
            xt = x.reshape(-1, D)
            T = xt.shape[0]
            scores = jax.nn.softmax(xt @ Wg.T, axis=-1)
            sg = scores.reshape(T, G, E // G)
            group_scores = sg.max(axis=-1)
            gidx = jax.lax.top_k(group_scores, TOPK_G)[1]
            gmask = jax.nn.one_hot(gidx, G, dtype=jnp.float32).sum(axis=1) > 0
            masked = jnp.where(gmask[:, :, None], sg, -jnp.inf).reshape(T, E)
            topi = jax.lax.top_k(masked, TOPK)[1]
            weights = jnp.take_along_axis(scores, topi, axis=1) * ROUTE_SCALE
            combine = jnp.zeros((T, E), xt.dtype).at[jnp.arange(T)[:, None], topi].add(weights)
            h = jax.nn.silu(jnp.einsum('td,eid->eti', xt, W1)) * jnp.einsum('td,eid->eti', xt, W3)
            expert_out = jnp.einsum('eti,edi->etd', h, W2)
            y = jnp.einsum('etd,te->td', expert_out, combine)
            z = jax.nn.silu(xt @ Ws1.T) * (xt @ Ws3.T) @ Ws2.T
            return (y + z).reshape(B, S, D)
        return _moe_forward(x, Wg, W1, W3, W2, Ws1, Ws3, Ws2)

    def _L1_attn_ref(hidden_states, Wq, Wk, Wv, Wo):
        import jax, jax.numpy as jnp
        import numpy as np
        HID, H, KV, D = (256, 16, 4, 128)
        ROPE_THETA = 10000.0
        GATE_NORM = 16.0

        def _rope_cos_sin(n, d, dtype=jnp.float32):
            inv_freq = 1.0 / ROPE_THETA ** (jnp.arange(0, d, 2, dtype=jnp.float32) / d)
            freqs = jnp.arange(n, dtype=jnp.float32)[:, None] * inv_freq[None, :]
            cos = jnp.cos(freqs).astype(dtype)[None, :, None, :]
            sin = jnp.sin(freqs).astype(dtype)[None, :, None, :]
            return (cos, sin)

        def _apply_rotary(x, cos, sin):
            x1, x2 = jnp.split(x, 2, axis=-1)
            return jnp.concatenate([x1 * cos - x2 * sin, x2 * cos + x1 * sin], axis=-1)

        def _forward(hidden_states, Wq, Wk, Wv, Wo):
            b, n, _ = hidden_states.shape
            groups = H // KV
            q = hidden_states @ Wq
            k = hidden_states @ Wk
            v = hidden_states @ Wv
            g = k
            q = q.reshape(b, n, H, D)
            k = k.reshape(b, n, KV, D)
            v = v.reshape(b, n, KV, D)
            g = g.reshape(b, n, KV, D)
            k = jnp.repeat(k, groups, axis=2)
            v = jnp.repeat(v, groups, axis=2)
            g = jnp.repeat(g, groups, axis=2)
            sq, sk, sv = (q, k, v)
            qs = jax.nn.softmax(q.astype(jnp.float32), axis=-1)
            ks = jax.nn.softmax(k.astype(jnp.float32), axis=-1)
            gl = jax.nn.log_sigmoid(g.astype(jnp.float32)) / GATE_NORM
            cos, sin = _rope_cos_sin(n, D)
            sq = _apply_rotary(sq, cos, sin)
            sk = _apply_rotary(sk, cos, sin)

            def step(S, inp):
                q_t, k_t, v_t, g_t = inp
                S = S * jnp.exp(g_t)[..., None] + k_t[..., None] * v_t[..., None, :]
                o_t = jnp.einsum('bhk,bhkv->bhv', q_t, S)
                return (S, o_t)
            xs = tuple((jnp.moveaxis(a, 1, 0) for a in (qs, ks, v, gl)))
            S0 = jnp.zeros((b, H, D, D), dtype=jnp.float32)
            _, o_gla = jax.lax.scan(step, S0, xs)
            o_gla = jnp.moveaxis(o_gla, 0, 1)
            scale = D ** (-0.5)
            scores = jnp.einsum('bqhd,bkhd->bhqk', sq, sk) * scale
            causal = jnp.tril(jnp.ones((n, n), dtype=bool))
            scores = jnp.where(causal[None, None], scores, jnp.finfo(scores.dtype).min)
            attn = jax.nn.softmax(scores, axis=-1)
            y = jnp.einsum('bhqk,bkhd->bqhd', attn, sv)
            o = 0.5 * y + 0.5 * o_gla
            o = o.reshape(b, n, H * D).astype(hidden_states.dtype)
            return o @ Wo
        return _forward(hidden_states, Wq, Wk, Wv, Wo)

    def _L1_ffn_ref(h_shard, w_gate_up, w_down):
        import jax, jax.numpy as jnp
        import numpy as np
        HIDDEN = 256
        INTER = 1024
        BATCH, LOCAL_SEQ = (2, 512)
        batch, local_seq, hidden = h_shard.shape
        gate_up = jnp.einsum('bsh,oh->bso', h_shard, w_gate_up)
        gate, up = jnp.split(gate_up, 2, axis=-1)
        h = jax.nn.silu(gate) * up
        out = jnp.einsum('bsi,hi->bsh', h, w_down)
        return out

    def _L2_attn_ref(x, Wq, Wk, Wv, Wo, norm_w):
        import jax, jax.numpy as jnp
        import numpy as np
        from jax import lax
        B, N, D = (4, 512, 256)
        E = 128
        H = D // E
        CHUNK = 64
        EPS = 1e-06

        def rmsnorm(x, w):
            var = jnp.mean(jnp.square(x), axis=-1, keepdims=True)
            return x * lax.rsqrt(var + EPS) * w

        def chunked_gla(q, v, log_f):
            b, n, h, e = q.shape
            nc = n // CHUNK
            k = 1.0 - jnp.exp(log_f)

            def to_chunks(t):
                return t.reshape(b, nc, CHUNK, h, e).transpose(1, 0, 2, 3, 4)
            qs, ks_, vs, lfs = map(to_chunks, (q, k, v, log_f))
            A = jnp.cumsum(lfs, axis=2)
            mask = jnp.tril(jnp.ones((CHUNK, CHUNK), dtype=bool))

            def step(S, xs):
                qc, kc, vc, Ac = xs
                q_dec = qc * jnp.exp(Ac)
                k_dec = kc * jnp.exp(-Ac)
                scores = jnp.einsum('bthe,bshe->bhts', q_dec, k_dec)
                scores = jnp.where(mask[None, None], scores, 0.0)
                o_intra = jnp.einsum('bhts,bshe->bthe', scores, vc)
                o_inter = jnp.einsum('bthe,bhef->bthf', q_dec, S)
                A_last = Ac[:, -1]
                k_rem = kc * jnp.exp(A_last[:, None] - Ac)
                S_new = jnp.exp(A_last)[..., None] * S + jnp.einsum('bthe,bthf->bhef', k_rem, vc)
                return (S_new, o_intra + o_inter)
            S0 = jnp.zeros((b, h, e, e), dtype=q.dtype)
            _, o = lax.scan(step, S0, (qs, ks_, vs, A))
            return o.transpose(1, 0, 2, 3, 4).reshape(b, n, h, e)
        b, n, d = x.shape
        q = jax.nn.silu(x @ Wq.T)
        f = jax.nn.sigmoid(x @ Wk.T)
        log_f = jax.nn.log_sigmoid(f)
        v = x @ Wv.T
        q, v, log_f = (t.reshape(b, n, H, E) for t in (q, v, log_f))
        o = chunked_gla(q, v, log_f)
        o = o.reshape(b, n, d)
        o = rmsnorm(o, norm_w)
        return o @ Wo.T

    def _L2_ffn_ref(hidden_states, norm_w, gate_w, w13, w2, shared_gate_w, shared_up_w, shared_down_w):
        import jax, jax.numpy as jnp
        import numpy as np
        H = 256
        I = 128
        E = 32
        K = 4
        N_SHARED = 1
        EPS = 1e-06

        def _rmsnorm(x, w, eps=EPS):
            var = jnp.mean(jnp.square(x), axis=-1, keepdims=True)
            return x * jax.lax.rsqrt(var + eps) * w

        def _moe_core(x, gate_w, w13, w2):
            T = x.shape[0]
            N = T * K
            C = 2 * N // E
            logits = jnp.einsum('th,eh->te', x.astype(jnp.float32), gate_w.astype(jnp.float32))
            scores = jax.nn.softmax(logits, axis=-1)
            topk_w, topk_ids = jax.lax.top_k(scores, K)
            topk_w = topk_w / jnp.sum(topk_w, axis=-1, keepdims=True)
            flat_ids = topk_ids.reshape(-1)
            flat_w = topk_w.reshape(-1)
            order = jnp.argsort(flat_ids)
            sorted_eid = flat_ids[order]
            tok = order // K
            counts = jnp.zeros((E,), jnp.int32).at[flat_ids].add(1)
            starts = jnp.cumsum(counts) - counts
            pos = jnp.arange(N) - starts[sorted_eid]
            buf = jnp.zeros((E, C, x.shape[1]), x.dtype).at[sorted_eid, pos].set(x[tok], mode='drop')
            gu = jnp.einsum('ech,ehf->ecf', buf, w13)
            g, u = jnp.split(gu, 2, axis=-1)
            act = jax.nn.silu(g) * u
            eo = jnp.einsum('eci,eih->ech', act, w2)
            out_slots = eo[sorted_eid, pos]
            routed = jnp.zeros_like(x).at[tok].add(out_slots * flat_w[order][:, None])
            return routed
        B, S, Hd = hidden_states.shape
        residual = hidden_states
        h = _rmsnorm(hidden_states, norm_w)
        x = h.reshape(-1, Hd)
        routed = _moe_core(x, gate_w, w13, w2)
        shared = jax.nn.silu(x @ shared_gate_w) * (x @ shared_up_w) @ shared_down_w
        out = residual + (routed + shared).reshape(B, S, Hd)
        return out

    def _L3_attn_ref(x, Wq, bq, Wk, bk, Wv, bv, Wo, bo):
        import jax, jax.numpy as jnp
        import numpy as np
        B, S, D, H = (4, 256, 256, 16)
        DK = D // H
        b, s, d = x.shape
        scale = DK ** 0.5

        def proj(W, bias):
            y = jnp.einsum('bsd,ed->bse', x, W) + bias
            return y.reshape(b, s, H, DK).transpose(0, 2, 1, 3)
        Q, K, V = (proj(Wq, bq), proj(Wk, bk), proj(Wv, bv))
        scores = jnp.einsum('bhqd,bhkd->bhqk', Q, K) / scale
        causal = jnp.triu(jnp.ones((s, s), dtype=bool), k=1)
        scores = jnp.where(causal[None, None], -jnp.inf, scores)
        attn = jax.nn.softmax(scores, axis=-1)
        ctx = jnp.einsum('bhqk,bhkd->bhqd', attn, V)
        ctx = ctx.transpose(0, 2, 1, 3).reshape(b, s, d)
        out = jnp.einsum('bsd,ed->bse', ctx, Wo) + bo
        return out

    def _L3_ffn_ref(x, router_w, router_bias, gate_w, up_w, down_w, sh_gate_w, sh_up_w, sh_down_w):
        import jax, jax.numpy as jnp
        import numpy as np
        B, T, D = (1, 256, 256)
        E, K, F = (64, 4, 64)
        S, SF = (2, 64 * 4)
        CAP = 32

        def _moe_forward(x, router_w, router_bias, gate_w, up_w, down_w, sh_gate_w, sh_up_w, sh_down_w):
            b, t, d = x.shape
            flat = x.reshape(b * t, d)
            N = flat.shape[0]
            logits = flat @ router_w.T
            scores = jax.nn.softmax(logits, axis=-1)
            _, topk_idx = jax.lax.top_k(logits + router_bias, K)
            topk_w = jnp.take_along_axis(scores, topk_idx, axis=-1)
            topk_w = topk_w / topk_w.sum(axis=-1, keepdims=True)
            P = N * K
            e_flat = topk_idx.reshape(-1)
            t_flat = jnp.repeat(jnp.arange(N), K)
            w_flat = topk_w.reshape(-1)
            order = jnp.argsort(e_flat)
            e_s, t_s, w_s = (e_flat[order], t_flat[order], w_flat[order])
            counts = jnp.bincount(e_s, length=E)
            starts = jnp.concatenate([jnp.zeros((1,), counts.dtype), jnp.cumsum(counts)[:-1]])
            pos = jnp.arange(P) - starts[e_s]
            slot = jnp.where(pos < CAP, pos, CAP)
            tok_table = jnp.zeros((E, CAP + 1), jnp.int32).at[e_s, slot].set(t_s)[:, :CAP]
            w_table = jnp.zeros((E, CAP + 1), w_s.dtype).at[e_s, slot].set(w_s)[:, :CAP]
            xg = flat[tok_table]
            g = jnp.einsum('ecd,efd->ecf', xg, gate_w)
            u = jnp.einsum('ecd,efd->ecf', xg, up_w)
            y = jnp.einsum('ecf,edf->ecd', jax.nn.silu(g) * u, down_w)
            out = jnp.zeros_like(flat).at[tok_table.reshape(-1)].add((y * w_table[..., None]).reshape(-1, d))
            sg = jnp.einsum('nd,sfd->nsf', flat, sh_gate_w)
            su = jnp.einsum('nd,sfd->nsf', flat, sh_up_w)
            out = out + jnp.einsum('nsf,sdf->nd', jax.nn.silu(sg) * su, sh_down_w)
            return out.reshape(b, t, d)
        return _moe_forward(x, router_w, router_bias, gate_w, up_w, down_w, sh_gate_w, sh_up_w, sh_down_w)
    x = L0_attn_X
    xn = _layernorm(x, axis=-1)
    x = x + _L0_attn_ref(xn, L0_attn_Wq, L0_attn_bq, L0_attn_Wk, L0_attn_bk, L0_attn_Wv, L0_attn_bv, L0_attn_Wo, L0_attn_bo) + _L0_ffn_ref(xn, L0_ffn_Wg, L0_ffn_W1, L0_ffn_W3, L0_ffn_W2, L0_ffn_Ws1, L0_ffn_Ws3, L0_ffn_Ws2)
    xn = _layernorm(x, axis=-1)
    x = x + _L1_attn_ref(xn, L1_attn_Wq, L1_attn_Wk, L1_attn_Wv, L1_attn_Wo) + _L1_ffn_ref(xn, L1_ffn_w_gate_up, L1_ffn_w_down)
    xn = _layernorm(x, axis=-1)
    x = x + _L2_attn_ref(xn, L2_attn_Wq, L2_attn_Wk, L2_attn_Wv, L2_attn_Wo, L2_attn_norm_w) + _L2_ffn_ref(xn, L2_ffn_norm_w, L2_ffn_gate_w, L2_ffn_w13, L2_ffn_w2, L2_ffn_shared_gate_w, L2_ffn_shared_up_w, L2_ffn_shared_down_w)
    xn = _layernorm(x, axis=-1)
    x = x + _L3_attn_ref(xn, L3_attn_Wq, L3_attn_bq, L3_attn_Wk, L3_attn_bk, L3_attn_Wv, L3_attn_bv, L3_attn_Wo, L3_attn_bo) + _L3_ffn_ref(xn, L3_ffn_router_w, L3_ffn_router_bias, L3_ffn_gate_w, L3_ffn_up_w, L3_ffn_down_w, L3_ffn_sh_gate_w, L3_ffn_sh_up_w, L3_ffn_sh_down_w)
    return x

_drawn_inputs = setup_inputs


def setup_inputs(seed=0):
    import zlib

    import numpy as np

    out = dict(_drawn_inputs(seed))
    spreads = {'L2_attn_norm_w': (1.0, 0.549),
     'L2_ffn_norm_w': (1.0, 0.2),
     'L3_attn_bq': (0.0, 2.0),
     'L3_attn_bk': (0.0, 2.0),
     'L3_attn_bv': (0.0, 0.745),
     'L3_attn_bo': (0.0, 0.71),
     'L3_ffn_router_bias': (0.0, 0.8)}
    factors = {'L0_attn_Wq': 8.0,
     'L0_attn_bq': 24.846,
     'L0_attn_Wk': 8.0,
     'L0_attn_bk': 64.0,
     'L0_attn_bv': 4.569,
     'L0_ffn_Wg': 8.0,
     'L0_ffn_W1': 8.0,
     'L0_ffn_W3': 8.0,
     'L0_ffn_W2': 8.0,
     'L1_attn_Wq': 8.0,
     'L1_attn_Wk': 8.0,
     'L2_attn_Wk': 8.0,
     'L3_ffn_router_w': 8.0,
     'L3_ffn_gate_w': 8.0,
     'L3_ffn_up_w': 8.0,
     'L3_ffn_down_w': 8.0,
     'L3_ffn_sh_gate_w': 5.059,
     'L3_ffn_sh_up_w': 5.052,
     'L3_ffn_sh_down_w': 5.017,
     'L0_attn_bo': 3.181,
     'L0_ffn_Ws3': 2.821,
     'L0_ffn_Ws2': 2.874,
     'L3_attn_Wq': 2.685}
    for name, (base, spread) in spreads.items():
        noise = np.random.default_rng([zlib.crc32(name.encode()), seed]).standard_normal(out[name].shape)
        drawn = base * np.exp(spread * noise) if base else spread * noise
        out[name] = jnp.asarray(drawn.astype(out[name].dtype))
    for name, factor in factors.items():
        out[name] = (out[name] * factor).astype(out[name].dtype)
    return out
```

```python
from contextlib import ExitStack

import numpy as np

import concourse.bass as bass
from concourse import mybir

STAGES = "0a,0f,1a,1f,2a,2f,3a,3f".split(",")

ALU = mybir.AluOpType
ACT = mybir.ActivationFunctionType
F32 = mybir.dt.float32
AX_X = mybir.AxisListType.X

P = 128
D = 256
KD = D // P
SEQ = 256
NB = 8
TOK = NB * SEQ
NT = TOK // P
QT = SEQ // P
BIG = 1.0e30
SMALL = ("wq", "wk", "wv", "wo", "bq", "bk", "bv", "bo")
CONSTS = ("ident", "cmask", "cmask01", "before", "ones")


class Chain:

    def __init__(self, eng, sem, base=0):
        self.eng, self.sem, self.base, self.count = eng, sem, base, 0

    def link(self, ins):
        self.count += 1
        ins.then_inc(self.sem, 1)
        self.eng.wait_ge(self.sem, self.base + self.count)


class Space:

    def __init__(self, nc, ctx, name):
        self.nc, self.ctx, self.name = nc, ctx, name
        self.sems = []
        ctx.callback(self.close)

    def sb(self, name, shape):
        return self.ctx.enter_context(self.nc.sbuf_tensor(f"{self.name}_{name}", shape, F32))

    def ps(self, name, shape):
        return self.ctx.enter_context(self.nc.psum_tensor(f"{self.name}_{name}", shape, F32))

    def sem(self, name):
        self.sems.append(self.nc.alloc_semaphore(name=f"{self.name}_{name}"))
        return self.sems[-1]

    def close(self):
        if self.sems:
            self.nc.clear_and_free_semaphores(self.sems)
            self.nc.all_engine_barrier()


def setup(nc, x_dram, const):
    with ExitStack() as ctx:
        load_all(nc, Space(nc, ctx, "setup"), x_dram, const)


def load_all(nc, sp, x_dram, const):
    loaded = sp.sem("loaded")
    with nc.Block() as block:
        @block.sync
        def _(sync):
            sync.dma_start(const["x"][:, :, :], x_dram.rearrange("b (s p) d -> p (b s) d", p=P)).then_inc(loaded, 16)
            for name in CONSTS:
                sync.dma_start(const[name][:, :], const[name + "_dram"]).then_inc(loaded, 16)
            sync.wait_ge(loaded, 16 * (1 + len(CONSTS)))


def store(nc, out, const):
    with ExitStack() as ctx:
        store_all(nc, Space(nc, ctx, "store"), out, const)


def store_all(nc, sp, out, const):
    stored = sp.sem("stored")
    with nc.Block() as block:
        @block.sync
        def _(sync):
            sync.dma_start(out.rearrange("b (s p) d -> p (b s) d", p=P), const["x"][:, :, :]).then_inc(stored, 16)
            sync.wait_ge(stored, 16)


def normalize(nc, name, src, const, xn, xT, eps, rms, w_dram=None, add_src=False):
    with ExitStack() as ctx:
        sp = Space(nc, ctx, name)
        stats = sp.sb("stats", [P, NT, 6])
        mv = sp.sb("mv", [P, NT, 2])
        std = sp.sb("std", [P, NT])
        rstd = sp.sb("rstd", [P, NT])
        tmp = sp.sb("tmp", [P, NT])
        epsb = sp.sb("epsb", [P, 1])
        wcol = sp.sb("wcol", [P, KD])
        pT = [sp.ps(f"pT{i}", [P, KD, P]) for i in range(2)]
        stat_done = sp.sem("stat_done")
        agg_done = sp.sem("agg_done")
        var_ready = sp.sem("var_ready")
        std_ready = sp.sem("std_ready")
        xn_ready = sp.sem("xn_ready")
        turned = sp.sem("turned")
        copied = sp.sem("copied")
        w_in = sp.sem("w_in")
        chain = sp.sem("chain")
        ident = const["ident"]
        with nc.Block() as block:
            if w_dram is not None:
                @block.sync
                def _(sync):
                    sync.dma_start(wcol[:, :], w_dram).then_inc(w_in, 16)

            @block.vector
            def _(dve):
                nc.vector.memset(epsb[:, :], eps).then_inc(chain, 1)
                if add_src:
                    nc.vector.tensor_tensor(const["x"][:, :, :], const["x"][:, :, :], src[:, :, :],
                                            ALU.add).then_inc(chain, 1)
                    dve.wait_ge(chain, 2)
                for t in range(NT):
                    nc.vector.bn_stats(stats[:, t, :], src[:, t, :]).then_inc(stat_done, 1)
                for t in range(NT):
                    dve.wait_ge(stat_done, t + 1)
                    nc.vector.bn_aggr(mv[:, t, :], stats[:, t, :]).then_inc(agg_done, 1)
                dve.wait_ge(agg_done, NT)
                if rms:
                    nc.vector.tensor_tensor(tmp[:, :], mv[:, :, 0], mv[:, :, 0], ALU.mult).then_inc(chain, 1)
                    dve.wait_ge(chain, 3 if add_src else 2)
                    nc.vector.tensor_tensor(tmp[:, :], tmp[:, :], mv[:, :, 1], ALU.add).then_inc(var_ready, 1)
                else:
                    nc.vector.tensor_copy(tmp[:, :], mv[:, :, 1]).then_inc(var_ready, 1)
                dve.wait_ge(std_ready, 1)
                nc.vector.reciprocal(rstd[:, :], std[:, :]).then_inc(std_ready, 1)
                dve.wait_ge(std_ready, 2)
                for t in range(NT):
                    if rms:
                        nc.vector.tensor_scalar(xn[:, t, :], src[:, t, :], rstd[:, t:t + 1], None,
                                                ALU.mult).then_inc(xn_ready, 1)
                    else:
                        nc.vector.tensor_scalar(xn[:, t, :], src[:, t, :], mv[:, t, 0:1], rstd[:, t:t + 1],
                                                ALU.subtract, ALU.mult).then_inc(xn_ready, 1)

            @block.tensor
            def _(pe):
                for t in range(NT):
                    pe.wait_ge(xn_ready, t + 1)
                    if t >= 2:
                        pe.wait_ge(copied, t - 1)
                    for k in range(KD):
                        last = nc.tensor.transpose(pT[t % 2][:, k, :], xn[:, t, k * P:(k + 1) * P], ident[:, :])
                    last.then_inc(turned, 1)

            @block.scalar
            def _(act):
                act.wait_ge(chain, 1)
                act.wait_ge(var_ready, 1)
                nc.scalar.activation(std[:, :], tmp[:, :], ACT.Sqrt, bias=epsb[:, 0:1]).then_inc(std_ready, 1)
                if w_dram is not None:
                    act.wait_ge(w_in, 16)
                for t in range(NT):
                    act.wait_ge(turned, t + 1)
                    if w_dram is None:
                        nc.scalar.activation(xT[:, :, t * P:(t + 1) * P], pT[t % 2][:, :, :],
                                             ACT.Copy).then_inc(copied, 1)
                    else:
                        for k in range(KD):
                            last = nc.scalar.activation(xT[:, k, t * P:(t + 1) * P], pT[t % 2][:, k, :],
                                                        ACT.Copy, scale=wcol[:, k:k + 1])
                        last.then_inc(copied, 1)


def route(nc, name, const, xT, w_dram, E, K, cT, groups=None, bias_dram=None, renorm=True, cap=None, extra=None):
    C = E + 1
    per = min(NT, 512 // E)
    banks = NT // per
    with ExitStack() as ctx:
        sp = Space(nc, ctx, name)
        w = sp.sb("w", [P, KD, E])
        bias = sp.sb("bias", [P, E])
        order = sp.sb("order", [P, E])
        lg = sp.sb("lg", [P, NT, E])
        ex = sp.sb("ex", [P, NT, E])
        key = sp.sb("key", [P, NT, E])
        sel = sp.sb("sel", [P, NT, E])
        eq = sp.sb("eq", [P, NT, E])
        c = sp.sb("c", [P, NT, C])
        m1 = sp.sb("m1", [P, NT, 1])
        m2 = sp.sb("m2", [P, NT, 1])
        plog = [sp.ps(f"plog{i}", [P, per, E]) for i in range(banks)]
        pT = [sp.ps(f"pT{i}", [P, 512]) for i in range(2)]
        w_in = sp.sem("w_in")
        logits = sp.sem("logits")
        chain = sp.sem("chain")
        shifted = sp.sem("shifted")
        exped = sp.sem("exped")
        chosen = sp.sem("chosen")
        ranked = sp.sem("ranked")
        c_ready = sp.sem("c_ready")
        turned = sp.sem("turned")
        copied = sp.sem("copied")
        if groups:
            GR, GK = groups
            gs = sp.sb("gs", [P, NT, GR])
            gsel = sp.sb("gsel", [P, NT, GR])
            geq = sp.sb("geq", [P, NT, GR])
        if cap:
            tot = sp.sb("tot", [P, NT, E])
            rank = sp.sb("rank", [P, NT, E])
            base = sp.sb("base", [P, NT, E])
            prank = [sp.ps(f"prank{i}", [P, per, E]) for i in range(banks)]
            ptot = [sp.ps(f"ptot{i}", [P, per, E]) for i in range(banks)] if banks == 1 else plog
        if extra:
            over = sp.sb("over", [P, NT, E])
            wcol = sp.sb("wcol", [P, KD])
            px = sp.ps("px", [P, KD, E])
        ident = const["ident"]
        n_in = 2 + (bias_dram is not None) + (extra is not None)
        with nc.Block() as block:
            @block.sync
            def _(sync):
                sync.dma_start(w[:, :, :], w_dram).then_inc(w_in, 16)
                sync.dma_start(order[:, :], const["order_dram"][:, 0:E]).then_inc(w_in, 16)
                if bias_dram is not None:
                    sync.dma_start(bias[:, :], bias_dram[0, :].partition_broadcast(P)).then_inc(w_in, 16)
                if extra:
                    sync.dma_start(wcol[:, :], extra[3]).then_inc(w_in, 16)

            @block.tensor
            def _(pe):
                pe.wait_ge(w_in, 16 * n_in)
                for t in range(NT):
                    for k in range(KD):
                        last = nc.tensor.matmul(plog[t // per][:, t % per, :], xT[:, k, t * P:(t + 1) * P], w[:, k, :],
                                                start=(k == 0), stop=(k == KD - 1))
                last.then_inc(logits, 1)
                if cap:
                    pe.wait_ge(chosen, 1)
                    for i in range(banks):
                        nc.tensor.matmul(prank[i][:, :, :], const["before"][:, :], sel[:, i * per:(i + 1) * per, :],
                                         start=True, stop=True)
                        last = nc.tensor.matmul(ptot[i][:, :, :], const["ones"][:, :], sel[:, i * per:(i + 1) * per, :],
                                                start=True, stop=True)
                    last.then_inc(ranked, 1)
                pe.wait_ge(c_ready, 1)
                for t in range(NT):
                    if t >= 2:
                        pe.wait_ge(copied, t - 1)
                    last = nc.tensor.transpose(pT[t % 2][0:C, 0:P], c[:, t, :], ident[:, :])
                    if extra:
                        last = nc.tensor.transpose(pT[t % 2][0:E, P:2 * P], over[:, t, :], ident[:, :])
                    last.then_inc(turned, 1)
                if extra:
                    for k in range(KD):
                        for t in range(NT):
                            last = nc.tensor.matmul(px[:, k, :], extra[0][:, t, k * P:(k + 1) * P], eq[:, t, :],
                                                    start=(t == 0), stop=(t == NT - 1))
                    last.then_inc(turned, 1)

            @block.scalar
            def _(act):
                act.wait_ge(shifted, 1)
                nc.scalar.activation(ex[:, :, :], ex[:, :, :], ACT.Exp).then_inc(exped, 1)
                for t in range(NT):
                    act.wait_ge(turned, t + 1)
                    last = nc.scalar.activation(cT[0:C, t * P:(t + 1) * P], pT[t % 2][0:C, 0:P], ACT.Copy)
                    if extra:
                        last = nc.scalar.activation(extra[2][0:E, t * P:(t + 1) * P], pT[t % 2][0:E, P:2 * P], ACT.Copy)
                    last.then_inc(copied, 1)
                if extra:
                    act.wait_ge(turned, NT + 1)
                    for k in range(KD):
                        nc.scalar.activation(extra[1][:, k, :], px[:, k, :], ACT.Copy, scale=wcol[:, k:k + 1])

            @block.vector
            def _(dve):
                ch = Chain(dve, chain)

                def wide(small, n):
                    return small[:, :, 0:1].broadcast_to([P, NT, n])

                def take_best(key, eq, sel, n, times):
                    ch.link(nc.vector.memset(sel[:, :, :], 0.0))
                    for _ in range(times):
                        ch.link(nc.vector.tensor_reduce(m1[:, :, 0], key[:, :, :], AX_X, ALU.max))
                        ch.link(nc.vector.tensor_tensor(eq[:, :, :], key[:, :, :], wide(m1, n), ALU.is_equal))
                        ch.link(nc.vector.tensor_tensor(eq[:, :, :], eq[:, :, :],
                                                        order[:, 0:n].unsqueeze(1).broadcast_to([P, NT, n]), ALU.mult))
                        ch.link(nc.vector.tensor_reduce(m1[:, :, 0], eq[:, :, :], AX_X, ALU.max))
                        ch.link(nc.vector.tensor_tensor(eq[:, :, :], eq[:, :, :], wide(m1, n), ALU.is_equal))
                        ch.link(nc.vector.scalar_tensor_tensor(out=key[:, :, :], in0=eq[:, :, :], scalar=-4 * BIG,
                                                               in1=key[:, :, :], op0=ALU.mult, op1=ALU.add))
                        ch.link(nc.vector.tensor_tensor(sel[:, :, :], sel[:, :, :], eq[:, :, :], ALU.add))

                dve.wait_ge(w_in, 16 * n_in)
                dve.wait_ge(logits, 1)
                for i in range(banks):
                    ch.link(nc.vector.tensor_copy(lg[:, i * per:(i + 1) * per, :], plog[i][:, :, :]))
                ch.link(nc.vector.tensor_reduce(m2[:, :, 0], lg[:, :, :], AX_X, ALU.max))
                nc.vector.tensor_tensor(ex[:, :, :], lg[:, :, :], wide(m2, E), ALU.subtract).then_inc(shifted, 1)
                if bias_dram is not None:
                    ch.link(nc.vector.tensor_tensor(key[:, :, :], lg[:, :, :],
                                                    bias[:, :].unsqueeze(1).broadcast_to([P, NT, E]), ALU.add))
                else:
                    ch.link(nc.vector.tensor_copy(key[:, :, :], lg[:, :, :]))
                if groups:
                    ch.link(nc.vector.tensor_reduce(gs[:, :, :], key[:, :, :].rearrange("p t (g e) -> p (t g) e", g=GR),
                                                    AX_X, ALU.max))
                    take_best(gs, geq, gsel, GR, GK)
                    ch.link(nc.vector.tensor_scalar(gsel[:, :, :], gsel[:, :, :], -1.0, BIG, ALU.add, ALU.mult))
                    kg = key[:, :, :].rearrange("p t (g e) -> p (t g) e", g=GR)
                    gg = gsel[:, :, :].rearrange("p t g -> p (t g)").unsqueeze(2).broadcast_to([P, NT * GR, E // GR])
                    ch.link(nc.vector.tensor_tensor(kg, kg, gg, ALU.add))
                take_best(key, eq, sel, E, K)
                if cap:
                    dve.sem_inc(chosen, 1)
                dve.wait_ge(exped, 1)
                if not renorm:
                    ch.link(nc.vector.tensor_reduce(m1[:, :, 0], ex[:, :, :], AX_X, ALU.add))
                ch.link(nc.vector.tensor_tensor(c[:, :, 0:E], ex[:, :, :], sel[:, :, :], ALU.mult))
                if renorm:
                    ch.link(nc.vector.tensor_reduce(m1[:, :, 0], c[:, :, 0:E], AX_X, ALU.add))
                ch.link(nc.vector.reciprocal(m2[:, :, 0], m1[:, :, 0]))
                ch.link(nc.vector.tensor_tensor(c[:, :, 0:E], c[:, :, 0:E], wide(m2, E), ALU.mult))
                ch.link(nc.vector.memset(c[:, :, E:C], 1.0))
                if cap:
                    dve.wait_ge(ranked, 1)
                    for i in range(banks):
                        ch.link(nc.vector.tensor_copy(rank[:, i * per:(i + 1) * per, :], prank[i][:, :, :]))
                        ch.link(nc.vector.tensor_copy(tot[:, i * per:(i + 1) * per, :], ptot[i][:, :, :]))
                    ch.link(nc.vector.memset(base[:, 0, :], 0.0))
                    for t in range(1, NT):
                        ch.link(nc.vector.tensor_tensor(base[:, t, :], base[:, t - 1, :], tot[:, t - 1, :], ALU.add))
                    ch.link(nc.vector.tensor_tensor(rank[:, :, :], rank[:, :, :], base[:, :, :], ALU.add))
                    if extra:
                        ch.link(nc.vector.tensor_scalar(eq[:, :, :], rank[:, :, :], float(cap - 1), None, ALU.is_equal))
                        ch.link(nc.vector.tensor_tensor(eq[:, :, :], eq[:, :, :], sel[:, :, :], ALU.mult))
                        ch.link(nc.vector.tensor_scalar(over[:, :, :], rank[:, :, :], float(cap), None, ALU.is_ge))
                        ch.link(nc.vector.tensor_tensor(over[:, :, :], over[:, :, :], c[:, :, 0:E], ALU.mult))
                        ch.link(nc.vector.memset(cT[:, TOK:TOK + E], 0.0))
                        ch.link(nc.vector.tensor_copy(cT[0:E, TOK:TOK + E], ident[0:E, 0:E]))
                    ch.link(nc.vector.tensor_scalar(rank[:, :, :], rank[:, :, :], float(cap), None, ALU.is_lt))
                    ch.link(nc.vector.tensor_tensor(c[:, :, 0:E], c[:, :, 0:E], rank[:, :, :], ALU.mult))
                dve.sem_inc(c_ready, 1)


HALF = TOK // 2
GRP = 512


def gated_ffn(nc, name, const, xT, bank, n_pieces, cT=None, extra=None):
    E = cT.shape[0] if cT is not None else 0
    WB = bank.shape[2]
    NX = extra[0].shape[2] if extra else 0
    G = 3 if extra else 2
    TH = HALF // P
    with ExitStack() as ctx:
        sp = Space(nc, ctx, name)
        w = [sp.sb(f"w{i}", [P, WB]) for i in range(2)]
        gate = [sp.sb(f"gate{g}", [P, GRP]) for g in range(2)]
        prod = sp.sb("prod", [P, GRP])
        hid = [sp.sb(f"hid{g}", [P, GRP]) for g in range(3)]
        zero = sp.sb("zero", [1, 512])
        pg = sp.ps("pg", [P, GRP])
        pu = sp.ps("pu", [P, GRP])
        pc = sp.ps("pc", [P, GRP])
        pout = [sp.ps(f"pout{i}", [P, 2, D]) for i in range(TH // 2)]
        if extra:
            pex = sp.ps("pex", [P, D])
            fex = sp.sb("fex", [P, D])
        w_in = [sp.sem(f"w_in{i}") for i in range(2)]
        w_used = sp.sem("w_used")
        zeroed = sp.sem("zeroed")
        g_done = sp.sem("g_done")
        u_done = sp.sem("u_done")
        c_done = sp.sem("c_done")
        silu_done = sp.sem("silu_done")
        prod_done = sp.sem("prod_done")
        hid_done = sp.sem("hid_done")
        ex_done = sp.sem("ex_done")
        fex_done = sp.sem("fex_done")
        out_done = sp.sem("out_done")
        added = sp.sem("added")

        hidden_ready = hid_done if cT is not None else prod_done
        odd = n_pieces % 2
        per_buf = [(n_pieces + 1) // 2, n_pieces // 2]

        def groups(half):
            at = [(xT, half * HALF + g * GRP, GRP, half * HALF + g * GRP) for g in range(2)]
            return at + ([(extra[0], 0, NX, TOK)] if extra else [])

        with nc.Block() as block:
            @block.sync
            def _(sync):
                def load(p, buf):
                    sync.dma_start(w[buf][:, :], bank[bass.ds(p, 1), :, :].rearrange("a p w -> p (a w)")
                                   ).then_inc(w_in[buf], 16)

                for half in range(2):
                    done = half * n_pieces
                    for buf in range(2):
                        if half:
                            sync.wait_ge(w_used, done - 1 + buf + (odd if buf == 0 else 0))
                        load(buf, buf)
                    with sync.Fori(1, n_pieces // 2) as i:
                        for buf in range(2):
                            sync.wait_ge(w_used, 2 * i + (done + buf - 1))
                            load(2 * i + buf, buf)
                    if odd:
                        sync.wait_ge(w_used, done + n_pieces - 2)
                        load(n_pieces - 1, 0)

            @block.tensor
            def _(pe):
                def piece(half, p, buf, turn):
                    n = p + half * n_pieces
                    pe.wait_ge(w_in[buf], turn * 16 + 16 * (half * per_buf[buf] + 1))
                    wb = w[buf]
                    for g, (xs, at, width, cat) in enumerate(groups(half)):
                        m = n * G + g
                        pe.wait_ge(silu_done, m + 1)
                        for k in range(KD):
                            last = nc.tensor.matmul(pg[:, 0:width], wb[:, k * 2 * P:k * 2 * P + P],
                                                    xs[:, k, at:at + width], start=(k == 0), stop=(k == KD - 1))
                        last.then_inc(g_done, 1)
                        pe.wait_ge(prod_done, m + 1)
                        for k in range(KD):
                            last = nc.tensor.matmul(pu[:, 0:width], wb[:, k * 2 * P + P:(k + 1) * 2 * P],
                                                    xs[:, k, at:at + width], start=(k == 0), stop=(k == KD - 1))
                        last.then_inc(u_done, 1)
                        if cT is not None:
                            pe.wait_ge(hid_done, m + 1)
                            nc.tensor.matmul(pc[:, 0:width], wb[0:E, KD * 2 * P + D:KD * 2 * P + D + P],
                                             cT[:, cat:cat + width], start=True, stop=True).then_inc(c_done, 1)
                    for g, (xs, at, width, cat) in enumerate(groups(half)):
                        pe.wait_ge(hidden_ready, n * G + (g + 2))
                        w2 = wb[:, KD * 2 * P:KD * 2 * P + D]
                        if g < 2:
                            for j in range(GRP // P):
                                t = g * (GRP // P) + j
                                last = nc.tensor.matmul(pout[t // 2][:, t % 2, :], hid[g][:, j * P:(j + 1) * P], w2,
                                                        start=False, stop=False, skip_group_check=True)
                        else:
                            last = nc.tensor.matmul(pex[0:NX, :], hid[2][:, 0:NX], w2,
                                                    start=False, stop=False, skip_group_check=True)
                    last.then_inc(w_used, 1)

                pe.wait_ge(zeroed, 1)
                for half in range(2):
                    pe.wait_ge(added, half * (TH // 2))
                    for i in range(TH // 2):
                        nc.tensor.matmul(pout[i][:, :, :], zero[:, 0:P], zero[:, :], start=True, stop=False,
                                         skip_group_check=True)
                    if extra:
                        nc.tensor.matmul(pex[:, :], zero[:, 0:P], zero[:, 0:D], start=True, stop=False,
                                         skip_group_check=True)
                    with pe.Fori(0, n_pieces // 2) as i:
                        for buf in range(2):
                            piece(half, 2 * i + buf, buf, i)
                    if odd:
                        piece(half, n_pieces - 1, 0, n_pieces // 2)
                    if extra:
                        pe.wait_ge(w_used, (half + 1) * n_pieces)
                        nc.tensor.matmul(pex[:, :], zero[:, 0:P], zero[:, 0:D], start=False, stop=True,
                                         skip_group_check=True).then_inc(ex_done, 1)
                        pe.wait_ge(fex_done, half + 1)
                        for t in range(TH):
                            at = half * HALF + t * P
                            nc.tensor.matmul(pout[t // 2][:, t % 2, :], extra[1][:, at:at + P], fex[0:NX, :],
                                             start=False, stop=False, skip_group_check=True)
                    for i in range(TH // 2):
                        last = nc.tensor.matmul(pout[i][:, :, :], zero[:, 0:P], zero[:, :], start=False, stop=True,
                                                skip_group_check=True)
                    last.then_inc(out_done, 1)

            @block.scalar
            def _(act):
                def piece(half, p):
                    n = p + half * n_pieces
                    for g, (xs, at, width, cat) in enumerate(groups(half)):
                        act.wait_ge(g_done, n * G + (g + 1))
                        nc.scalar.activation(gate[g % 2][:, 0:width], pg[:, 0:width], ACT.Silu).then_inc(silu_done, 1)

                act.sem_inc(silu_done, 1)
                for half in range(2):
                    with act.Fori(0, n_pieces // 2) as i:
                        for buf in range(2):
                            piece(half, 2 * i + buf)
                    if odd:
                        piece(half, n_pieces - 1)
                    if extra:
                        act.wait_ge(ex_done, half + 1)
                        nc.scalar.activation(fex[:, :], pex[:, :], ACT.Copy).then_inc(fex_done, 1)

            @block.vector
            def _(dve):
                def piece(half, p):
                    n = p + half * n_pieces
                    for g, (xs, at, width, cat) in enumerate(groups(half)):
                        m = n * G + g
                        dve.wait_ge(silu_done, m + 2)
                        dve.wait_ge(u_done, m + 1)
                        dve.wait_ge(hidden_ready, m + 1)
                        to = prod if cT is not None else hid[g]
                        last = nc.vector.tensor_tensor(to[:, 0:width], gate[g % 2][:, 0:width], pu[:, 0:width], ALU.mult)
                        last.then_inc(prod_done, 1)
                        if cT is not None:
                            dve.wait_ge(prod_done, m + 2)
                            dve.wait_ge(c_done, m + 1)
                            nc.vector.tensor_tensor(hid[g][:, 0:width], prod[:, 0:width], pc[:, 0:width],
                                                    ALU.mult).then_inc(hid_done, 1)

                nc.vector.memset(zero[:, :], 0.0).then_inc(zeroed, 1)
                dve.sem_inc(prod_done, 1)
                if cT is not None:
                    dve.sem_inc(hid_done, 1)
                for half in range(2):
                    with dve.Fori(0, n_pieces // 2) as i:
                        for buf in range(2):
                            piece(half, 2 * i + buf)
                    if odd:
                        piece(half, n_pieces - 1)
                    dve.wait_ge(out_done, half + 1)
                    for i in range(TH // 2):
                        t = half * TH + 2 * i
                        nc.vector.tensor_tensor(const["x"][:, t:t + 2, :], const["x"][:, t:t + 2, :],
                                                pout[i][:, :, :], ALU.add).then_inc(added, 1)


HS = 16
DH = D // HS
HP = 32
GH = P // HP
NCH = HS // GH
SC = P + SEQ


def attention_small(nc, name, const, xT, w, scale):
    with ExitStack() as ctx:
        sp = Space(nc, ctx, name)
        wq = sp.sb("wq", [P, KD, NCH * P])
        wk = sp.sb("wk", [P, KD, NCH * P])
        wv = sp.sb("wv", [P, KD, D])
        wo = sp.sb("wo", [P, KD, D])
        bq = sp.sb("bq", [P, NCH])
        bk = sp.sb("bk", [P, NCH])
        bv = sp.sb("bv", [1, D])
        bo = sp.sb("bo", [1, D])
        xb = sp.sb("xb", [P, KD, SEQ])
        qT = sp.sb("qT", [P, NCH, SEQ])
        kT = sp.sb("kT", [P, NCH, SEQ])
        v = sp.sb("v", [P, QT, D])
        s = sp.sb("s", [P, 2, GH, SC])
        nmax = sp.sb("nmax", [P, 2, GH, QT])
        rsum = sp.sb("rsum", [P, QT, HS])
        rinv = sp.sb("rinv", [P, QT, HS])
        pT = [sp.sb(f"pT{i}", [P, SC]) for i in range(2)]
        o = sp.sb("o", [P, QT, D])
        oT = sp.sb("oT", [P, QT, KD, P])
        ring = [sp.ps(f"ring{i}", [P, 512]) for i in range(4)]
        pv = sp.ps("pv", [P, QT, D])
        ppT = [sp.ps(f"ppT{i}", [P, 512]) for i in range(2)]
        pend = sp.ps("pend", [P, 512])
        w_in = sp.sem("w_in")
        xb_ready = sp.sem("xb_ready")
        xb_used = sp.sem("xb_used")
        proj_done = sp.sem("proj_done")
        qk_ready = sp.sem("qk_ready")
        v_ready = sp.sem("v_ready")
        s_done = sp.sem("s_done")
        s_read = sp.sem("s_read")
        max_ready = sp.sem("max_ready")
        exp_ready = sp.sem("exp_ready")
        turned = sp.sem("turned")
        even_copied = sp.sem("even_copied")
        odd_copied = sp.sem("odd_copied")
        pv_done = sp.sem("pv_done")
        inv_ready = sp.sem("inv_ready")
        o_ready = sp.sem("o_ready")
        oT_done = sp.sem("oT_done")
        oT_ready = sp.sem("oT_ready")
        out_done = sp.sem("out_done")
        added = sp.sem("added")
        ident, ones, cmask = const["ident"], const["ones"], const["cmask"]
        blocks = [(0, 0, 0), (1, 0, P), (1, 1, 2 * P)]

        with nc.Block() as block:
            @block.sync
            def _(sync):
                for to, what in ((wq, "wq"), (wk, "wk"), (wv, "wv"), (wo, "wo")):
                    sync.dma_start(to[:, :, :], w[what]).then_inc(w_in, 16)
                for to, what in ((bq, "bq"), (bk, "bk"), (bv, "bv"), (bo, "bo")):
                    sync.dma_start(to[:, :], w[what]).then_inc(w_in, 16)

            @block.gpsimd
            def _(pool):
                with pool.Fori(0, NB) as b:
                    pool.wait_ge(xb_used, b + 1)
                    nc.gpsimd.tensor_copy(xb[:, :, :], xT[:, :, bass.ds(b * SEQ, SEQ)]).then_inc(xb_ready, 1)

            @block.tensor
            def _(pe):
                pe.sem_inc(xb_used, 1)
                pe.sem_inc(turned, 1 + GH)
                pe.wait_ge(w_in, 16 * 8)
                with pe.Fori(0, NB) as b:
                    def scores(j):
                        for h in range(j * GH, (j + 1) * GH):
                            r = (h % GH) * HP
                            if h >= 4:
                                pe.wait_ge(s_read, b * HS + (h - 2))
                            nc.tensor.matmul(ring[h % 4][:, 0:P], qT[r:r + HP, j, 0:P], kT[r:r + HP, j, 0:P],
                                             start=True, stop=True)
                            nc.tensor.matmul(ring[h % 4][:, P:SC], qT[r:r + HP, j, P:SEQ], kT[r:r + HP, j, :],
                                             start=True, stop=True).then_inc(s_done, 1)

                    def turn(h):
                        pe.wait_ge(exp_ready, b * HS + (h + 1))
                        pe.wait_ge(odd_copied if h % 2 else even_copied, b * (HS // 2) + (h // 2 + 1))
                        for i in range(3):
                            last = nc.tensor.transpose(ppT[h % 2][:, i * P:(i + 1) * P],
                                                       s[:, (h // GH) % 2, h % GH, i * P:(i + 1) * P], ident[:, :])
                        last.then_inc(turned, 1)

                    def values(h):
                        pe.wait_ge(odd_copied if h % 2 else even_copied, b * (HS // 2) + (h // 2 + 2))
                        for qt, kt, at in blocks:
                            last = nc.tensor.matmul(pv[:, qt, h * DH:(h + 1) * DH], pT[h % 2][:, at:at + P],
                                                    v[:, kt, h * DH:(h + 1) * DH], start=(kt == 0), stop=(kt == qt))
                        if h == HS - 1:
                            last.then_inc(pv_done, 1)

                    pe.wait_ge(xb_ready, b + 1)
                    pe.wait_ge(s_read, b * HS + 1)
                    for n, wt in enumerate((wq, wk)):
                        for j in range(NCH):
                            for k in range(KD):
                                last = nc.tensor.matmul(ring[2 * n + j // 2][:, (j % 2) * SEQ:(j % 2 + 1) * SEQ],
                                                        wt[:, k, j * P:(j + 1) * P], xb[:, k, :],
                                                        start=(k == 0), stop=(k == KD - 1))
                        last.then_inc(proj_done, 1)
                    pe.wait_ge(o_ready, b + 1)
                    for t in range(QT):
                        for k in range(KD):
                            nc.tensor.matmul(pv[:, t, :], xb[:, k, t * P:(t + 1) * P], wv[:, k, :],
                                             start=(k == 0), stop=False)
                        last = nc.tensor.matmul(pv[:, t, :], ones[0:1, :], bv[:, :], start=False, stop=True)
                    last.then_inc(proj_done, 1)
                    pe.wait_ge(qk_ready, 2 * b + 2)
                    scores(0)
                    pe.wait_ge(v_ready, b + 1)
                    for j in range(NCH):
                        if j + 1 < NCH:
                            scores(j + 1)
                        for h in range(j * GH, (j + 1) * GH):
                            turn(h)
                            if h:
                                values(h - 1)
                    values(HS - 1)
                    pe.wait_ge(o_ready, b + 2)
                    pe.wait_ge(added, b + 1)
                    for t in range(QT):
                        for k in range(KD):
                            at = (t * KD + k) * P
                            last = nc.tensor.transpose(pend[:, at:at + P], o[:, t, k * P:(k + 1) * P], ident[:, :])
                    last.then_inc(oT_done, 1)
                    pe.wait_ge(oT_ready, b + 1)
                    for t in range(QT):
                        for k in range(KD):
                            nc.tensor.matmul(pend[:, t * D:(t + 1) * D], oT[:, t, k, :], wo[:, k, :],
                                             start=(k == 0), stop=False)
                        last = nc.tensor.matmul(pend[:, t * D:(t + 1) * D], ones[0:1, :], bo[:, :],
                                                start=False, stop=True)
                    last.then_inc(out_done, 1)

            @block.scalar
            def _(act):
                act.sem_inc(even_copied, 1)
                with act.Fori(0, NB) as b:
                    def exps(j):
                        act.wait_ge(max_ready, b * NCH + (j + 1))
                        for g in range(GH):
                            h = j * GH + g
                            for t, (lo, hi) in enumerate(((0, P), (P, SC))):
                                last = nc.scalar.activation(s[:, j % 2, g, lo:hi], s[:, j % 2, g, lo:hi], ACT.Exp,
                                                            bias=nmax[:, j % 2, g, t:t + 1],
                                                            accum_out=rsum[:, t, h:h + 1])
                            last.then_inc(exp_ready, 1)

                    for n, (to, bias) in enumerate(((qT, bq), (kT, bk))):
                        act.wait_ge(proj_done, 3 * b + (n + 1))
                        for j in range(NCH):
                            last = nc.scalar.activation(to[:, j, :], ring[2 * n + j // 2][:, (j % 2) * SEQ:(j % 2 + 1) * SEQ],
                                                        ACT.Identity, bias=bias[:, j:j + 1])
                        last.then_inc(qk_ready, 1)
                    exps(0)
                    for j in range(NCH):
                        if j + 1 < NCH:
                            exps(j + 1)
                        for h in range(j * GH, (j + 1) * GH, 2):
                            act.wait_ge(turned, b * HS + (h + 2 + GH))
                            nc.scalar.activation(pT[0][:, :], ppT[0][:, 0:SC], ACT.Copy).then_inc(even_copied, 1)
                    act.wait_ge(oT_done, b + 1)
                    nc.scalar.activation(oT[:, :, :, :], pend[:, :].rearrange("p (t k c) -> p t k c", t=QT, k=KD),
                                         ACT.Copy).then_inc(oT_ready, 1)

            @block.vector
            def _(dve):
                dve.sem_inc(s_read, 1)
                dve.sem_inc(odd_copied, 1)
                dve.sem_inc(o_ready, 1)
                dve.sem_inc(added, 1)
                with dve.Fori(0, NB) as b:
                    def maxima(j):
                        dve.wait_ge(turned, b * HS + (j * GH + 1))
                        for g in range(GH):
                            h = j * GH + g
                            dve.wait_ge(s_done, b * HS + (h + 1))
                            nc.vector.scalar_tensor_tensor(out=s[:, j % 2, g, :], in0=ring[h % 4][:, 0:SC], scalar=scale,
                                                           in1=cmask[:, :], op0=ALU.mult, op1=ALU.add).then_inc(s_read, 1)
                        dve.wait_ge(s_read, b * HS + (j * GH + GH + 1))
                        nc.vector.tensor_reduce(nmax[:, j % 2, :, 0], s[:, j % 2, :, 0:P], AX_X, ALU.max, negate=True)
                        nc.vector.tensor_reduce(nmax[:, j % 2, :, 1], s[:, j % 2, :, P:SC], AX_X, ALU.max,
                                                negate=True).then_inc(max_ready, 1)

                    dve.wait_ge(proj_done, 3 * b + 3)
                    nc.vector.tensor_copy(v[:, :, :], pv[:, :, :]).then_inc(v_ready, 1)
                    dve.sem_inc(xb_used, 1)
                    maxima(0)
                    for j in range(NCH):
                        if j + 1 < NCH:
                            maxima(j + 1)
                        for h in range(j * GH + 1, (j + 1) * GH, 2):
                            dve.wait_ge(turned, b * HS + (h + 2 + GH))
                            nc.vector.tensor_copy(pT[1][:, :], ppT[1][:, 0:SC]).then_inc(odd_copied, 1)
                    dve.wait_ge(exp_ready, (b + 1) * HS)
                    nc.vector.reciprocal(rinv[:, :, :], rsum[:, :, :]).then_inc(inv_ready, 1)
                    dve.wait_ge(inv_ready, b + 1)
                    dve.wait_ge(pv_done, b + 1)
                    nc.vector.tensor_tensor(o[:, :, :].rearrange("p t (h d) -> p (t h) d", h=HS),
                                            pv[:, :, :].rearrange("p t (h d) -> p (t h) d", h=HS),
                                            rinv[:, :, :].rearrange("p t h -> p (t h)").unsqueeze(2).broadcast_to([P, QT * HS, DH]),
                                            ALU.mult).then_inc(o_ready, 1)
                    dve.wait_ge(out_done, b + 1)
                    nc.vector.tensor_tensor(const["x"][:, bass.ds(2 * b, QT), :], const["x"][:, bass.ds(2 * b, QT), :],
                                            pend[:, :].rearrange("p (t d) -> p t d", t=QT), ALU.add).then_inc(added, 1)


HL = 2
EL = D // HL


def linear_attention(nc, name, const, xT, w, o):
    with ExitStack() as ctx:
        sp = Space(nc, ctx, name)
        wts = {n: sp.sb(n, [P, KD, D]) for n in ("wq", "wk", "wv")}
        cm = sp.sb("cm", [P, SC])
        xb = sp.sb("xb", [P, KD, SEQ])
        v = sp.sb("v", [P, QT, D])
        q = sp.sb("q", [P, HL, SEQ])
        k = sp.sb("k", [P, HL, SEQ])
        f = sp.sb("f", [P, HL, SEQ])
        a = sp.sb("a", [P, HL, SEQ])
        up = sp.sb("up", [P, HL, SEQ])
        down = sp.sb("down", [P, HL, SEQ])
        nmid = sp.sb("nmid", [P, HL, QT])
        edge = sp.sb("edge", [P, HL, 2])
        qx = sp.sb("qx", [P, HL, P])
        kx = sp.sb("kx", [P, HL, P])
        sT = sp.sb("sT", [P, HL, SC])
        pq = sp.ps("pq", [P, HL, SEQ])
        pk = sp.ps("pk", [P, HL, SEQ])
        pv = sp.ps("pv", [P, QT, D])
        psT = [sp.ps(f"psT{h}", [P, 512]) for h in range(HL)]
        po = sp.ps("po", [P, QT, D])
        w_in = sp.sem("w_in")
        xb_ready = sp.sem("xb_ready")
        q_done = sp.sem("q_done")
        k_done = sp.sem("k_done")
        v_done = sp.sem("v_done")
        v_ready = sp.sem("v_ready")
        act_done = sp.sem("act_done")
        chain = sp.sem("chain")
        dve_done = sp.sem("dve_done")
        scores_done = sp.sem("scores_done")
        scores_ready = sp.sem("scores_ready")
        o_done = sp.sem("o_done")
        o_ready = sp.sem("o_ready")
        NCHAIN = 17
        ones = const["ones"]
        tiles = [(h, t) for h in range(HL) for t in range(QT)]

        with nc.Block() as block:
            @block.sync
            def _(sync):
                for n in ("wq", "wk", "wv"):
                    sync.dma_start(wts[n][:, :, :], w[n]).then_inc(w_in, 16)
                sync.dma_start(cm[:, :], const["cmask01T_dram"]).then_inc(w_in, 16)

            @block.gpsimd
            def _(pool):
                with pool.Fori(0, NB) as b:
                    pool.wait_ge(v_done, b + 1)
                    nc.gpsimd.tensor_copy(xb[:, :, :], xT[:, :, bass.ds(b * SEQ, SEQ)]).then_inc(xb_ready, 1)

            @block.tensor
            def _(pe):
                pe.sem_inc(v_done, 1)
                pe.wait_ge(w_in, 16 * 4)
                with pe.Fori(0, NB) as b:
                    pe.wait_ge(xb_ready, b + 1)
                    pe.wait_ge(scores_ready, 2 * b + 1)
                    for to, n, done in ((pk, "wk", k_done), (pq, "wq", q_done)):
                        for h in range(HL):
                            for c in range(KD):
                                last = nc.tensor.matmul(to[:, h, :], wts[n][:, c, h * EL:(h + 1) * EL], xb[:, c, :],
                                                        start=(c == 0), stop=(c == KD - 1))
                        last.then_inc(done, 1)
                    for t in range(QT):
                        for c in range(KD):
                            last = nc.tensor.matmul(pv[:, t, :], xb[:, c, t * P:(t + 1) * P], wts["wv"][:, c, :],
                                                    start=(c == 0), stop=(c == KD - 1))
                    last.then_inc(v_done, 1)
                    pe.wait_ge(dve_done, b + 1)
                    for h in range(HL):
                        nc.tensor.matmul(psT[h][:, 0:P], k[:, h, 0:P], q[:, h, 0:P], start=True, stop=True)
                        nc.tensor.matmul(psT[h][:, P:2 * P], kx[:, h, :], qx[:, h, :], start=True, stop=True)
                        nc.tensor.matmul(psT[h][:, 2 * P:SC], k[:, h, P:SEQ], q[:, h, P:SEQ],
                                         start=True, stop=True).then_inc(scores_done, 1)
                    pe.wait_ge(v_ready, b + 1)
                    pe.wait_ge(o_ready, b + 1)
                    for h in range(HL):
                        pe.wait_ge(scores_ready, 2 * b + (h + 2))
                        for qt, kt, at in ((0, 0, 0), (1, 0, P), (1, 1, 2 * P)):
                            last = nc.tensor.matmul(po[:, qt, h * EL:(h + 1) * EL], sT[:, h, at:at + P],
                                                    v[:, kt, h * EL:(h + 1) * EL], start=(kt == 0), stop=(kt == qt))
                    last.then_inc(o_done, 1)

            @block.scalar
            def _(act):
                act.sem_inc(o_ready, 1)
                with act.Fori(0, NB) as b:
                    act.wait_ge(k_done, b + 1)
                    nc.scalar.activation(f[:, :, :], pk[:, :, :], ACT.Exp, scale=-1.0).then_inc(act_done, 1)
                    act.wait_ge(q_done, b + 1)
                    nc.scalar.activation(q[:, :, :], pq[:, :, :], ACT.Exp, scale=-1.0).then_inc(act_done, 1)
                    act.wait_ge(v_done, b + 2)
                    nc.scalar.activation(v[:, :, :], pv[:, :, :], ACT.Copy).then_inc(v_ready, 1)
                    act.wait_ge(chain, b * NCHAIN + 2)
                    nc.scalar.activation(f[:, :, :], f[:, :, :], ACT.Exp, scale=-1.0).then_inc(act_done, 1)
                    act.wait_ge(chain, b * NCHAIN + 7)
                    nc.scalar.activation(f[:, :, :], k[:, :, :], ACT.Ln).then_inc(act_done, 1)
                    act.wait_ge(chain, b * NCHAIN + 13)
                    for h, t in tiles:
                        nc.scalar.activation(up[:, h, t * P:(t + 1) * P], a[:, h, t * P:(t + 1) * P], ACT.Exp,
                                             bias=nmid[:, h, t:t + 1])
                        last = nc.scalar.activation(down[:, h, t * P:(t + 1) * P], a[:, h, t * P:(t + 1) * P], ACT.Exp,
                                                    bias=a[:, h, t * P + P // 2 - 1:t * P + P // 2], scale=-1.0)
                    last.then_inc(act_done, 1)
                    for h in range(HL):
                        nc.scalar.activation(edge[:, h, 0:1], a[:, h, P + P // 2 - 1:P + P // 2], ACT.Exp)
                        last = nc.scalar.activation(edge[:, h, 1:2], a[:, h, P - 1:P], ACT.Exp, bias=nmid[:, h, 0:1])
                    last.then_inc(act_done, 1)
                    act.wait_ge(o_done, b + 1)
                    nc.scalar.activation(o[:, bass.ds(2 * b, QT), :], po[:, :, :], ACT.Copy).then_inc(o_ready, 1)

            @block.vector
            def _(dve):
                NA = 6
                dve.sem_inc(scores_ready, 1)
                with dve.Fori(0, NB) as b:
                    ch = Chain(dve, chain, b * NCHAIN)
                    dve.wait_ge(act_done, b * NA + 1)
                    ch.link(nc.vector.tensor_scalar(f[:, :, :], f[:, :, :], 1.0, None, ALU.add))
                    ch.link(nc.vector.reciprocal(f[:, :, :], f[:, :, :]))
                    dve.wait_ge(act_done, b * NA + 2)
                    ch.link(nc.vector.tensor_scalar(q[:, :, :], q[:, :, :], 1.0, None, ALU.add))
                    ch.link(nc.vector.reciprocal(q[:, :, :], q[:, :, :]))
                    ch.link(nc.vector.tensor_tensor(q[:, :, :], q[:, :, :], pq[:, :, :], ALU.mult))
                    dve.wait_ge(act_done, b * NA + 3)
                    ch.link(nc.vector.tensor_scalar(f[:, :, :], f[:, :, :], 1.0, None, ALU.add))
                    ch.link(nc.vector.reciprocal(k[:, :, :], f[:, :, :]))
                    dve.wait_ge(act_done, b * NA + 4)
                    for h, t in tiles:
                        sl = slice(t * P, (t + 1) * P)
                        ch.link(nc.vector.tensor_tensor_scan(a[:, h, sl], ones[:, :], f[:, h, sl], 0.0, ALU.mult, ALU.add))
                    ch.link(nc.vector.tensor_scalar(k[:, :, :], k[:, :, :], -1.0, 1.0, ALU.mult, ALU.add))
                    ch.link(nc.vector.tensor_scalar(nmid[:, :, :], a[:, :, :].rearrange("p h (t c) -> p h t c", t=QT)
                                                    [:, :, :, P // 2 - 1], -1.0, None, ALU.mult))
                    dve.wait_ge(act_done, b * NA + 5)
                    ch.link(nc.vector.tensor_tensor(q[:, :, :], q[:, :, :], up[:, :, :], ALU.mult))
                    ch.link(nc.vector.tensor_tensor(k[:, :, :], k[:, :, :], down[:, :, :], ALU.mult))
                    dve.wait_ge(act_done, b * NA + 6)
                    for h in range(HL):
                        nc.vector.tensor_scalar(qx[:, h, :], q[:, h, P:SEQ], edge[:, h, 0:1], None, ALU.mult)
                        last = nc.vector.tensor_scalar(kx[:, h, :], k[:, h, 0:P], edge[:, h, 1:2], None, ALU.mult)
                        if h == 0:
                            ch.link(last)
                    ch.link(last)
                    dve.sem_inc(dve_done, 1)
                    assert ch.count == NCHAIN, ch.count
                    for h in range(HL):
                        dve.wait_ge(scores_done, 2 * b + (h + 1))
                        nc.vector.tensor_tensor(sT[:, h, :], psT[h][:, 0:SC], cm[:, :], ALU.mult).then_inc(scores_ready, 1)


def project(nc, name, const, xT, w_dram):
    with ExitStack() as ctx:
        sp = Space(nc, ctx, name)
        w = sp.sb("w", [P, KD, D])
        po = [sp.ps(f"po{i}", [P, 2, D]) for i in range(4)]
        w_in = sp.sem("w_in")
        done = sp.sem("done")
        added = sp.sem("added")
        with nc.Block() as block:
            @block.sync
            def _(sync):
                sync.dma_start(w[:, :, :], w_dram).then_inc(w_in, 16)

            @block.tensor
            def _(pe):
                pe.wait_ge(w_in, 16)
                for i in range(NT // 2):
                    if i >= 4:
                        pe.wait_ge(added, i - 3)
                    for t in (2 * i, 2 * i + 1):
                        for k in range(KD):
                            last = nc.tensor.matmul(po[i % 4][:, t % 2, :], xT[:, k, t * P:(t + 1) * P], w[:, k, :],
                                                    start=(k == 0), stop=(k == KD - 1))
                    last.then_inc(done, 1)

            @block.vector
            def _(dve):
                for i in range(NT // 2):
                    dve.wait_ge(done, i + 1)
                    nc.vector.tensor_tensor(const["x"][:, 2 * i:2 * i + 2, :], const["x"][:, 2 * i:2 * i + 2, :],
                                            po[i % 4][:, :, :], ALU.add).then_inc(added, 1)


HQ = 16
HKV = 4
GQ = HQ // HKV
HB = GQ + 1
EH = 128
NBLK = 2 * HB * QT
NTT = NBLK // 4


def attention_mixed(nc, name, const, xT, w):
    scale = float(EH) ** -0.5
    with ExitStack() as ctx:
        sp = Space(nc, ctx, name)
        wq = sp.sb("wq", [P, KD, HKV, GQ * EH])
        wkv = sp.sb("wkv", [P, KD, HKV, 2 * EH])
        wo = sp.sb("wo", [P, HQ, D])
        cos = sp.sb("cos", [P, QT, EH])
        sin = sp.sb("sin", [P, QT, EH])
        decay = sp.sb("decay", [P, QT, P])
        xb = sp.sb("xb", [P, KD, SEQ])
        qk = sp.sb("qk", [P, QT, HB, EH])
        e = sp.sb("e", [P, QT, HB, EH])
        rcos = sp.sb("rcos", [P, QT, HB, EH])
        rsin = sp.sb("rsin", [P, QT, HB, EH])
        src = sp.sb("src", [P, 2, QT, HB, EH])
        tt = sp.sb("tt", [P, 2, HB, QT, P])
        gate = sp.sb("gate", [P, QT, EH])
        up = sp.sb("up", [P, QT, EH])
        down = sp.sb("down", [P, QT, EH])
        v = sp.sb("v", [P, QT, EH])
        top = sp.sb("top", [P, QT * HB])
        total = sp.sb("total", [P, QT * HB])
        inv_next = sp.sb("inv_next", [P, QT * HB])
        inv = sp.sb("inv", [P, QT * HB])
        s = [sp.sb(f"s{i}", [P, SC]) for i in range(2)]
        g = [sp.sb(f"g{i}", [P, SC]) for i in range(2)]
        nmax = [sp.sb(f"nmax{i}", [P, QT]) for i in range(2)]
        rsum = [sp.sb(f"rsum{i}", [P, QT]) for i in range(2)]
        rinv = [sp.sb(f"rinv{i}", [P, QT]) for i in range(2)]
        pT = [sp.sb(f"pT{i}", [P, SC]) for i in range(2)]
        oT = [sp.sb(f"oT{i}", [P, SEQ]) for i in range(2)]
        pq = [sp.ps(f"pq{i}", [P, 512]) for i in range(2)]
        pkv = sp.ps("pkv", [P, QT, 2 * EH])
        po = sp.ps("po", [P, SEQ])
        pS = sp.ps("pS", [P, 512])
        pG = sp.ps("pG", [P, 512])
        ppT = sp.ps("ppT", [P, 512])
        pout = sp.ps("pout", [P, QT, D])
        w_in = sp.sem("w_in")
        xb_ready = sp.sem("xb_ready")
        kv_done = sp.sem("kv_done")
        q_done = sp.sem("q_done")
        gate_exp = sp.sem("gate_exp")
        gate_ready = sp.sem("gate_ready")
        decay_done = sp.sem("decay_done")
        decay_ready = sp.sem("decay_ready")
        qk_ready = sp.sem("qk_ready")
        rotated = sp.sem("rotated")
        pool_chain = sp.sem("pool_chain")
        top_ready = sp.sem("top_ready")
        sub_ready = sp.sem("sub_ready")
        e_ready = sp.sem("e_ready")
        total_ready = sp.sem("total_ready")
        inv_ready = sp.sem("inv_ready")
        prepared = sp.sem("prepared")
        tt_done = sp.sem("tt_done")
        tt_read = sp.sem("tt_read")
        v_ready = sp.sem("v_ready")
        s_done = sp.sem("s_done")
        s_read = sp.sem("s_read")
        g_done = sp.sem("g_done")
        g_read = sp.sem("g_read")
        max_ready = sp.sem("max_ready")
        exp_ready = sp.sem("exp_ready")
        rinv_ready = sp.sem("rinv_ready")
        p_ready = sp.sem("p_ready")
        pT_done = sp.sem("pT_done")
        pT_read = sp.sem("pT_read")
        oT_done = sp.sem("oT_done")
        oT_read = sp.sem("oT_read")
        out_done = sp.sem("out_done")
        added = sp.sem("added")
        inv_moved = sp.sem("inv_moved")
        ident = const["ident"]
        spans = ((0, P), (P, SC))

        def steps(eng, run):
            with eng.Fori(0, NB - 1) as b:
                for gr in range(HKV):
                    i = b * HKV + gr
                    nxt = (i + 1, b, gr + 1) if gr + 1 < HKV else (b * HKV + HKV, b + 1, 0)
                    run(i, b, gr, nxt)
            for gr in range(HKV):
                i = (NB - 1) * HKV + gr
                run(i, NB - 1, gr, (i + 1, NB - 1, gr + 1) if gr + 1 < HKV else None)

        with nc.Block() as block:
            @block.sync
            def _(sync):
                sync.dma_start(wkv[:, :, :, :], w["wkv"]).then_inc(w_in, 16)
                sync.dma_start(wq[:, :, :, :], w["wq"]).then_inc(w_in, 16)
                for to, n in ((cos, "cos"), (sin, "sin"), (decay, "decay"), (wo, "wo")):
                    sync.dma_start(to[:, :, :], w[n]).then_inc(w_in, 16)

            @block.gpsimd
            def _(pool):
                def load(b):
                    nc.gpsimd.tensor_copy(xb[:, :, :], xT[:, :, bass.ds(b * SEQ, SEQ)]).then_inc(xb_ready, 1)

                def rotate(n):
                    pool.wait_ge(qk_ready, n + 1)
                    wide = [P, QT, HB, EH]
                    half = [P, QT, HB, EH // 2]
                    nc.gpsimd.tensor_tensor(rcos[:, :, :, :], qk[:, :, :, :],
                                            cos[:, :, :].unsqueeze(2).broadcast_to(wide), ALU.mult).then_inc(pool_chain, 1)
                    nc.gpsimd.tensor_tensor(rsin[:, :, :, 0:EH // 2], qk[:, :, :, EH // 2:EH],
                                            sin[:, :, 0:EH // 2].unsqueeze(2).broadcast_to(half),
                                            ALU.mult).then_inc(pool_chain, 1)
                    nc.gpsimd.tensor_tensor(rsin[:, :, :, EH // 2:EH], qk[:, :, :, 0:EH // 2],
                                            sin[:, :, EH // 2:EH].unsqueeze(2).broadcast_to(half),
                                            ALU.mult).then_inc(pool_chain, 1)
                    pool.wait_ge(pool_chain, 3 * n + 3)
                    nc.gpsimd.tensor_tensor(src[:, 0, :, :, :], rcos[:, :, :, :], rsin[:, :, :, :],
                                            ALU.add).then_inc(rotated, 1)

                pool.wait_ge(w_in, 16 * 6)
                nc.gpsimd.tensor_copy(xb[:, :, :], xT[:, :, 0:SEQ]).then_inc(xb_ready, 1)
                rotate(0)

                def run(i, b, gr, nxt):
                    if nxt:
                        if gr == HKV - 1:
                            pool.wait_ge(q_done, i + 1)
                            load(nxt[1])
                        rotate(nxt[0])

                steps(pool, run)

            @block.tensor
            def _(pe):
                def project(n, b, gr):
                    if gr == 0:
                        pe.wait_ge(xb_ready, b + 1)
                    pe.wait_ge(tt_read, n * NTT + 1)
                    pe.wait_ge(v_ready, n + 1)
                    for t in range(QT):
                        for k in range(KD):
                            last = nc.tensor.matmul(pkv[:, t, :], xb[:, k, t * P:(t + 1) * P], wkv[:, k, gr, :],
                                                    start=(k == 0), stop=(k == KD - 1))
                    last.then_inc(kv_done, 1)
                    for t in range(QT):
                        for k in range(KD):
                            last = nc.tensor.matmul(pq[t][:, :], xb[:, k, t * P:(t + 1) * P], wq[:, k, gr, :],
                                                    start=(k == 0), stop=(k == KD - 1))
                    last.then_inc(q_done, 1)

                def decays(n):
                    pe.wait_ge(gate_ready, n + 1)
                    for t in range(QT):
                        last = nc.tensor.matmul(pkv[:, t, 0:EH], decay[:, t, :], gate[:, t, :],
                                                start=True, stop=True)
                    last.then_inc(decay_done, 1)

                def turn(n):
                    pe.wait_ge(prepared, n + 1)
                    for m in range(NTT):
                        if m >= 2:
                            pe.wait_ge(tt_read, n * NTT + m)
                        for c in range(4):
                            blk = 4 * m + c
                            kind, h, t = blk // (HB * QT), blk // QT % HB, blk % QT
                            last = nc.tensor.transpose(pq[m % 2][:, c * P:(c + 1) * P], src[:, kind, t, h, :],
                                                       ident[:, :])
                        last.then_inc(tt_done, 1)

                def scores(i, h):
                    for kind, bank, read, done in ((0, pS, s_read, s_done), (1, pG, g_read, g_done)):
                        pe.wait_ge(read, i * GQ + (h + 1))
                        nc.tensor.matmul(bank[:, 0:P], tt[:, kind, h, 0, :], tt[:, kind, GQ, 0, :], start=True, stop=True)
                        nc.tensor.matmul(bank[:, P:SC], tt[:, kind, h, 1, :], tt[:, kind, GQ, :, :],
                                         start=True, stop=True).then_inc(done, 1)

                def turn_p(i, h):
                    pe.wait_ge(p_ready, i * GQ + (h + 1))
                    pe.wait_ge(pT_read, i * GQ + (h + 1))
                    for c in range(3):
                        last = nc.tensor.transpose(ppT[:, c * P:(c + 1) * P], s[h % 2][:, c * P:(c + 1) * P], ident[:, :])
                    last.then_inc(pT_done, 1)

                def values(i, h):
                    pe.wait_ge(pT_read, i * GQ + (h + 2))
                    pe.wait_ge(oT_read, i * GQ + (h + 1))
                    nc.tensor.matmul(po[:, :], v[:, 0, :], pT[h % 2][:, 0:SEQ], start=True, stop=False,
                                     skip_group_check=True)
                    nc.tensor.matmul(po[:, P:SEQ], v[:, 1, :], pT[h % 2][:, SEQ:SC], start=False, stop=True,
                                     skip_group_check=True).then_inc(oT_done, 1)

                def output(i, gr, h):
                    pe.wait_ge(oT_read, i * GQ + (h + 2))
                    if h == 0:
                        pe.wait_ge(added, i + 1)
                    for t in range(QT):
                        last = nc.tensor.matmul(pout[:, t, :], oT[h % 2][:, t * P:(t + 1) * P], wo[:, gr * GQ + h, :],
                                                start=(h == 0 and t == 0), stop=(h == GQ - 1), skip_group_check=True)
                    if h == GQ - 1:
                        last.then_inc(out_done, 1)

                def run(i, b, gr, nxt):
                    if nxt:
                        project(*nxt)
                    pe.wait_ge(tt_read, i * NTT + (NTT + 1))
                    pe.wait_ge(v_ready, i + 2)
                    scores(i, 0)
                    for h in range(GQ):
                        if h + 1 < GQ:
                            scores(i, h + 1)
                        turn_p(i, h)
                        if h:
                            output(i, gr, h - 1)
                        values(i, h)
                        if h == 0 and nxt:
                            decays(nxt[0])
                    output(i, gr, GQ - 1)
                    if nxt:
                        turn(nxt[0])

                pe.wait_ge(w_in, 16 * 6)
                project(0, 0, 0)
                decays(0)
                turn(0)
                steps(pe, run)

            @block.scalar
            def _(act):
                act.sem_inc(tt_read, 1)
                act.sem_inc(v_ready, 1)
                act.sem_inc(pT_read, 1)
                act.sem_inc(oT_read, 1)

                def gates(n):
                    act.wait_ge(kv_done, n + 1)
                    nc.scalar.activation(gate[:, :, :], pkv[:, :, 0:EH], ACT.Exp, scale=-1.0).then_inc(gate_exp, 1)
                    nc.scalar.activation(qk[:, :, GQ, :], pkv[:, :, 0:EH], ACT.Copy)
                    act.wait_ge(gate_exp, n + 1)
                    nc.scalar.activation(gate[:, :, :], gate[:, :, :], ACT.Ln, bias=1.0).then_inc(gate_ready, 1)
                    act.wait_ge(q_done, n + 1)
                    for t in range(QT):
                        last = nc.scalar.activation(qk[:, t, 0:GQ, :], pq[t][:, :].rearrange("p (h e) -> p h e", h=GQ),
                                                    ACT.Copy)
                    last.then_inc(qk_ready, 1)

                def softmax_exps(n):
                    act.wait_ge(sub_ready, n + 1)
                    nc.scalar.activation(e[:, :, :, :], e[:, :, :, :], ACT.Exp).then_inc(e_ready, 1)

                def decay_exps(n):
                    act.wait_ge(decay_done, n + 1)
                    nc.scalar.activation(up[:, :, :], pkv[:, :, 0:EH], ACT.Exp)
                    nc.scalar.activation(down[:, :, :], pkv[:, :, 0:EH], ACT.Exp,
                                         scale=-1.0).then_inc(decay_ready, 1)

                def copies(n):
                    for m in range(NTT):
                        act.wait_ge(tt_done, n * NTT + (m + 1))
                        flat = tt[:, :, :, :, :].rearrange("p a h t c -> p (a h t) c")
                        nc.scalar.activation(flat[:, 4 * m:4 * m + 4, :],
                                             pq[m % 2][:, :].rearrange("p (a c) -> p a c", a=4), ACT.Copy).then_inc(tt_read, 1)
                    nc.scalar.activation(v[:, :, :], pkv[:, :, EH:2 * EH], ACT.Copy).then_inc(v_ready, 1)

                def exps(i, h):
                    act.wait_ge(max_ready, i * GQ + (h + 1))
                    for t, (lo, hi) in enumerate(spans):
                        last = nc.scalar.activation(s[h % 2][:, lo:hi], s[h % 2][:, lo:hi], ACT.Exp,
                                                    bias=nmax[h % 2][:, t:t + 1], accum_out=rsum[h % 2][:, t:t + 1])
                    last.then_inc(exp_ready, 1)

                def outs(i, h):
                    act.wait_ge(pT_done, i * GQ + (h + 1))
                    nc.scalar.activation(pT[h % 2][:, :], ppT[:, 0:SC], ACT.Copy).then_inc(pT_read, 1)
                    act.wait_ge(oT_done, i * GQ + (h + 1))
                    nc.scalar.activation(oT[h % 2][:, :], po[:, :], ACT.Copy, scale=0.5).then_inc(oT_read, 1)

                def run(i, b, gr, nxt):
                    exps(i, 0)
                    if nxt:
                        gates(nxt[0])
                    exps(i, 1)
                    outs(i, 0)
                    if nxt:
                        softmax_exps(nxt[0])
                    exps(i, 2)
                    outs(i, 1)
                    if nxt:
                        decay_exps(nxt[0])
                    exps(i, 3)
                    outs(i, 2)
                    outs(i, 3)
                    if nxt:
                        copies(nxt[0])

                gates(0)
                softmax_exps(0)
                decay_exps(0)
                copies(0)
                steps(act, run)

            @block.vector
            def _(dve):
                dve.sem_inc(s_read, 1)
                dve.sem_inc(g_read, 1)
                dve.sem_inc(added, 1)
                nf = "p t h e -> p (t h) e"

                def shift(n):
                    dve.wait_ge(qk_ready, n + 1)
                    nc.vector.tensor_reduce(top[:, :], qk[:, :, :, :].rearrange(nf), AX_X, ALU.max).then_inc(top_ready, 1)
                    dve.wait_ge(top_ready, n + 1)
                    nc.vector.tensor_tensor(e[:, :, :, :].rearrange(nf), qk[:, :, :, :].rearrange(nf),
                                            top[:, :].unsqueeze(2).broadcast_to([P, QT * HB, EH]),
                                            ALU.subtract).then_inc(sub_ready, 1)

                def sums(n):
                    dve.wait_ge(e_ready, n + 1)
                    nc.vector.tensor_reduce(total[:, :], e[:, :, :, :].rearrange(nf), AX_X, ALU.add).then_inc(total_ready, 1)
                    dve.wait_ge(total_ready, n + 1)
                    nc.vector.reciprocal(inv_next[:, :], total[:, :]).then_inc(inv_ready, 1)

                def decay(n):
                    dve.wait_ge(inv_ready, n + 1)
                    dve.wait_ge(decay_ready, n + 1)
                    for t in range(QT):
                        nc.vector.scalar_tensor_tensor(out=src[:, 1, t, GQ, :], in0=e[:, t, GQ, :],
                                                       scalar=inv_next[:, t * HB + GQ:t * HB + GQ + 1],
                                                       in1=down[:, t, :], op0=ALU.mult, op1=ALU.mult)
                    nc.vector.tensor_tensor(src[:, 1, :, 0:GQ, :], e[:, :, 0:GQ, :],
                                            up[:, :, :].unsqueeze(2).broadcast_to([P, QT, GQ, EH]), ALU.mult)
                    dve.wait_ge(rotated, n + 1)

                def maxima(i, h):
                    dve.wait_ge(s_done, i * GQ + (h + 1))
                    nc.vector.scalar_tensor_tensor(out=s[h % 2][:, :], in0=pS[:, 0:SC], scalar=scale,
                                                   in1=const["cmask"][:, :], op0=ALU.mult, op1=ALU.add).then_inc(s_read, 1)
                    dve.wait_ge(s_read, i * GQ + (h + 2))
                    for t, (lo, hi) in enumerate(spans):
                        last = nc.vector.tensor_reduce(nmax[h % 2][:, t:t + 1], s[h % 2][:, lo:hi], AX_X, ALU.max,
                                                       negate=True)
                    last.then_inc(max_ready, 1)
                    dve.wait_ge(g_done, i * GQ + (h + 1))
                    for t, (lo, hi) in enumerate(spans):
                        last = nc.vector.scalar_tensor_tensor(out=g[h % 2][:, lo:hi], in0=pG[:, lo:hi],
                                                              scalar=inv[:, t * HB + h:t * HB + h + 1],
                                                              in1=const["cmask01"][:, lo:hi], op0=ALU.mult, op1=ALU.mult)
                    last.then_inc(g_read, 1)

                def join(i, h):
                    dve.wait_ge(exp_ready, i * GQ + (h + 1))
                    nc.vector.reciprocal(rinv[h % 2][:, :], rsum[h % 2][:, :]).then_inc(rinv_ready, 1)
                    dve.wait_ge(rinv_ready, i * GQ + (h + 1))
                    dve.wait_ge(g_read, i * GQ + (h + 2))
                    for t, (lo, hi) in enumerate(spans):
                        last = nc.vector.scalar_tensor_tensor(out=s[h % 2][:, lo:hi], in0=s[h % 2][:, lo:hi],
                                                              scalar=rinv[h % 2][:, t:t + 1], in1=g[h % 2][:, lo:hi],
                                                              op0=ALU.mult, op1=ALU.add)
                    last.then_inc(p_ready, 1)

                def finish_prepare(n):
                    nc.vector.tensor_copy(inv[:, :], inv_next[:, :]).then_inc(prepared, 1)

                def run(i, b, gr, nxt):
                    dve.wait_ge(prepared, i + 1)
                    maxima(i, 0)
                    if nxt:
                        shift(nxt[0])
                    maxima(i, 1)
                    join(i, 0)
                    dve.wait_ge(pT_done, i * GQ + 1)
                    maxima(i, 2)
                    join(i, 1)
                    if nxt:
                        sums(nxt[0])
                    dve.wait_ge(pT_done, i * GQ + 2)
                    maxima(i, 3)
                    join(i, 2)
                    if nxt:
                        decay(nxt[0])
                    join(i, 3)
                    if nxt:
                        finish_prepare(nxt[0])
                    dve.wait_ge(out_done, i + 1)
                    nc.vector.tensor_tensor(const["x"][:, bass.ds(2 * b, QT), :], const["x"][:, bass.ds(2 * b, QT), :],
                                            pout[:, :, :], ALU.add).then_inc(added, 1)

                shift(0)
                sums(0)
                decay(0)
                finish_prepare(0)
                steps(dve, run)


def program(nc, a, out):
    with ExitStack() as ctx:
        sp = Space(nc, ctx, "all")
        const = {"x": sp.sb("x", [P, NT, D])}
        for c in CONSTS:
            const[c] = sp.sb(c, list(a[c].shape))
            const[c + "_dram"] = a[c]
        const["cmask01T_dram"] = a["cmask01T"]
        const["order_dram"] = a["order"]
        xn = sp.sb("xn", [P, NT, D])
        xT = sp.sb("xT", [P, KD, TOK])
        setup(nc, a["X"], const)
        if "0a" in STAGES or "0f" in STAGES:
            normalize(nc, "n0", const["x"], const, xn, xT, 1e-5, False)
        if "0a" in STAGES:
            attention_small(nc, "a0", const, xT, {k: a["L0_" + k] for k in SMALL}, 0.25)
        if "0f" in STAGES:
            with nc.sbuf_tensor("cT0", [17, TOK], F32) as cT:
                route(nc, "r0", const, xT, a["L0_Wg"], 16, 4, cT, groups=(4, 2), renorm=False)
                gated_ffn(nc, "f0", const, xT, a["L0_bank"], 25, cT=cT)
        if "1a" in STAGES or "1f" in STAGES:
            normalize(nc, "n1", const["x"], const, xn, xT, 1e-5, False)
        if "1a" in STAGES:
            attention_mixed(nc, "a1", const, xT, {k: a["L1_" + k] for k in ("wq", "wkv", "wo", "cos", "sin", "decay")})
        if "1f" in STAGES:
            gated_ffn(nc, "f1", const, xT, a["L1_bank"], 8)
        if "2a" in STAGES or "2f" in STAGES:
            normalize(nc, "n2", const["x"], const, xn, xT, 1e-5, False)
        if "2a" in STAGES:
            with nc.sbuf_tensor("o2", [P, NT, D], F32) as o:
                linear_attention(nc, "a2", const, xT, {k: a["L2_" + k] for k in ("wq", "wk", "wv")}, o)
                normalize(nc, "n2o", o, const, o, xT, 1e-6, True, a["L2_attn_norm"])
            project(nc, "p2", const, xT, a["L2_wo"])
        if "2f" in STAGES:
            E = 32
            normalize(nc, "n2f", xn, const, xn, xT, 1e-6, True, a["L2_ffn_norm"], add_src=True)
            with (nc.sbuf_tensor("cT2", [E + 1, TOK + E], F32) as cT, nc.sbuf_tensor("cover2", [E, TOK], F32) as coverT,
                  nc.sbuf_tensor("xs2", [P, KD, E], F32) as xsT):
                route(nc, "r2", const, xT, a["L2_gate"], E, 4, cT, cap=2 * TOK * 4 // E,
                      extra=(xn, xsT, coverT, a["L2_ffn_norm"]))
                gated_ffn(nc, "f2", const, xT, a["L2_bank"], 33, cT=cT, extra=(xsT, coverT))
        if "3a" in STAGES or "3f" in STAGES:
            normalize(nc, "n3", const["x"], const, xn, xT, 1e-5, False)
        if "3a" in STAGES:
            attention_small(nc, "a3", const, xT, {k: a["L3_" + k] for k in SMALL}, 0.25)
        if "3f" in STAGES:
            with nc.sbuf_tensor("cT3", [65, TOK], F32) as cT:
                route(nc, "r3", const, xT, a["L3_router"], 64, 4, cT, bias_dram=a["L3_router_bias"], cap=32)
                gated_ffn(nc, "f3", const, xT, a["L3_bank"], 36, cT=cT)
        store(nc, out, const)


def host_layout(inp):
    f = {k: np.asarray(v) for k, v in inp.items()}
    a = {"X": f["L0_attn_X"]}

    def bank(w1, w3, w2, expert_of):
        rows = w1.shape[0]
        n = -(-rows // P)
        E = int(expert_of.max()) + 1
        b = np.zeros((n, P, KD * 2 * P + D + P), np.float32)
        for p in range(n):
            r = slice(p * P, min((p + 1) * P, rows))
            m = r.stop - r.start
            for k in range(KD):
                b[p, :, k * 2 * P:k * 2 * P + m] = w1[r, k * P:(k + 1) * P].T
                b[p, :, k * 2 * P + P:k * 2 * P + P + m] = w3[r, k * P:(k + 1) * P].T
            b[p, :m, KD * 2 * P:KD * 2 * P + D] = w2[r]
            b[p, :E, KD * 2 * P + D:][expert_of[r], np.arange(m)] = 1.0
        return b

    gu = f["L1_ffn_w_gate_up"]
    n = gu.shape[0] // 2
    a["L1_bank"] = bank(gu[:n], gu[n:], f["L1_ffn_w_down"].T, np.zeros(n, np.int64))

    def col(w):
        return w.reshape(KD, P).T

    def chan(w):
        return w.T.reshape(KD, P, -1).transpose(1, 0, 2)

    def heads_padded(w):
        z = np.zeros(w.shape[:-1] + (HS, HP), np.float32)
        z[..., :DH] = w.reshape(w.shape[:-1] + (HS, DH))
        return z.reshape(w.shape[:-1] + (HS * HP,))

    for l in ("L0_", "L3_"):
        g = l + "attn_"
        for n in "qk":
            a[l + "w" + n] = heads_padded(chan(f[g + "W" + n]))
            a[l + "b" + n] = heads_padded(f[g + "b" + n]).reshape(NCH, P).T
        for n in "vo":
            a[l + "w" + n] = chan(f[g + "W" + n])
            a[l + "b" + n] = f[g + "b" + n].reshape(1, D)
    a["L0_Wg"] = chan(f["L0_ffn_Wg"])
    E, I = f["L0_ffn_W1"].shape[:2]
    sh = f["L0_ffn_Ws1"].shape[0]
    a["L0_bank"] = bank(np.concatenate([f["L0_ffn_W1"].reshape(E * I, D), f["L0_ffn_Ws1"]]),
                        np.concatenate([f["L0_ffn_W3"].reshape(E * I, D), f["L0_ffn_Ws3"]]),
                        np.concatenate([f["L0_ffn_W2"].transpose(0, 2, 1).reshape(E * I, D), f["L0_ffn_Ws2"].T]),
                        np.concatenate([np.repeat(np.arange(E), I), np.full(sh, E)]))
    def rows(w):
        return w.reshape(KD, P, -1).transpose(1, 0, 2)

    a["L1_wq"] = rows(f["L1_attn_Wq"]).reshape(P, KD, HKV, GQ * EH)
    a["L1_wkv"] = np.concatenate([rows(f["L1_attn_W" + n]).reshape(P, KD, HKV, EH) for n in "kv"], 3)
    a["L1_wo"] = f["L1_attn_Wo"].reshape(HQ, P, D).transpose(1, 0, 2)
    for n in "qkvo":
        a["L2_w" + n] = chan(f["L2_attn_W" + n])
    a["L2_attn_norm"] = col(f["L2_attn_norm_w"])
    a["L2_gate"] = chan(f["L2_ffn_gate_w"])
    a["L2_ffn_norm"] = col(f["L2_ffn_norm_w"])
    E, I = f["L2_ffn_w2"].shape[:2]
    w13 = f["L2_ffn_w13"].transpose(0, 2, 1)
    a["L2_bank"] = bank(np.concatenate([w13[:, :I].reshape(E * I, D), f["L2_ffn_shared_gate_w"].T]),
                        np.concatenate([w13[:, I:].reshape(E * I, D), f["L2_ffn_shared_up_w"].T]),
                        np.concatenate([f["L2_ffn_w2"].reshape(E * I, D), f["L2_ffn_shared_down_w"]]),
                        np.concatenate([np.repeat(np.arange(E), I), np.full(I, E)]))
    a["L3_router"] = chan(f["L3_ffn_router_w"])
    a["L3_router_bias"] = f["L3_ffn_router_bias"].reshape(1, -1)
    E, I = f["L3_ffn_gate_w"].shape[:2]
    S, SF = f["L3_ffn_sh_gate_w"].shape[:2]
    a["L3_bank"] = bank(np.concatenate([f["L3_ffn_gate_w"].reshape(E * I, D), f["L3_ffn_sh_gate_w"].reshape(S * SF, D)]),
                        np.concatenate([f["L3_ffn_up_w"].reshape(E * I, D), f["L3_ffn_sh_up_w"].reshape(S * SF, D)]),
                        np.concatenate([f["L3_ffn_down_w"].transpose(0, 2, 1).reshape(E * I, D),
                                        f["L3_ffn_sh_down_w"].transpose(0, 2, 1).reshape(S * SF, D)]),
                        np.concatenate([np.repeat(np.arange(E), I), np.full(S * SF, E)]))

    a["order"] = np.tile(np.arange(64, 0, -1, dtype=np.float32), (P, 1))
    a["ident"] = np.eye(P, dtype=np.float32)
    tri = np.tril(np.ones((P, P), np.float32))
    ones = np.ones((P, P), np.float32)
    a["cmask01"] = np.concatenate([tri, ones, tri], 1)
    a["cmask"] = np.where(a["cmask01"] > 0, np.float32(0), np.float32(-BIG)).astype(np.float32)
    a["cmask01T"] = np.concatenate([tri.T, ones, tri.T], 1)
    freq = (1.0 / np.float32(10000.0) ** (np.arange(0, EH, 2, dtype=np.float32) / np.float32(EH))).astype(np.float32)
    angle = (np.arange(SEQ, dtype=np.float32)[:, None] * freq[None, :]).reshape(QT, P, EH // 2).transpose(1, 0, 2)
    c, s = np.cos(angle).astype(np.float32), np.sin(angle).astype(np.float32)
    a["L1_cos"] = np.concatenate([c, c], 2)
    a["L1_sin"] = np.concatenate([-s, s], 2)
    a["L1_decay"] = np.stack([(ones - tri.T) / 16, -tri.T / 16], 1).astype(np.float32)
    a["before"] = ones - tri
    a["ones"] = ones
    return a


def kernel(**inputs):
    import concourse.bacc as _bacc
    from concourse.bass_utils import run_bass_kernel_spmd as _run

    nc = _bacc.Bacc("TRN2", target_bir_lowering=False, num_devices=1)
    a = host_layout(inputs)
    arrays = {f"in_{k}": np.ascontiguousarray(v) for k, v in a.items()}
    args = {k: nc.dram_tensor(f"in_{k}", arrays[f"in_{k}"].shape, F32, kind="ExternalInput").ap() for k in a}
    out = nc.dram_tensor("out_0", (NB, SEQ, D), F32, kind="ExternalOutput").ap()
    program(nc, args, out)
    r = _run(nc, [arrays], core_ids=[0])
    return r.results[0]["out_0"]
```

```python
from contextlib import ExitStack

import numpy as np

import concourse.bass as bass
from concourse import mybir

STAGES = "0a,0f,1a,1f,2a,2f,3a,3f".split(",")

ALU = mybir.AluOpType
ACT = mybir.ActivationFunctionType
F32 = mybir.dt.float32
AX_X = mybir.AxisListType.X

P = 128
D = 256
KD = D // P
SEQ = 256
NB = 8
TOK = NB * SEQ
NT = TOK // P
QT = SEQ // P
BIG = 1.0e30
SMALL = ("wq", "wk", "wv", "wo", "bq", "bk", "bv", "bo")
CONSTS = ("ident", "cmask", "cmask01", "before", "ones")


class Chain:

    def __init__(self, eng, sem, base=0):
        self.eng, self.sem, self.base, self.count = eng, sem, base, 0

    def link(self, ins):
        self.count += 1
        ins.then_inc(self.sem, 1)
        self.eng.wait_ge(self.sem, self.base + self.count)


class Space:

    def __init__(self, nc, ctx, name):
        self.nc, self.ctx, self.name = nc, ctx, name
        self.sems = []
        ctx.callback(self.close)

    def sb(self, name, shape):
        return self.ctx.enter_context(self.nc.sbuf_tensor(f"{self.name}_{name}", shape, F32))

    def ps(self, name, shape):
        return self.ctx.enter_context(self.nc.psum_tensor(f"{self.name}_{name}", shape, F32))

    def sem(self, name):
        self.sems.append(self.nc.alloc_semaphore(name=f"{self.name}_{name}"))
        return self.sems[-1]

    def close(self):
        if self.sems:
            self.nc.clear_and_free_semaphores(self.sems)
            self.nc.all_engine_barrier()


def setup(nc, x_dram, const):
    with ExitStack() as ctx:
        load_all(nc, Space(nc, ctx, "setup"), x_dram, const)


def load_all(nc, sp, x_dram, const):
    loaded = sp.sem("loaded")
    with nc.Block() as block:
        @block.sync
        def _(sync):
            sync.dma_start(const["x"][:, :, :], x_dram.rearrange("b (s p) d -> p (b s) d", p=P)).then_inc(loaded, 16)
            for name in CONSTS:
                sync.dma_start(const[name][:, :], const[name + "_dram"]).then_inc(loaded, 16)
            sync.wait_ge(loaded, 16 * (1 + len(CONSTS)))


def store(nc, out, const):
    with ExitStack() as ctx:
        store_all(nc, Space(nc, ctx, "store"), out, const)


def store_all(nc, sp, out, const):
    stored = sp.sem("stored")
    with nc.Block() as block:
        @block.sync
        def _(sync):
            sync.dma_start(out.rearrange("b (s p) d -> p (b s) d", p=P), const["x"][:, :, :]).then_inc(stored, 16)
            sync.wait_ge(stored, 16)


def normalize(nc, name, src, const, xn, xT, eps, rms, w_dram=None, add_src=False):
    with ExitStack() as ctx:
        sp = Space(nc, ctx, name)
        stats = sp.sb("stats", [P, NT, 6])
        mv = sp.sb("mv", [P, NT, 2])
        std = sp.sb("std", [P, NT])
        rstd = sp.sb("rstd", [P, NT])
        tmp = sp.sb("tmp", [P, NT])
        epsb = sp.sb("epsb", [P, 1])
        wcol = sp.sb("wcol", [P, KD])
        pT = [sp.ps(f"pT{i}", [P, KD, P]) for i in range(2)]
        stat_done = sp.sem("stat_done")
        agg_done = sp.sem("agg_done")
        var_ready = sp.sem("var_ready")
        std_ready = sp.sem("std_ready")
        xn_ready = sp.sem("xn_ready")
        turned = sp.sem("turned")
        copied = sp.sem("copied")
        w_in = sp.sem("w_in")
        chain = sp.sem("chain")
        ident = const["ident"]
        with nc.Block() as block:
            if w_dram is not None:
                @block.sync
                def _(sync):
                    sync.dma_start(wcol[:, :], w_dram).then_inc(w_in, 16)

            @block.vector
            def _(dve):
                nc.vector.memset(epsb[:, :], eps).then_inc(chain, 1)
                if add_src:
                    nc.vector.tensor_tensor(const["x"][:, :, :], const["x"][:, :, :], src[:, :, :],
                                            ALU.add).then_inc(chain, 1)
                    dve.wait_ge(chain, 2)
                for t in range(NT):
                    nc.vector.bn_stats(stats[:, t, :], src[:, t, :]).then_inc(stat_done, 1)
                for t in range(NT):
                    dve.wait_ge(stat_done, t + 1)
                    nc.vector.bn_aggr(mv[:, t, :], stats[:, t, :]).then_inc(agg_done, 1)
                dve.wait_ge(agg_done, NT)
                if rms:
                    nc.vector.tensor_tensor(tmp[:, :], mv[:, :, 0], mv[:, :, 0], ALU.mult).then_inc(chain, 1)
                    dve.wait_ge(chain, 3 if add_src else 2)
                    nc.vector.tensor_tensor(tmp[:, :], tmp[:, :], mv[:, :, 1], ALU.add).then_inc(var_ready, 1)
                else:
                    nc.vector.tensor_copy(tmp[:, :], mv[:, :, 1]).then_inc(var_ready, 1)
                dve.wait_ge(std_ready, 1)
                nc.vector.reciprocal(rstd[:, :], std[:, :]).then_inc(std_ready, 1)
                dve.wait_ge(std_ready, 2)
                for t in range(NT):
                    if rms:
                        nc.vector.tensor_scalar(xn[:, t, :], src[:, t, :], rstd[:, t:t + 1], None,
                                                ALU.mult).then_inc(xn_ready, 1)
                    else:
                        nc.vector.tensor_scalar(xn[:, t, :], src[:, t, :], mv[:, t, 0:1], rstd[:, t:t + 1],
                                                ALU.subtract, ALU.mult).then_inc(xn_ready, 1)

            @block.tensor
            def _(pe):
                for t in range(NT):
                    pe.wait_ge(xn_ready, t + 1)
                    if t >= 2:
                        pe.wait_ge(copied, t - 1)
                    for k in range(KD):
                        last = nc.tensor.transpose(pT[t % 2][:, k, :], xn[:, t, k * P:(k + 1) * P], ident[:, :])
                    last.then_inc(turned, 1)

            @block.scalar
            def _(act):
                act.wait_ge(chain, 1)
                act.wait_ge(var_ready, 1)
                nc.scalar.activation(std[:, :], tmp[:, :], ACT.Sqrt, bias=epsb[:, 0:1]).then_inc(std_ready, 1)
                if w_dram is not None:
                    act.wait_ge(w_in, 16)
                for t in range(NT):
                    act.wait_ge(turned, t + 1)
                    if w_dram is None:
                        nc.scalar.activation(xT[:, :, t * P:(t + 1) * P], pT[t % 2][:, :, :],
                                             ACT.Copy).then_inc(copied, 1)
                    else:
                        for k in range(KD):
                            last = nc.scalar.activation(xT[:, k, t * P:(t + 1) * P], pT[t % 2][:, k, :],
                                                        ACT.Copy, scale=wcol[:, k:k + 1])
                        last.then_inc(copied, 1)


def route(nc, name, const, xT, w_dram, E, K, cT, groups=None, bias_dram=None, renorm=True, cap=None, extra=None):
    C = E + 1
    per = min(NT, 512 // E)
    banks = NT // per
    with ExitStack() as ctx:
        sp = Space(nc, ctx, name)
        w = sp.sb("w", [P, KD, E])
        bias = sp.sb("bias", [P, E])
        order = sp.sb("order", [P, E])
        lg = sp.sb("lg", [P, NT, E])
        ex = sp.sb("ex", [P, NT, E])
        key = sp.sb("key", [P, NT, E])
        sel = sp.sb("sel", [P, NT, E])
        eq = sp.sb("eq", [P, NT, E])
        c = sp.sb("c", [P, NT, C])
        m1 = sp.sb("m1", [P, NT, 1])
        m2 = sp.sb("m2", [P, NT, 1])
        plog = [sp.ps(f"plog{i}", [P, per, E]) for i in range(banks)]
        pT = [sp.ps(f"pT{i}", [P, 512]) for i in range(2)]
        w_in = sp.sem("w_in")
        logits = sp.sem("logits")
        chain = sp.sem("chain")
        shifted = sp.sem("shifted")
        exped = sp.sem("exped")
        chosen = sp.sem("chosen")
        ranked = sp.sem("ranked")
        c_ready = sp.sem("c_ready")
        turned = sp.sem("turned")
        copied = sp.sem("copied")
        if groups:
            GR, GK = groups
            gs = sp.sb("gs", [P, NT, GR])
            gsel = sp.sb("gsel", [P, NT, GR])
            geq = sp.sb("geq", [P, NT, GR])
        if cap:
            tot = sp.sb("tot", [P, NT, E])
            rank = sp.sb("rank", [P, NT, E])
            base = sp.sb("base", [P, NT, E])
            prank = [sp.ps(f"prank{i}", [P, per, E]) for i in range(banks)]
            ptot = [sp.ps(f"ptot{i}", [P, per, E]) for i in range(banks)] if banks == 1 else plog
        if extra:
            over = sp.sb("over", [P, NT, E])
            wcol = sp.sb("wcol", [P, KD])
            px = sp.ps("px", [P, KD, E])
        ident = const["ident"]
        n_in = 2 + (bias_dram is not None) + (extra is not None)
        with nc.Block() as block:
            @block.sync
            def _(sync):
                sync.dma_start(w[:, :, :], w_dram).then_inc(w_in, 16)
                sync.dma_start(order[:, :], const["order_dram"][:, 0:E]).then_inc(w_in, 16)
                if bias_dram is not None:
                    sync.dma_start(bias[:, :], bias_dram[0, :].partition_broadcast(P)).then_inc(w_in, 16)
                if extra:
                    sync.dma_start(wcol[:, :], extra[3]).then_inc(w_in, 16)

            @block.tensor
            def _(pe):
                pe.wait_ge(w_in, 16 * n_in)
                for t in range(NT):
                    for k in range(KD):
                        last = nc.tensor.matmul(plog[t // per][:, t % per, :], xT[:, k, t * P:(t + 1) * P], w[:, k, :],
                                                start=(k == 0), stop=(k == KD - 1))
                last.then_inc(logits, 1)
                if cap:
                    pe.wait_ge(chosen, 1)
                    for i in range(banks):
                        nc.tensor.matmul(prank[i][:, :, :], const["before"][:, :], sel[:, i * per:(i + 1) * per, :],
                                         start=True, stop=True)
                        last = nc.tensor.matmul(ptot[i][:, :, :], const["ones"][:, :], sel[:, i * per:(i + 1) * per, :],
                                                start=True, stop=True)
                    last.then_inc(ranked, 1)
                pe.wait_ge(c_ready, 1)
                for t in range(NT):
                    if t >= 2:
                        pe.wait_ge(copied, t - 1)
                    last = nc.tensor.transpose(pT[t % 2][0:C, 0:P], c[:, t, :], ident[:, :])
                    if extra:
                        last = nc.tensor.transpose(pT[t % 2][0:E, P:2 * P], over[:, t, :], ident[:, :])
                    last.then_inc(turned, 1)
                if extra:
                    for k in range(KD):
                        for t in range(NT):
                            last = nc.tensor.matmul(px[:, k, :], extra[0][:, t, k * P:(k + 1) * P], eq[:, t, :],
                                                    start=(t == 0), stop=(t == NT - 1))
                    last.then_inc(turned, 1)

            @block.scalar
            def _(act):
                act.wait_ge(shifted, 1)
                nc.scalar.activation(ex[:, :, :], ex[:, :, :], ACT.Exp).then_inc(exped, 1)
                for t in range(NT):
                    act.wait_ge(turned, t + 1)
                    last = nc.scalar.activation(cT[0:C, t * P:(t + 1) * P], pT[t % 2][0:C, 0:P], ACT.Copy)
                    if extra:
                        last = nc.scalar.activation(extra[2][0:E, t * P:(t + 1) * P], pT[t % 2][0:E, P:2 * P], ACT.Copy)
                    last.then_inc(copied, 1)
                if extra:
                    act.wait_ge(turned, NT + 1)
                    for k in range(KD):
                        nc.scalar.activation(extra[1][:, k, :], px[:, k, :], ACT.Copy, scale=wcol[:, k:k + 1])

            @block.vector
            def _(dve):
                ch = Chain(dve, chain)

                def wide(small, n):
                    return small[:, :, 0:1].broadcast_to([P, NT, n])

                def take_best(key, eq, sel, n, times):
                    ch.link(nc.vector.memset(sel[:, :, :], 0.0))
                    for _ in range(times):
                        ch.link(nc.vector.tensor_reduce(m1[:, :, 0], key[:, :, :], AX_X, ALU.max))
                        ch.link(nc.vector.tensor_tensor(eq[:, :, :], key[:, :, :], wide(m1, n), ALU.is_equal))
                        ch.link(nc.vector.tensor_tensor(eq[:, :, :], eq[:, :, :],
                                                        order[:, 0:n].unsqueeze(1).broadcast_to([P, NT, n]), ALU.mult))
                        ch.link(nc.vector.tensor_reduce(m1[:, :, 0], eq[:, :, :], AX_X, ALU.max))
                        ch.link(nc.vector.tensor_tensor(eq[:, :, :], eq[:, :, :], wide(m1, n), ALU.is_equal))
                        ch.link(nc.vector.scalar_tensor_tensor(out=key[:, :, :], in0=eq[:, :, :], scalar=-4 * BIG,
                                                               in1=key[:, :, :], op0=ALU.mult, op1=ALU.add))
                        ch.link(nc.vector.tensor_tensor(sel[:, :, :], sel[:, :, :], eq[:, :, :], ALU.add))

                dve.wait_ge(w_in, 16 * n_in)
                dve.wait_ge(logits, 1)
                for i in range(banks):
                    ch.link(nc.vector.tensor_copy(lg[:, i * per:(i + 1) * per, :], plog[i][:, :, :]))
                ch.link(nc.vector.tensor_reduce(m2[:, :, 0], lg[:, :, :], AX_X, ALU.max))
                nc.vector.tensor_tensor(ex[:, :, :], lg[:, :, :], wide(m2, E), ALU.subtract).then_inc(shifted, 1)
                if bias_dram is not None:
                    ch.link(nc.vector.tensor_tensor(key[:, :, :], lg[:, :, :],
                                                    bias[:, :].unsqueeze(1).broadcast_to([P, NT, E]), ALU.add))
                else:
                    ch.link(nc.vector.tensor_copy(key[:, :, :], lg[:, :, :]))
                if groups:
                    ch.link(nc.vector.tensor_reduce(gs[:, :, :], key[:, :, :].rearrange("p t (g e) -> p (t g) e", g=GR),
                                                    AX_X, ALU.max))
                    take_best(gs, geq, gsel, GR, GK)
                    ch.link(nc.vector.tensor_scalar(gsel[:, :, :], gsel[:, :, :], -1.0, BIG, ALU.add, ALU.mult))
                    kg = key[:, :, :].rearrange("p t (g e) -> p (t g) e", g=GR)
                    gg = gsel[:, :, :].rearrange("p t g -> p (t g)").unsqueeze(2).broadcast_to([P, NT * GR, E // GR])
                    ch.link(nc.vector.tensor_tensor(kg, kg, gg, ALU.add))
                take_best(key, eq, sel, E, K)
                if cap:
                    dve.sem_inc(chosen, 1)
                dve.wait_ge(exped, 1)
                if not renorm:
                    ch.link(nc.vector.tensor_reduce(m1[:, :, 0], ex[:, :, :], AX_X, ALU.add))
                ch.link(nc.vector.tensor_tensor(c[:, :, 0:E], ex[:, :, :], sel[:, :, :], ALU.mult))
                if renorm:
                    ch.link(nc.vector.tensor_reduce(m1[:, :, 0], c[:, :, 0:E], AX_X, ALU.add))
                ch.link(nc.vector.reciprocal(m2[:, :, 0], m1[:, :, 0]))
                ch.link(nc.vector.tensor_tensor(c[:, :, 0:E], c[:, :, 0:E], wide(m2, E), ALU.mult))
                ch.link(nc.vector.memset(c[:, :, E:C], 1.0))
                if cap:
                    dve.wait_ge(ranked, 1)
                    for i in range(banks):
                        ch.link(nc.vector.tensor_copy(rank[:, i * per:(i + 1) * per, :], prank[i][:, :, :]))
                        ch.link(nc.vector.tensor_copy(tot[:, i * per:(i + 1) * per, :], ptot[i][:, :, :]))
                    ch.link(nc.vector.memset(base[:, 0, :], 0.0))
                    for t in range(1, NT):
                        ch.link(nc.vector.tensor_tensor(base[:, t, :], base[:, t - 1, :], tot[:, t - 1, :], ALU.add))
                    ch.link(nc.vector.tensor_tensor(rank[:, :, :], rank[:, :, :], base[:, :, :], ALU.add))
                    if extra:
                        ch.link(nc.vector.tensor_scalar(eq[:, :, :], rank[:, :, :], float(cap - 1), None, ALU.is_equal))
                        ch.link(nc.vector.tensor_tensor(eq[:, :, :], eq[:, :, :], sel[:, :, :], ALU.mult))
                        ch.link(nc.vector.tensor_scalar(over[:, :, :], rank[:, :, :], float(cap), None, ALU.is_ge))
                        ch.link(nc.vector.tensor_tensor(over[:, :, :], over[:, :, :], c[:, :, 0:E], ALU.mult))
                        ch.link(nc.vector.memset(cT[:, TOK:TOK + E], 0.0))
                        ch.link(nc.vector.tensor_copy(cT[0:E, TOK:TOK + E], ident[0:E, 0:E]))
                    ch.link(nc.vector.tensor_scalar(rank[:, :, :], rank[:, :, :], float(cap), None, ALU.is_lt))
                    ch.link(nc.vector.tensor_tensor(c[:, :, 0:E], c[:, :, 0:E], rank[:, :, :], ALU.mult))
                dve.sem_inc(c_ready, 1)


HALF = TOK // 2
GRP = 512


def gated_ffn(nc, name, const, xT, bank, n_pieces, cT=None, extra=None):
    E = cT.shape[0] if cT is not None else 0
    WB = bank.shape[2]
    NX = extra[0].shape[2] if extra else 0
    G = 3 if extra else 2
    TH = HALF // P
    with ExitStack() as ctx:
        sp = Space(nc, ctx, name)
        w = [sp.sb(f"w{i}", [P, WB]) for i in range(2)]
        gate = [sp.sb(f"gate{g}", [P, GRP]) for g in range(2)]
        prod = sp.sb("prod", [P, GRP])
        hid = [sp.sb(f"hid{g}", [P, GRP]) for g in range(3)]
        zero = sp.sb("zero", [1, 512])
        pg = sp.ps("pg", [P, GRP])
        pu = sp.ps("pu", [P, GRP])
        pc = sp.ps("pc", [P, GRP])
        pout = [sp.ps(f"pout{i}", [P, 2, D]) for i in range(TH // 2)]
        if extra:
            pex = sp.ps("pex", [P, D])
            fex = sp.sb("fex", [P, D])
        w_in = [sp.sem(f"w_in{i}") for i in range(2)]
        w_used = sp.sem("w_used")
        zeroed = sp.sem("zeroed")
        g_done = sp.sem("g_done")
        u_done = sp.sem("u_done")
        c_done = sp.sem("c_done")
        silu_done = sp.sem("silu_done")
        prod_done = sp.sem("prod_done")
        hid_done = sp.sem("hid_done")
        ex_done = sp.sem("ex_done")
        fex_done = sp.sem("fex_done")
        out_done = sp.sem("out_done")
        added = sp.sem("added")

        hidden_ready = hid_done if cT is not None else prod_done
        odd = n_pieces % 2
        per_buf = [(n_pieces + 1) // 2, n_pieces // 2]

        def groups(half):
            at = [(xT, half * HALF + g * GRP, GRP, half * HALF + g * GRP) for g in range(2)]
            return at + ([(extra[0], 0, NX, TOK)] if extra else [])

        with nc.Block() as block:
            @block.sync
            def _(sync):
                def load(p, buf):
                    sync.dma_start(w[buf][:, :], bank[bass.ds(p, 1), :, :].rearrange("a p w -> p (a w)")
                                   ).then_inc(w_in[buf], 16)

                for half in range(2):
                    done = half * n_pieces
                    for buf in range(2):
                        if half:
                            sync.wait_ge(w_used, done - 1 + buf + (odd if buf == 0 else 0))
                        load(buf, buf)
                    with sync.Fori(1, n_pieces // 2) as i:
                        for buf in range(2):
                            sync.wait_ge(w_used, 2 * i + (done + buf - 1))
                            load(2 * i + buf, buf)
                    if odd:
                        sync.wait_ge(w_used, done + n_pieces - 2)
                        load(n_pieces - 1, 0)

            @block.tensor
            def _(pe):
                def piece(half, p, buf, turn):
                    n = p + half * n_pieces
                    pe.wait_ge(w_in[buf], turn * 16 + 16 * (half * per_buf[buf] + 1))
                    wb = w[buf]
                    for g, (xs, at, width, cat) in enumerate(groups(half)):
                        m = n * G + g
                        pe.wait_ge(silu_done, m + 1)
                        for k in range(KD):
                            last = nc.tensor.matmul(pg[:, 0:width], wb[:, k * 2 * P:k * 2 * P + P],
                                                    xs[:, k, at:at + width], start=(k == 0), stop=(k == KD - 1))
                        last.then_inc(g_done, 1)
                        pe.wait_ge(prod_done, m + 1)
                        for k in range(KD):
                            last = nc.tensor.matmul(pu[:, 0:width], wb[:, k * 2 * P + P:(k + 1) * 2 * P],
                                                    xs[:, k, at:at + width], start=(k == 0), stop=(k == KD - 1))
                        last.then_inc(u_done, 1)
                        if cT is not None:
                            pe.wait_ge(hid_done, m + 1)
                            nc.tensor.matmul(pc[:, 0:width], wb[0:E, KD * 2 * P + D:KD * 2 * P + D + P],
                                             cT[:, cat:cat + width], start=True, stop=True).then_inc(c_done, 1)
                    for g, (xs, at, width, cat) in enumerate(groups(half)):
                        pe.wait_ge(hidden_ready, n * G + (g + 2))
                        w2 = wb[:, KD * 2 * P:KD * 2 * P + D]
                        if g < 2:
                            for j in range(GRP // P):
                                t = g * (GRP // P) + j
                                last = nc.tensor.matmul(pout[t // 2][:, t % 2, :], hid[g][:, j * P:(j + 1) * P], w2,
                                                        start=False, stop=False, skip_group_check=True)
                        else:
                            last = nc.tensor.matmul(pex[0:NX, :], hid[2][:, 0:NX], w2,
                                                    start=False, stop=False, skip_group_check=True)
                    last.then_inc(w_used, 1)

                pe.wait_ge(zeroed, 1)
                for half in range(2):
                    pe.wait_ge(added, half * (TH // 2))
                    for i in range(TH // 2):
                        nc.tensor.matmul(pout[i][:, :, :], zero[:, 0:P], zero[:, :], start=True, stop=False,
                                         skip_group_check=True)
                    if extra:
                        nc.tensor.matmul(pex[:, :], zero[:, 0:P], zero[:, 0:D], start=True, stop=False,
                                         skip_group_check=True)
                    with pe.Fori(0, n_pieces // 2) as i:
                        for buf in range(2):
                            piece(half, 2 * i + buf, buf, i)
                    if odd:
                        piece(half, n_pieces - 1, 0, n_pieces // 2)
                    if extra:
                        pe.wait_ge(w_used, (half + 1) * n_pieces)
                        nc.tensor.matmul(pex[:, :], zero[:, 0:P], zero[:, 0:D], start=False, stop=True,
                                         skip_group_check=True).then_inc(ex_done, 1)
                        pe.wait_ge(fex_done, half + 1)
                        for t in range(TH):
                            at = half * HALF + t * P
                            nc.tensor.matmul(pout[t // 2][:, t % 2, :], extra[1][:, at:at + P], fex[0:NX, :],
                                             start=False, stop=False, skip_group_check=True)
                    for i in range(TH // 2):
                        last = nc.tensor.matmul(pout[i][:, :, :], zero[:, 0:P], zero[:, :], start=False, stop=True,
                                                skip_group_check=True)
                    last.then_inc(out_done, 1)

            @block.scalar
            def _(act):
                def piece(half, p):
                    n = p + half * n_pieces
                    for g, (xs, at, width, cat) in enumerate(groups(half)):
                        act.wait_ge(g_done, n * G + (g + 1))
                        nc.scalar.activation(gate[g % 2][:, 0:width], pg[:, 0:width], ACT.Silu).then_inc(silu_done, 1)

                act.sem_inc(silu_done, 1)
                for half in range(2):
                    with act.Fori(0, n_pieces // 2) as i:
                        for buf in range(2):
                            piece(half, 2 * i + buf)
                    if odd:
                        piece(half, n_pieces - 1)
                    if extra:
                        act.wait_ge(ex_done, half + 1)
                        nc.scalar.activation(fex[:, :], pex[:, :], ACT.Copy).then_inc(fex_done, 1)

            @block.vector
            def _(dve):
                def piece(half, p):
                    n = p + half * n_pieces
                    for g, (xs, at, width, cat) in enumerate(groups(half)):
                        m = n * G + g
                        dve.wait_ge(silu_done, m + 2)
                        dve.wait_ge(u_done, m + 1)
                        dve.wait_ge(hidden_ready, m + 1)
                        to = prod if cT is not None else hid[g]
                        last = nc.vector.tensor_tensor(to[:, 0:width], gate[g % 2][:, 0:width], pu[:, 0:width], ALU.mult)
                        last.then_inc(prod_done, 1)
                        if cT is not None:
                            dve.wait_ge(prod_done, m + 2)
                            dve.wait_ge(c_done, m + 1)
                            nc.vector.tensor_tensor(hid[g][:, 0:width], prod[:, 0:width], pc[:, 0:width],
                                                    ALU.mult).then_inc(hid_done, 1)

                nc.vector.memset(zero[:, :], 0.0).then_inc(zeroed, 1)
                dve.sem_inc(prod_done, 1)
                if cT is not None:
                    dve.sem_inc(hid_done, 1)
                for half in range(2):
                    with dve.Fori(0, n_pieces // 2) as i:
                        for buf in range(2):
                            piece(half, 2 * i + buf)
                    if odd:
                        piece(half, n_pieces - 1)
                    dve.wait_ge(out_done, half + 1)
                    for i in range(TH // 2):
                        t = half * TH + 2 * i
                        nc.vector.tensor_tensor(const["x"][:, t:t + 2, :], const["x"][:, t:t + 2, :],
                                                pout[i][:, :, :], ALU.add).then_inc(added, 1)


HS = 16
DH = D // HS
HC = P // DH
SC = P + SEQ
AHEAD = 4
SLOTS = 2 * AHEAD


def attention_small(nc, name, const, xT, w, scale):
    with ExitStack() as ctx:
        sp = Space(nc, ctx, name)
        wts = {n: sp.sb(n, [P, KD, D]) for n in ("wq", "wk", "wv", "wo")}
        bq = sp.sb("bq", [P, KD])
        bk = sp.sb("bk", [P, KD])
        bv = sp.sb("bv", [1, D])
        bo = sp.sb("bo", [1, D])
        heads = sp.sb("heads", [P, HC])
        bkh = sp.sb("bkh", [P, HS])
        xb = sp.sb("xb", [P, KD, SEQ])
        qT = sp.sb("qT", [P, KD, SEQ])
        kT = sp.sb("kT", [P, HS, SEQ])
        v = sp.sb("v", [P, QT, D])
        s = sp.sb("s", [P, SLOTS, SC])
        nmax = sp.sb("nmax", [P, SLOTS, QT])
        rsum = sp.sb("rsum", [P, QT, HS])
        rinv = sp.sb("rinv", [P, QT, HS])
        pT = [sp.sb(f"pT{i}", [P, SC]) for i in range(2)]
        o = sp.sb("o", [P, QT, D])
        oT = sp.sb("oT", [P, QT, KD, P])
        ring = [sp.ps(f"ring{i}", [P, 512]) for i in range(4)]
        pv = sp.ps("pv", [P, QT, D])
        ppT = [sp.ps(f"ppT{i}", [P, 512]) for i in range(2)]
        pend = sp.ps("pend", [P, 512])
        w_in = sp.sem("w_in")
        bkh_ready = sp.sem("bkh_ready")
        xb_ready = sp.sem("xb_ready")
        q_done = sp.sem("q_done")
        k_done = sp.sem("k_done")
        v_done = sp.sem("v_done")
        q_ready = sp.sem("q_ready")
        k0_ready = sp.sem("k0_ready")
        k1_ready = sp.sem("k1_ready")
        v_ready = sp.sem("v_ready")
        s_done = sp.sem("s_done")
        s_read = sp.sem("s_read")
        max_ready = sp.sem("max_ready")
        exp_ready = sp.sem("exp_ready")
        turned = sp.sem("turned")
        even_copied = sp.sem("even_copied")
        odd_copied = sp.sem("odd_copied")
        pv_done = sp.sem("pv_done")
        inv_ready = sp.sem("inv_ready")
        o_ready = sp.sem("o_ready")
        oT_done = sp.sem("oT_done")
        oT_ready = sp.sem("oT_ready")
        out_done = sp.sem("out_done")
        added = sp.sem("added")
        ident, ones, cmask = const["ident"], const["ones"], const["cmask"]
        blocks = [(0, 0, 0), (1, 0, P), (1, 1, 2 * P)]
        spans = ((0, P), (P, SC))

        def batches(eng, run):
            with eng.Fori(0, NB - 1) as b:
                run(b, True)
            run(NB - 1, False)

        with nc.Block() as block:
            @block.sync
            def _(sync):
                for n in ("wq", "wk", "wv", "wo"):
                    sync.dma_start(wts[n][:, :, :], w[n]).then_inc(w_in, 16)
                for to, n in ((bq, "bq"), (bk, "bk"), (bv, "bv"), (bo, "bo"), (heads, "heads")):
                    sync.dma_start(to[:, :], w[n]).then_inc(w_in, 16)

            @block.gpsimd
            def _(pool):
                nc.gpsimd.tensor_copy(xb[:, :, :], xT[:, :, 0:SEQ]).then_inc(xb_ready, 1)
                with pool.Fori(1, NB) as b:
                    pool.wait_ge(v_done, b)
                    nc.gpsimd.tensor_copy(xb[:, :, :], xT[:, :, bass.ds(b * SEQ, SEQ)]).then_inc(xb_ready, 1)

            @block.tensor
            def _(pe):
                def project(b):
                    pe.wait_ge(xb_ready, b + 1)
                    for n, bank, done in (("wk", 1, k_done), ("wq", 0, q_done)):
                        for c in range(KD):
                            to = ring[bank + c] if n == "wk" else ring[bank]
                            at = 0 if n == "wk" else c * SEQ
                            for k in range(KD):
                                last = nc.tensor.matmul(to[:, at:at + SEQ], wts[n][:, k, c * P:(c + 1) * P], xb[:, k, :],
                                                        start=(k == 0), stop=(k == KD - 1))
                        last.then_inc(done, 1)
                    for t in range(QT):
                        for k in range(KD):
                            nc.tensor.matmul(ring[3][:, t * D:(t + 1) * D], xb[:, k, t * P:(t + 1) * P],
                                             wts["wv"][:, k, :], start=(k == 0), stop=False)
                        last = nc.tensor.matmul(ring[3][:, t * D:(t + 1) * D], ones[0:1, :], bv[:, :],
                                                start=False, stop=True)
                    last.then_inc(v_done, 1)

                def scores(b, h):
                    if h >= 4:
                        pe.wait_ge(s_read, b * HS + (h - 3))
                    c = h // HC
                    nc.tensor.matmul(ring[h % 4][:, 0:P], qT[:, c, 0:P], kT[:, h, 0:P], start=True, stop=True)
                    nc.tensor.matmul(ring[h % 4][:, P:SC], qT[:, c, P:SEQ], kT[:, h, :],
                                     start=True, stop=True).then_inc(s_done, 1)

                def turn(b, h):
                    pe.wait_ge(exp_ready, b * HS + (h + 1))
                    pe.wait_ge(odd_copied if h % 2 else even_copied, b * (HS // 2) + (h // 2 + 1))
                    for i in range(3):
                        last = nc.tensor.transpose(ppT[h % 2][:, i * P:(i + 1) * P],
                                                   s[:, h % SLOTS, i * P:(i + 1) * P], ident[:, :])
                    last.then_inc(turned, 1)

                def values(b, h):
                    pe.wait_ge(odd_copied if h % 2 else even_copied, b * (HS // 2) + (h // 2 + 2))
                    if h == 0:
                        pe.wait_ge(o_ready, b + 1)
                    for qt, kt, at in blocks:
                        last = nc.tensor.matmul(pv[:, qt, h * DH:(h + 1) * DH], pT[h % 2][:, at:at + P],
                                                v[:, kt, h * DH:(h + 1) * DH], start=(kt == 0), stop=(kt == qt))
                    if h == HS - 1:
                        last.then_inc(pv_done, 1)

                def run(b, more):
                    pe.wait_ge(q_ready, b + 1)
                    pe.wait_ge(k0_ready, b + 1)
                    pe.wait_ge(k1_ready, b + 1)
                    pe.wait_ge(v_ready, b + 1)
                    for h in range(AHEAD):
                        scores(b, h)
                    for h in range(HS):
                        if h + AHEAD < HS:
                            scores(b, h + AHEAD)
                        turn(b, h)
                        if h:
                            values(b, h - 1)
                    values(b, HS - 1)
                    if more:
                        pe.wait_ge(s_read, (b + 1) * HS)
                        project(b + 1)
                    pe.wait_ge(o_ready, b + 2)
                    pe.wait_ge(added, b + 1)
                    for t in range(QT):
                        for k in range(KD):
                            at = (t * KD + k) * P
                            last = nc.tensor.transpose(pend[:, at:at + P], o[:, t, k * P:(k + 1) * P], ident[:, :])
                    last.then_inc(oT_done, 1)
                    pe.wait_ge(oT_ready, b + 1)
                    for t in range(QT):
                        for k in range(KD):
                            nc.tensor.matmul(pend[:, t * D:(t + 1) * D], oT[:, t, k, :], wts["wo"][:, k, :],
                                             start=(k == 0), stop=False)
                        last = nc.tensor.matmul(pend[:, t * D:(t + 1) * D], ones[0:1, :], bo[:, :],
                                                start=False, stop=True)
                    last.then_inc(out_done, 1)

                pe.wait_ge(w_in, 16 * 9)
                project(0)
                batches(pe, run)

            @block.scalar
            def _(act):
                def load_qk(b):
                    act.wait_ge(k_done, b + 1)
                    for h in range(HC):
                        last = nc.scalar.activation(kT[:, h, :], ring[1][:, 0:SEQ], ACT.Identity,
                                                    bias=bkh[:, h:h + 1], scale=heads[:, h:h + 1])
                    last.then_inc(k0_ready, 1)
                    act.wait_ge(q_done, b + 1)
                    for c in range(KD):
                        last = nc.scalar.activation(qT[:, c, :], ring[0][:, c * SEQ:(c + 1) * SEQ],
                                                    ACT.Identity, bias=bq[:, c:c + 1])
                    last.then_inc(q_ready, 1)

                def exps(b, h):
                    act.wait_ge(max_ready, b * HS + (h + 1))
                    for t, (lo, hi) in enumerate(spans):
                        last = nc.scalar.activation(s[:, h % SLOTS, lo:hi], s[:, h % SLOTS, lo:hi], ACT.Exp,
                                                    bias=nmax[:, h % SLOTS, t:t + 1], accum_out=rsum[:, t, h:h + 1])
                    last.then_inc(exp_ready, 1)

                def run(b, more):
                    for h in range(AHEAD):
                        exps(b, h)
                    for h in range(HS):
                        if h + AHEAD < HS:
                            exps(b, h + AHEAD)
                        if h % 2 == 0:
                            act.wait_ge(turned, b * HS + (h + 1 + SLOTS))
                            nc.scalar.activation(pT[0][:, :], ppT[0][:, 0:SC], ACT.Copy).then_inc(even_copied, 1)
                    if more:
                        load_qk(b + 1)
                    act.wait_ge(oT_done, b + 1)
                    nc.scalar.activation(oT[:, :, :, :], pend[:, :].rearrange("p (t k c) -> p t k c", t=QT, k=KD),
                                         ACT.Copy).then_inc(oT_ready, 1)

                act.sem_inc(even_copied, 1)
                act.wait_ge(bkh_ready, KD)
                load_qk(0)
                batches(act, run)

            @block.vector
            def _(dve):
                def load_kv(b):
                    dve.wait_ge(k_done, b + 1)
                    for h in range(HC, HS):
                        last = nc.vector.tensor_scalar(kT[:, h, :], ring[2][:, 0:SEQ], heads[:, h - HC:h - HC + 1],
                                                       bkh[:, h:h + 1], ALU.mult, ALU.add)
                    last.then_inc(k1_ready, 1)
                    dve.wait_ge(v_done, b + 1)
                    nc.vector.tensor_copy(v[:, :, :], ring[3][:, :].rearrange("p (t d) -> p t d", t=QT)
                                          ).then_inc(v_ready, 1)

                def maxima(b, h):
                    dve.wait_ge(turned, b * HS + (h + 1))
                    dve.wait_ge(s_done, b * HS + (h + 1))
                    nc.vector.scalar_tensor_tensor(out=s[:, h % SLOTS, :], in0=ring[h % 4][:, 0:SC], scalar=scale,
                                                   in1=cmask[:, :], op0=ALU.mult, op1=ALU.add).then_inc(s_read, 1)
                    dve.wait_ge(s_read, b * HS + (h + 1))
                    for t, (lo, hi) in enumerate(spans):
                        last = nc.vector.tensor_reduce(nmax[:, h % SLOTS, t:t + 1], s[:, h % SLOTS, lo:hi], AX_X,
                                                       ALU.max, negate=True)
                    last.then_inc(max_ready, 1)

                def run(b, more):
                    for h in range(AHEAD):
                        maxima(b, h)
                    for h in range(HS):
                        if h + AHEAD < HS:
                            maxima(b, h + AHEAD)
                        if h % 2:
                            dve.wait_ge(turned, b * HS + (h + 1 + SLOTS))
                            nc.vector.tensor_copy(pT[1][:, :], ppT[1][:, 0:SC]).then_inc(odd_copied, 1)
                    dve.wait_ge(exp_ready, (b + 1) * HS)
                    nc.vector.reciprocal(rinv[:, :, :], rsum[:, :, :]).then_inc(inv_ready, 1)
                    dve.wait_ge(inv_ready, b + 1)
                    dve.wait_ge(pv_done, b + 1)
                    nc.vector.tensor_tensor(o[:, :, :].rearrange("p t (h d) -> p (t h) d", h=HS),
                                            pv[:, :, :].rearrange("p t (h d) -> p (t h) d", h=HS),
                                            rinv[:, :, :].rearrange("p t h -> p (t h)").unsqueeze(2)
                                            .broadcast_to([P, QT * HS, DH]), ALU.mult).then_inc(o_ready, 1)
                    if more:
                        load_kv(b + 1)
                    dve.wait_ge(out_done, b + 1)
                    nc.vector.tensor_tensor(const["x"][:, bass.ds(2 * b, QT), :], const["x"][:, bass.ds(2 * b, QT), :],
                                            pend[:, :].rearrange("p (t d) -> p t d", t=QT), ALU.add).then_inc(added, 1)

                dve.sem_inc(odd_copied, 1)
                dve.sem_inc(o_ready, 1)
                dve.sem_inc(added, 1)
                dve.sem_inc(turned, SLOTS)
                dve.wait_ge(w_in, 16 * 9)
                for c in range(KD):
                    nc.vector.tensor_scalar(bkh[:, c * HC:(c + 1) * HC], heads[:, :], bk[:, c:c + 1], None,
                                            ALU.mult).then_inc(bkh_ready, 1)
                dve.wait_ge(bkh_ready, KD)
                load_kv(0)
                batches(dve, run)


HL = 2
EL = D // HL


def linear_attention(nc, name, const, xT, w, o):
    with ExitStack() as ctx:
        sp = Space(nc, ctx, name)
        wts = {n: sp.sb(n, [P, KD, D]) for n in ("wq", "wk", "wv")}
        cm = sp.sb("cm", [P, SC])
        xb = sp.sb("xb", [P, KD, SEQ])
        v = sp.sb("v", [P, QT, D])
        q = sp.sb("q", [P, HL, SEQ])
        k = sp.sb("k", [P, HL, SEQ])
        f = sp.sb("f", [P, HL, SEQ])
        a = sp.sb("a", [P, HL, SEQ])
        up = sp.sb("up", [P, HL, SEQ])
        down = sp.sb("down", [P, HL, SEQ])
        nmid = sp.sb("nmid", [P, HL, QT])
        edge = sp.sb("edge", [P, HL, 2])
        qx = sp.sb("qx", [P, HL, P])
        kx = sp.sb("kx", [P, HL, P])
        sT = sp.sb("sT", [P, HL, SC])
        pq = sp.ps("pq", [P, HL, SEQ])
        pk = sp.ps("pk", [P, HL, SEQ])
        pv = sp.ps("pv", [P, QT, D])
        psT = [sp.ps(f"psT{h}", [P, 512]) for h in range(HL)]
        po = sp.ps("po", [P, QT, D])
        w_in = sp.sem("w_in")
        xb_ready = sp.sem("xb_ready")
        q_done = sp.sem("q_done")
        k_done = sp.sem("k_done")
        v_done = sp.sem("v_done")
        v_ready = sp.sem("v_ready")
        act_done = sp.sem("act_done")
        chain = sp.sem("chain")
        dve_done = sp.sem("dve_done")
        scores_done = sp.sem("scores_done")
        scores_ready = sp.sem("scores_ready")
        o_done = sp.sem("o_done")
        o_ready = sp.sem("o_ready")
        NCHAIN = 17
        ones = const["ones"]
        tiles = [(h, t) for h in range(HL) for t in range(QT)]

        with nc.Block() as block:
            @block.sync
            def _(sync):
                for n in ("wq", "wk", "wv"):
                    sync.dma_start(wts[n][:, :, :], w[n]).then_inc(w_in, 16)
                sync.dma_start(cm[:, :], const["cmask01T_dram"]).then_inc(w_in, 16)

            @block.gpsimd
            def _(pool):
                with pool.Fori(0, NB) as b:
                    pool.wait_ge(v_done, b + 1)
                    nc.gpsimd.tensor_copy(xb[:, :, :], xT[:, :, bass.ds(b * SEQ, SEQ)]).then_inc(xb_ready, 1)

            @block.tensor
            def _(pe):
                pe.sem_inc(v_done, 1)
                pe.wait_ge(w_in, 16 * 4)
                with pe.Fori(0, NB) as b:
                    pe.wait_ge(xb_ready, b + 1)
                    pe.wait_ge(scores_ready, 2 * b + 1)
                    for to, n, done in ((pk, "wk", k_done), (pq, "wq", q_done)):
                        for h in range(HL):
                            for c in range(KD):
                                last = nc.tensor.matmul(to[:, h, :], wts[n][:, c, h * EL:(h + 1) * EL], xb[:, c, :],
                                                        start=(c == 0), stop=(c == KD - 1))
                        last.then_inc(done, 1)
                    for t in range(QT):
                        for c in range(KD):
                            last = nc.tensor.matmul(pv[:, t, :], xb[:, c, t * P:(t + 1) * P], wts["wv"][:, c, :],
                                                    start=(c == 0), stop=(c == KD - 1))
                    last.then_inc(v_done, 1)
                    pe.wait_ge(dve_done, b + 1)
                    for h in range(HL):
                        nc.tensor.matmul(psT[h][:, 0:P], k[:, h, 0:P], q[:, h, 0:P], start=True, stop=True)
                        nc.tensor.matmul(psT[h][:, P:2 * P], kx[:, h, :], qx[:, h, :], start=True, stop=True)
                        nc.tensor.matmul(psT[h][:, 2 * P:SC], k[:, h, P:SEQ], q[:, h, P:SEQ],
                                         start=True, stop=True).then_inc(scores_done, 1)
                    pe.wait_ge(v_ready, b + 1)
                    pe.wait_ge(o_ready, b + 1)
                    for h in range(HL):
                        pe.wait_ge(scores_ready, 2 * b + (h + 2))
                        for qt, kt, at in ((0, 0, 0), (1, 0, P), (1, 1, 2 * P)):
                            last = nc.tensor.matmul(po[:, qt, h * EL:(h + 1) * EL], sT[:, h, at:at + P],
                                                    v[:, kt, h * EL:(h + 1) * EL], start=(kt == 0), stop=(kt == qt))
                    last.then_inc(o_done, 1)

            @block.scalar
            def _(act):
                act.sem_inc(o_ready, 1)
                with act.Fori(0, NB) as b:
                    act.wait_ge(k_done, b + 1)
                    nc.scalar.activation(f[:, :, :], pk[:, :, :], ACT.Exp, scale=-1.0).then_inc(act_done, 1)
                    act.wait_ge(q_done, b + 1)
                    nc.scalar.activation(q[:, :, :], pq[:, :, :], ACT.Exp, scale=-1.0).then_inc(act_done, 1)
                    act.wait_ge(v_done, b + 2)
                    nc.scalar.activation(v[:, :, :], pv[:, :, :], ACT.Copy).then_inc(v_ready, 1)
                    act.wait_ge(chain, b * NCHAIN + 2)
                    nc.scalar.activation(f[:, :, :], f[:, :, :], ACT.Exp, scale=-1.0).then_inc(act_done, 1)
                    act.wait_ge(chain, b * NCHAIN + 7)
                    nc.scalar.activation(f[:, :, :], k[:, :, :], ACT.Ln).then_inc(act_done, 1)
                    act.wait_ge(chain, b * NCHAIN + 13)
                    for h, t in tiles:
                        nc.scalar.activation(up[:, h, t * P:(t + 1) * P], a[:, h, t * P:(t + 1) * P], ACT.Exp,
                                             bias=nmid[:, h, t:t + 1])
                        last = nc.scalar.activation(down[:, h, t * P:(t + 1) * P], a[:, h, t * P:(t + 1) * P], ACT.Exp,
                                                    bias=a[:, h, t * P + P // 2 - 1:t * P + P // 2], scale=-1.0)
                    last.then_inc(act_done, 1)
                    for h in range(HL):
                        nc.scalar.activation(edge[:, h, 0:1], a[:, h, P + P // 2 - 1:P + P // 2], ACT.Exp)
                        last = nc.scalar.activation(edge[:, h, 1:2], a[:, h, P - 1:P], ACT.Exp, bias=nmid[:, h, 0:1])
                    last.then_inc(act_done, 1)
                    act.wait_ge(o_done, b + 1)
                    nc.scalar.activation(o[:, bass.ds(2 * b, QT), :], po[:, :, :], ACT.Copy).then_inc(o_ready, 1)

            @block.vector
            def _(dve):
                NA = 6
                dve.sem_inc(scores_ready, 1)
                with dve.Fori(0, NB) as b:
                    ch = Chain(dve, chain, b * NCHAIN)
                    dve.wait_ge(act_done, b * NA + 1)
                    ch.link(nc.vector.tensor_scalar(f[:, :, :], f[:, :, :], 1.0, None, ALU.add))
                    ch.link(nc.vector.reciprocal(f[:, :, :], f[:, :, :]))
                    dve.wait_ge(act_done, b * NA + 2)
                    ch.link(nc.vector.tensor_scalar(q[:, :, :], q[:, :, :], 1.0, None, ALU.add))
                    ch.link(nc.vector.reciprocal(q[:, :, :], q[:, :, :]))
                    ch.link(nc.vector.tensor_tensor(q[:, :, :], q[:, :, :], pq[:, :, :], ALU.mult))
                    dve.wait_ge(act_done, b * NA + 3)
                    ch.link(nc.vector.tensor_scalar(f[:, :, :], f[:, :, :], 1.0, None, ALU.add))
                    ch.link(nc.vector.reciprocal(k[:, :, :], f[:, :, :]))
                    dve.wait_ge(act_done, b * NA + 4)
                    for h, t in tiles:
                        sl = slice(t * P, (t + 1) * P)
                        ch.link(nc.vector.tensor_tensor_scan(a[:, h, sl], ones[:, :], f[:, h, sl], 0.0, ALU.mult, ALU.add))
                    ch.link(nc.vector.tensor_scalar(k[:, :, :], k[:, :, :], -1.0, 1.0, ALU.mult, ALU.add))
                    ch.link(nc.vector.tensor_scalar(nmid[:, :, :], a[:, :, :].rearrange("p h (t c) -> p h t c", t=QT)
                                                    [:, :, :, P // 2 - 1], -1.0, None, ALU.mult))
                    dve.wait_ge(act_done, b * NA + 5)
                    ch.link(nc.vector.tensor_tensor(q[:, :, :], q[:, :, :], up[:, :, :], ALU.mult))
                    ch.link(nc.vector.tensor_tensor(k[:, :, :], k[:, :, :], down[:, :, :], ALU.mult))
                    dve.wait_ge(act_done, b * NA + 6)
                    for h in range(HL):
                        nc.vector.tensor_scalar(qx[:, h, :], q[:, h, P:SEQ], edge[:, h, 0:1], None, ALU.mult)
                        last = nc.vector.tensor_scalar(kx[:, h, :], k[:, h, 0:P], edge[:, h, 1:2], None, ALU.mult)
                        if h == 0:
                            ch.link(last)
                    ch.link(last)
                    dve.sem_inc(dve_done, 1)
                    assert ch.count == NCHAIN, ch.count
                    for h in range(HL):
                        dve.wait_ge(scores_done, 2 * b + (h + 1))
                        nc.vector.tensor_tensor(sT[:, h, :], psT[h][:, 0:SC], cm[:, :], ALU.mult).then_inc(scores_ready, 1)


def project(nc, name, const, xT, w_dram):
    with ExitStack() as ctx:
        sp = Space(nc, ctx, name)
        w = sp.sb("w", [P, KD, D])
        po = [sp.ps(f"po{i}", [P, 2, D]) for i in range(4)]
        w_in = sp.sem("w_in")
        done = sp.sem("done")
        added = sp.sem("added")
        with nc.Block() as block:
            @block.sync
            def _(sync):
                sync.dma_start(w[:, :, :], w_dram).then_inc(w_in, 16)

            @block.tensor
            def _(pe):
                pe.wait_ge(w_in, 16)
                for i in range(NT // 2):
                    if i >= 4:
                        pe.wait_ge(added, i - 3)
                    for t in (2 * i, 2 * i + 1):
                        for k in range(KD):
                            last = nc.tensor.matmul(po[i % 4][:, t % 2, :], xT[:, k, t * P:(t + 1) * P], w[:, k, :],
                                                    start=(k == 0), stop=(k == KD - 1))
                    last.then_inc(done, 1)

            @block.vector
            def _(dve):
                for i in range(NT // 2):
                    dve.wait_ge(done, i + 1)
                    nc.vector.tensor_tensor(const["x"][:, 2 * i:2 * i + 2, :], const["x"][:, 2 * i:2 * i + 2, :],
                                            po[i % 4][:, :, :], ALU.add).then_inc(added, 1)


HQ = 16
HKV = 4
GQ = HQ // HKV
HB = GQ + 1
EH = 128
NBLK = 2 * HB * QT
NTT = NBLK // 4


def attention_mixed(nc, name, const, xT, w):
    scale = float(EH) ** -0.5
    with ExitStack() as ctx:
        sp = Space(nc, ctx, name)
        wq = sp.sb("wq", [P, KD, HKV, GQ * EH])
        wk = sp.sb("wk", [P, KD, HKV * EH])
        wv = sp.sb("wv", [P, KD, HKV * EH])
        wo = sp.sb("wo", [P, HQ, D])
        cos = sp.sb("cos", [P, QT, EH])
        sin = sp.sb("sin", [P, QT, EH])
        decay = sp.sb("decay", [P, QT, P])
        xb = sp.sb("xb", [P, KD, SEQ])
        qk = sp.sb("qk", [P, QT, HB, EH])
        e = sp.sb("e", [P, QT, HB, EH])
        rcos = sp.sb("rcos", [P, QT, HB, EH])
        rsin = sp.sb("rsin", [P, QT, HB, EH])
        src = sp.sb("src", [P, 2, QT, HB, EH])
        tt = sp.sb("tt", [P, 2, HB, QT, P])
        keys = sp.sb("keys", [P, QT, HKV, EH])
        gate = sp.sb("gate", [P, QT, HKV, EH])
        up = sp.sb("up", [P, QT, HKV, EH])
        down = sp.sb("down", [P, QT, HKV, EH])
        v = sp.sb("v", [P, QT, EH])
        top = sp.sb("top", [P, QT * HB])
        total = sp.sb("total", [P, QT * HB])
        inv_next = sp.sb("inv_next", [P, QT * HB])
        inv = sp.sb("inv", [P, QT * HB])
        s = [sp.sb(f"s{i}", [P, SC]) for i in range(2)]
        g = [sp.sb(f"g{i}", [P, SC]) for i in range(2)]
        nmax = [sp.sb(f"nmax{i}", [P, QT]) for i in range(2)]
        rsum = [sp.sb(f"rsum{i}", [P, QT]) for i in range(2)]
        rinv = [sp.sb(f"rinv{i}", [P, QT]) for i in range(2)]
        pT = [sp.sb(f"pT{i}", [P, SC]) for i in range(2)]
        oT = [sp.sb(f"oT{i}", [P, SEQ]) for i in range(2)]
        pq = [sp.ps(f"pq{i}", [P, 512]) for i in range(2)]
        pv = sp.ps("pv", [P, QT, EH])
        po = sp.ps("po", [P, SEQ])
        pS = sp.ps("pS", [P, 512])
        pG = sp.ps("pG", [P, 512])
        ppT = sp.ps("ppT", [P, 512])
        pout = sp.ps("pout", [P, QT, D])
        turn_banks = (pq[0], pq[1], pS, pG)
        w_in = sp.sem("w_in")
        xb_ready = sp.sem("xb_ready")
        k_done = sp.sem("k_done")
        v_done = sp.sem("v_done")
        q_done = sp.sem("q_done")
        gate_exp = sp.sem("gate_exp")
        gate_ready = sp.sem("gate_ready")
        decay_done = sp.sem("decay_done")
        decay_ready = sp.sem("decay_ready")
        qk_ready = sp.sem("qk_ready")
        rotated = sp.sem("rotated")
        pool_chain = sp.sem("pool_chain")
        top_ready = sp.sem("top_ready")
        sub_ready = sp.sem("sub_ready")
        e_ready = sp.sem("e_ready")
        total_ready = sp.sem("total_ready")
        inv_ready = sp.sem("inv_ready")
        prepared = sp.sem("prepared")
        tt_done = sp.sem("tt_done")
        tt_even_read = sp.sem("tt_even_read")
        tt_odd_read = sp.sem("tt_odd_read")
        v_ready = sp.sem("v_ready")
        s_done = sp.sem("s_done")
        s_read = sp.sem("s_read")
        g_done = sp.sem("g_done")
        g_read = sp.sem("g_read")
        max_ready = sp.sem("max_ready")
        exp_ready = sp.sem("exp_ready")
        rinv_ready = sp.sem("rinv_ready")
        p_ready = sp.sem("p_ready")
        pT_done = sp.sem("pT_done")
        pT_read = sp.sem("pT_read")
        oT_done = sp.sem("oT_done")
        oT_read = sp.sem("oT_read")
        out_done = sp.sem("out_done")
        added = sp.sem("added")
        inv_moved = sp.sem("inv_moved")
        ident = const["ident"]
        flat = tt[:, :, :, :, :].rearrange("p a h t c -> p (a h t) c")
        spans = ((0, P), (P, SC))

        def steps(eng, run):
            with eng.Fori(0, NB - 1) as b:
                for gr in range(HKV):
                    i = b * HKV + gr
                    nxt = (i + 1, b, gr + 1) if gr + 1 < HKV else (b * HKV + HKV, b + 1, 0)
                    run(i, b, gr, nxt)
            for gr in range(HKV):
                i = (NB - 1) * HKV + gr
                run(i, NB - 1, gr, (i + 1, NB - 1, gr + 1) if gr + 1 < HKV else None)

        with nc.Block() as block:
            @block.sync
            def _(sync):
                sync.dma_start(wk[:, :, :], w["wk"]).then_inc(w_in, 16)
                sync.dma_start(wv[:, :, :], w["wv"]).then_inc(w_in, 16)
                sync.dma_start(wq[:, :, :, :], w["wq"]).then_inc(w_in, 16)
                for to, n in ((cos, "cos"), (sin, "sin"), (decay, "decay"), (wo, "wo")):
                    sync.dma_start(to[:, :, :], w[n]).then_inc(w_in, 16)

            @block.gpsimd
            def _(pool):
                def load(b):
                    nc.gpsimd.tensor_copy(xb[:, :, :], xT[:, :, bass.ds(b * SEQ, SEQ)]).then_inc(xb_ready, 1)

                def rotate(n):
                    pool.wait_ge(qk_ready, n + 1)
                    wide = [P, QT, HB, EH]
                    half = [P, QT, HB, EH // 2]
                    nc.gpsimd.tensor_tensor(rcos[:, :, :, :], qk[:, :, :, :],
                                            cos[:, :, :].unsqueeze(2).broadcast_to(wide), ALU.mult).then_inc(pool_chain, 1)
                    nc.gpsimd.tensor_tensor(rsin[:, :, :, 0:EH // 2], qk[:, :, :, EH // 2:EH],
                                            sin[:, :, 0:EH // 2].unsqueeze(2).broadcast_to(half),
                                            ALU.mult).then_inc(pool_chain, 1)
                    nc.gpsimd.tensor_tensor(rsin[:, :, :, EH // 2:EH], qk[:, :, :, 0:EH // 2],
                                            sin[:, :, EH // 2:EH].unsqueeze(2).broadcast_to(half),
                                            ALU.mult).then_inc(pool_chain, 1)
                    pool.wait_ge(pool_chain, 3 * n + 3)
                    nc.gpsimd.tensor_tensor(src[:, 0, :, :, :], rcos[:, :, :, :], rsin[:, :, :, :],
                                            ALU.add).then_inc(rotated, 1)

                pool.wait_ge(w_in, 16 * 7)
                nc.gpsimd.tensor_copy(xb[:, :, :], xT[:, :, 0:SEQ]).then_inc(xb_ready, 1)
                rotate(0)

                def run(i, b, gr, nxt):
                    if nxt:
                        if gr == HKV - 1:
                            pool.wait_ge(v_done, i + 1)
                            load(nxt[1])
                        rotate(nxt[0])

                steps(pool, run)

            @block.tensor
            def _(pe):
                def project_keys(n, b):
                    pe.wait_ge(xb_ready, b + 1)
                    pe.wait_ge(tt_even_read, n * 3 + 1)
                    pe.wait_ge(tt_odd_read, n * 2 + 1)
                    for t in range(QT):
                        for k in range(KD):
                            last = nc.tensor.matmul(pq[t][:, :], xb[:, k, t * P:(t + 1) * P], wk[:, k, :],
                                                    start=(k == 0), stop=(k == KD - 1))
                    last.then_inc(k_done, 1)

                def decays(b):
                    pe.wait_ge(gate_ready, b + 1)
                    for t in range(QT):
                        last = nc.tensor.matmul(pq[t][:, :], decay[:, t, :], gate[:, t, :, :], start=True, stop=True)
                    last.then_inc(decay_done, 1)

                def project(n, b, gr):
                    pe.wait_ge(tt_even_read, n * 3 + 1)
                    pe.wait_ge(tt_odd_read, n * 2 + 1)
                    if gr == 0:
                        pe.wait_ge(decay_ready, b + 1)
                    project_tile(gr, 0)

                def project_tile(gr, t):
                    for k in range(KD):
                        last = nc.tensor.matmul(pq[t][:, :], xb[:, k, t * P:(t + 1) * P], wq[:, k, gr, :],
                                                start=(k == 0), stop=(k == KD - 1))
                    last.then_inc(q_done, 1)

                def project_rest(n, gr):
                    project_tile(gr, 1)
                    pe.wait_ge(v_ready, n + 1)
                    for t in range(QT):
                        for k in range(KD):
                            last = nc.tensor.matmul(pv[:, t, :], xb[:, k, t * P:(t + 1) * P], wv[:, k, gr * EH:(gr + 1) * EH],
                                                    start=(k == 0), stop=(k == KD - 1))
                    last.then_inc(v_done, 1)

                def turn(n):
                    pe.wait_ge(prepared, n + 1)
                    for m in range(NTT):
                        if m == 4:
                            pe.wait_ge(tt_even_read, n * 3 + 2)
                        for c in range(4):
                            blk = 4 * m + c
                            kind, h, t = blk // (HB * QT), blk // QT % HB, blk % QT
                            last = nc.tensor.transpose(turn_banks[m % 4][:, c * P:(c + 1) * P], src[:, kind, t, h, :],
                                                       ident[:, :])
                        last.then_inc(tt_done, 1)

                def scores(i, h):
                    for kind, bank, read, done in ((0, pS, s_read, s_done), (1, pG, g_read, g_done)):
                        pe.wait_ge(read, i * GQ + (h + 1))
                        nc.tensor.matmul(bank[:, 0:P], tt[:, kind, h, 0, :], tt[:, kind, GQ, 0, :], start=True, stop=True)
                        nc.tensor.matmul(bank[:, P:SC], tt[:, kind, h, 1, :], tt[:, kind, GQ, :, :],
                                         start=True, stop=True).then_inc(done, 1)

                def turn_p(i, h):
                    pe.wait_ge(p_ready, i * GQ + (h + 1))
                    pe.wait_ge(pT_read, i * GQ + (h + 1))
                    for c in range(3):
                        last = nc.tensor.transpose(ppT[:, c * P:(c + 1) * P], s[h % 2][:, c * P:(c + 1) * P], ident[:, :])
                    last.then_inc(pT_done, 1)

                def values(i, h):
                    pe.wait_ge(pT_read, i * GQ + (h + 2))
                    pe.wait_ge(oT_read, i * GQ + (h + 1))
                    nc.tensor.matmul(po[:, :], v[:, 0, :], pT[h % 2][:, 0:SEQ], start=True, stop=False,
                                     skip_group_check=True)
                    nc.tensor.matmul(po[:, P:SEQ], v[:, 1, :], pT[h % 2][:, SEQ:SC], start=False, stop=True,
                                     skip_group_check=True).then_inc(oT_done, 1)

                def output(i, gr, h):
                    pe.wait_ge(oT_read, i * GQ + (h + 2))
                    if h == 0:
                        pe.wait_ge(added, i + 1)
                    for t in range(QT):
                        last = nc.tensor.matmul(pout[:, t, :], oT[h % 2][:, t * P:(t + 1) * P], wo[:, gr * GQ + h, :],
                                                start=(h == 0 and t == 0), stop=(h == GQ - 1), skip_group_check=True)
                    if h == GQ - 1:
                        last.then_inc(out_done, 1)

                def run(i, b, gr, nxt):
                    new_batch = nxt and nxt[2] == 0
                    if new_batch:
                        project_keys(nxt[0], nxt[1])
                    pe.wait_ge(tt_even_read, i * 3 + 4)
                    pe.wait_ge(tt_odd_read, i * 2 + 3)
                    pe.wait_ge(v_ready, i + 2)
                    scores(i, 0)
                    if nxt and not new_batch:
                        project(*nxt)
                    scores(i, 1)
                    if nxt and not new_batch:
                        project_rest(nxt[0], nxt[2])
                    turn_p(i, 0)
                    if new_batch:
                        decays(nxt[1])
                    scores(i, 2)
                    values(i, 0)
                    turn_p(i, 1)
                    output(i, gr, 0)
                    values(i, 1)
                    if new_batch:
                        project(*nxt)
                        project_rest(nxt[0], nxt[2])
                    scores(i, 3)
                    turn_p(i, 2)
                    output(i, gr, 1)
                    values(i, 2)
                    turn_p(i, 3)
                    output(i, gr, 2)
                    values(i, 3)
                    output(i, gr, 3)
                    if nxt:
                        turn(nxt[0])

                pe.wait_ge(w_in, 16 * 7)
                project_keys(0, 0)
                decays(0)
                project(0, 0, 0)
                project_rest(0, 0)
                turn(0)
                steps(pe, run)

            @block.scalar
            def _(act):
                act.sem_inc(tt_even_read, 1)
                act.sem_inc(v_ready, 1)
                act.sem_inc(pT_read, 1)
                act.sem_inc(oT_read, 1)

                def gates(b):
                    act.wait_ge(k_done, b + 1)
                    for t in range(QT):
                        nc.scalar.activation(gate[:, t, :, :], pq[t][:, :].rearrange("p (h e) -> p h e", h=HKV), ACT.Exp,
                                             scale=-1.0)
                        last = nc.scalar.activation(keys[:, t, :, :], pq[t][:, :].rearrange("p (h e) -> p h e", h=HKV),
                                                    ACT.Copy)
                    last.then_inc(gate_exp, 1)
                    act.wait_ge(gate_exp, b + 1)
                    nc.scalar.activation(gate[:, :, :, :], gate[:, :, :, :], ACT.Ln, bias=1.0).then_inc(gate_ready, 1)

                def decay_exps(b):
                    act.wait_ge(decay_done, b + 1)
                    for t in range(QT):
                        pd = pq[t][:, :].rearrange("p (h e) -> p h e", h=HKV)
                        nc.scalar.activation(up[:, t, :, :], pd, ACT.Exp)
                        last = nc.scalar.activation(down[:, t, :, :], pd, ACT.Exp, scale=-1.0)
                    last.then_inc(decay_ready, 1)

                def gather_qk(n, gr):
                    nc.scalar.activation(qk[:, :, GQ, :], keys[:, :, gr, :], ACT.Copy)
                    for t in range(QT):
                        act.wait_ge(q_done, n * QT + (t + 1))
                        last = nc.scalar.activation(qk[:, t, 0:GQ, :], pq[t][:, :].rearrange("p (h e) -> p h e", h=GQ),
                                                    ACT.Copy)
                    last.then_inc(qk_ready, 1)

                def softmax_exps(n):
                    act.wait_ge(sub_ready, n + 1)
                    nc.scalar.activation(e[:, :, :, :], e[:, :, :, :], ACT.Exp).then_inc(e_ready, 1)

                def copies(n):
                    for m in range(0, NTT, 2):
                        act.wait_ge(tt_done, n * NTT + (m + 1))
                        nc.scalar.activation(flat[:, 4 * m:4 * m + 4, :],
                                             turn_banks[m % 4][:, :].rearrange("p (a c) -> p a c", a=4),
                                             ACT.Copy).then_inc(tt_even_read, 1)
                    act.wait_ge(v_done, n + 1)
                    nc.scalar.activation(v[:, :, :], pv[:, :, :], ACT.Copy).then_inc(v_ready, 1)

                def exps(i, h):
                    act.wait_ge(max_ready, i * GQ + (h + 1))
                    for t, (lo, hi) in enumerate(spans):
                        last = nc.scalar.activation(s[h % 2][:, lo:hi], s[h % 2][:, lo:hi], ACT.Exp,
                                                    bias=nmax[h % 2][:, t:t + 1], accum_out=rsum[h % 2][:, t:t + 1])
                    last.then_inc(exp_ready, 1)

                def outs(i, h):
                    act.wait_ge(pT_done, i * GQ + (h + 1))
                    nc.scalar.activation(pT[h % 2][:, :], ppT[:, 0:SC], ACT.Copy).then_inc(pT_read, 1)
                    act.wait_ge(oT_done, i * GQ + (h + 1))
                    nc.scalar.activation(oT[h % 2][:, :], po[:, :], ACT.Copy, scale=0.5).then_inc(oT_read, 1)

                def run(i, b, gr, nxt):
                    new_batch = nxt and nxt[2] == 0
                    exps(i, 0)
                    if new_batch:
                        gates(nxt[1])
                    exps(i, 1)
                    if nxt and not new_batch:
                        gather_qk(nxt[0], nxt[2])
                    outs(i, 0)
                    if new_batch:
                        decay_exps(nxt[1])
                    outs(i, 1)
                    if new_batch:
                        gather_qk(nxt[0], nxt[2])
                    exps(i, 2)
                    if nxt and not new_batch:
                        softmax_exps(nxt[0])
                    exps(i, 3)
                    outs(i, 2)
                    if new_batch:
                        softmax_exps(nxt[0])
                    outs(i, 3)
                    if nxt:
                        copies(nxt[0])

                gates(0)
                decay_exps(0)
                gather_qk(0, 0)
                softmax_exps(0)
                copies(0)
                steps(act, run)

            @block.vector
            def _(dve):
                dve.sem_inc(s_read, 1)
                dve.sem_inc(g_read, 1)
                dve.sem_inc(tt_odd_read, 1)
                dve.sem_inc(added, 1)
                nf = "p t h e -> p (t h) e"

                def shift(n):
                    dve.wait_ge(qk_ready, n + 1)
                    nc.vector.tensor_reduce(top[:, :], qk[:, :, :, :].rearrange(nf), AX_X, ALU.max).then_inc(top_ready, 1)
                    dve.wait_ge(top_ready, n + 1)
                    nc.vector.tensor_tensor(e[:, :, :, :].rearrange(nf), qk[:, :, :, :].rearrange(nf),
                                            top[:, :].unsqueeze(2).broadcast_to([P, QT * HB, EH]),
                                            ALU.subtract).then_inc(sub_ready, 1)

                def sums(n):
                    dve.wait_ge(e_ready, n + 1)
                    nc.vector.tensor_reduce(total[:, :], e[:, :, :, :].rearrange(nf), AX_X, ALU.add).then_inc(total_ready, 1)
                    dve.wait_ge(total_ready, n + 1)
                    nc.vector.reciprocal(inv_next[:, :], total[:, :]).then_inc(inv_ready, 1)

                def decay(n, b, gr):
                    dve.wait_ge(inv_ready, n + 1)
                    dve.wait_ge(decay_ready, b + 1)
                    for t in range(QT):
                        nc.vector.scalar_tensor_tensor(out=src[:, 1, t, GQ, :], in0=e[:, t, GQ, :],
                                                       scalar=inv_next[:, t * HB + GQ:t * HB + GQ + 1],
                                                       in1=down[:, t, gr, :], op0=ALU.mult, op1=ALU.mult)
                    nc.vector.tensor_tensor(src[:, 1, :, 0:GQ, :], e[:, :, 0:GQ, :],
                                            up[:, :, gr, :].unsqueeze(2).broadcast_to([P, QT, GQ, EH]), ALU.mult)
                    dve.wait_ge(rotated, n + 1)

                def maxima(i, h):
                    dve.wait_ge(s_done, i * GQ + (h + 1))
                    nc.vector.scalar_tensor_tensor(out=s[h % 2][:, :], in0=pS[:, 0:SC], scalar=scale,
                                                   in1=const["cmask"][:, :], op0=ALU.mult, op1=ALU.add).then_inc(s_read, 1)
                    dve.wait_ge(s_read, i * GQ + (h + 2))
                    for t, (lo, hi) in enumerate(spans):
                        last = nc.vector.tensor_reduce(nmax[h % 2][:, t:t + 1], s[h % 2][:, lo:hi], AX_X, ALU.max,
                                                       negate=True)
                    last.then_inc(max_ready, 1)
                    dve.wait_ge(g_done, i * GQ + (h + 1))
                    for t, (lo, hi) in enumerate(spans):
                        last = nc.vector.scalar_tensor_tensor(out=g[h % 2][:, lo:hi], in0=pG[:, lo:hi],
                                                              scalar=inv[:, t * HB + h:t * HB + h + 1],
                                                              in1=const["cmask01"][:, lo:hi], op0=ALU.mult, op1=ALU.mult)
                    last.then_inc(g_read, 1)

                def join(i, h):
                    dve.wait_ge(exp_ready, i * GQ + (h + 1))
                    nc.vector.reciprocal(rinv[h % 2][:, :], rsum[h % 2][:, :]).then_inc(rinv_ready, 1)
                    dve.wait_ge(rinv_ready, i * GQ + (h + 1))
                    dve.wait_ge(g_read, i * GQ + (h + 2))
                    for t, (lo, hi) in enumerate(spans):
                        last = nc.vector.scalar_tensor_tensor(out=s[h % 2][:, lo:hi], in0=s[h % 2][:, lo:hi],
                                                              scalar=rinv[h % 2][:, t:t + 1], in1=g[h % 2][:, lo:hi],
                                                              op0=ALU.mult, op1=ALU.add)
                    last.then_inc(p_ready, 1)

                def finish_prepare(n):
                    nc.vector.tensor_copy(inv[:, :], inv_next[:, :]).then_inc(prepared, 1)
                    for m in range(1, NTT, 2):
                        dve.wait_ge(tt_done, n * NTT + (m + 1))
                        nc.vector.tensor_copy(flat[:, 4 * m:4 * m + 4, :],
                                              turn_banks[m % 4][:, :].rearrange("p (a c) -> p a c", a=4)
                                              ).then_inc(tt_odd_read, 1)

                def run(i, b, gr, nxt):
                    new_batch = nxt and nxt[2] == 0
                    dve.wait_ge(prepared, i + 1)
                    maxima(i, 0)
                    maxima(i, 1)
                    join(i, 0)
                    join(i, 1)
                    dve.wait_ge(pT_done, i * GQ + 1)
                    maxima(i, 2)
                    if nxt:
                        shift(nxt[0])
                    join(i, 2)
                    dve.wait_ge(pT_done, i * GQ + 2)
                    maxima(i, 3)
                    if nxt:
                        sums(nxt[0])
                    join(i, 3)
                    if nxt:
                        decay(*nxt)
                        finish_prepare(nxt[0])
                    dve.wait_ge(out_done, i + 1)
                    nc.vector.tensor_tensor(const["x"][:, bass.ds(2 * b, QT), :], const["x"][:, bass.ds(2 * b, QT), :],
                                            pout[:, :, :], ALU.add).then_inc(added, 1)

                shift(0)
                sums(0)
                decay(0, 0, 0)
                finish_prepare(0)
                steps(dve, run)


def program(nc, a, out):
    with ExitStack() as ctx:
        sp = Space(nc, ctx, "all")
        const = {"x": sp.sb("x", [P, NT, D])}
        for c in CONSTS:
            const[c] = sp.sb(c, list(a[c].shape))
            const[c + "_dram"] = a[c]
        const["cmask01T_dram"] = a["cmask01T"]
        const["order_dram"] = a["order"]
        xn = sp.sb("xn", [P, NT, D])
        xT = sp.sb("xT", [P, KD, TOK])
        setup(nc, a["X"], const)
        if "0a" in STAGES or "0f" in STAGES:
            normalize(nc, "n0", const["x"], const, xn, xT, 1e-5, False)
        if "0a" in STAGES:
            attention_small(nc, "a0", const, xT, {**{k: a["L0_" + k] for k in SMALL}, "heads": a["heads"]}, 0.25)
        if "0f" in STAGES:
            with nc.sbuf_tensor("cT0", [17, TOK], F32) as cT:
                route(nc, "r0", const, xT, a["L0_Wg"], 16, 4, cT, groups=(4, 2), renorm=False)
                gated_ffn(nc, "f0", const, xT, a["L0_bank"], 25, cT=cT)
        if "1a" in STAGES or "1f" in STAGES:
            normalize(nc, "n1", const["x"], const, xn, xT, 1e-5, False)
        if "1a" in STAGES:
            attention_mixed(nc, "a1", const, xT, {k: a["L1_" + k] for k in ("wq", "wk", "wv", "wo", "cos", "sin", "decay")})
        if "1f" in STAGES:
            gated_ffn(nc, "f1", const, xT, a["L1_bank"], 8)
        if "2a" in STAGES or "2f" in STAGES:
            normalize(nc, "n2", const["x"], const, xn, xT, 1e-5, False)
        if "2a" in STAGES:
            with nc.sbuf_tensor("o2", [P, NT, D], F32) as o:
                linear_attention(nc, "a2", const, xT, {k: a["L2_" + k] for k in ("wq", "wk", "wv")}, o)
                normalize(nc, "n2o", o, const, o, xT, 1e-6, True, a["L2_attn_norm"])
            project(nc, "p2", const, xT, a["L2_wo"])
        if "2f" in STAGES:
            E = 32
            normalize(nc, "n2f", xn, const, xn, xT, 1e-6, True, a["L2_ffn_norm"], add_src=True)
            with (nc.sbuf_tensor("cT2", [E + 1, TOK + E], F32) as cT, nc.sbuf_tensor("cover2", [E, TOK], F32) as coverT,
                  nc.sbuf_tensor("xs2", [P, KD, E], F32) as xsT):
                route(nc, "r2", const, xT, a["L2_gate"], E, 4, cT, cap=2 * TOK * 4 // E,
                      extra=(xn, xsT, coverT, a["L2_ffn_norm"]))
                gated_ffn(nc, "f2", const, xT, a["L2_bank"], 33, cT=cT, extra=(xsT, coverT))
        if "3a" in STAGES or "3f" in STAGES:
            normalize(nc, "n3", const["x"], const, xn, xT, 1e-5, False)
        if "3a" in STAGES:
            attention_small(nc, "a3", const, xT, {**{k: a["L3_" + k] for k in SMALL}, "heads": a["heads"]}, 0.25)
        if "3f" in STAGES:
            with nc.sbuf_tensor("cT3", [65, TOK], F32) as cT:
                route(nc, "r3", const, xT, a["L3_router"], 64, 4, cT, bias_dram=a["L3_router_bias"], cap=32)
                gated_ffn(nc, "f3", const, xT, a["L3_bank"], 36, cT=cT)
        store(nc, out, const)


def host_layout(inp):
    f = {k: np.asarray(v) for k, v in inp.items()}
    a = {"X": f["L0_attn_X"]}

    def bank(w1, w3, w2, expert_of):
        rows = w1.shape[0]
        n = -(-rows // P)
        E = int(expert_of.max()) + 1
        b = np.zeros((n, P, KD * 2 * P + D + P), np.float32)
        for p in range(n):
            r = slice(p * P, min((p + 1) * P, rows))
            m = r.stop - r.start
            for k in range(KD):
                b[p, :, k * 2 * P:k * 2 * P + m] = w1[r, k * P:(k + 1) * P].T
                b[p, :, k * 2 * P + P:k * 2 * P + P + m] = w3[r, k * P:(k + 1) * P].T
            b[p, :m, KD * 2 * P:KD * 2 * P + D] = w2[r]
            b[p, :E, KD * 2 * P + D:][expert_of[r], np.arange(m)] = 1.0
        return b

    gu = f["L1_ffn_w_gate_up"]
    n = gu.shape[0] // 2
    a["L1_bank"] = bank(gu[:n], gu[n:], f["L1_ffn_w_down"].T, np.zeros(n, np.int64))

    def col(w):
        return w.reshape(KD, P).T

    def chan(w):
        return w.T.reshape(KD, P, -1).transpose(1, 0, 2)

    for l in ("L0_", "L3_"):
        g = l + "attn_"
        for n in "qk":
            a[l + "w" + n] = chan(f[g + "W" + n])
            a[l + "b" + n] = col(f[g + "b" + n])
        for n in "vo":
            a[l + "w" + n] = chan(f[g + "W" + n])
            a[l + "b" + n] = f[g + "b" + n].reshape(1, D)
    a["L0_Wg"] = chan(f["L0_ffn_Wg"])
    E, I = f["L0_ffn_W1"].shape[:2]
    sh = f["L0_ffn_Ws1"].shape[0]
    a["L0_bank"] = bank(np.concatenate([f["L0_ffn_W1"].reshape(E * I, D), f["L0_ffn_Ws1"]]),
                        np.concatenate([f["L0_ffn_W3"].reshape(E * I, D), f["L0_ffn_Ws3"]]),
                        np.concatenate([f["L0_ffn_W2"].transpose(0, 2, 1).reshape(E * I, D), f["L0_ffn_Ws2"].T]),
                        np.concatenate([np.repeat(np.arange(E), I), np.full(sh, E)]))
    def rows(w):
        return w.reshape(KD, P, -1).transpose(1, 0, 2)

    a["L1_wq"] = rows(f["L1_attn_Wq"]).reshape(P, KD, HKV, GQ * EH)
    a["L1_wk"] = rows(f["L1_attn_Wk"])
    a["L1_wv"] = rows(f["L1_attn_Wv"])
    a["L1_wo"] = f["L1_attn_Wo"].reshape(HQ, P, D).transpose(1, 0, 2)
    for n in "qkvo":
        a["L2_w" + n] = chan(f["L2_attn_W" + n])
    a["L2_attn_norm"] = col(f["L2_attn_norm_w"])
    a["L2_gate"] = chan(f["L2_ffn_gate_w"])
    a["L2_ffn_norm"] = col(f["L2_ffn_norm_w"])
    E, I = f["L2_ffn_w2"].shape[:2]
    w13 = f["L2_ffn_w13"].transpose(0, 2, 1)
    a["L2_bank"] = bank(np.concatenate([w13[:, :I].reshape(E * I, D), f["L2_ffn_shared_gate_w"].T]),
                        np.concatenate([w13[:, I:].reshape(E * I, D), f["L2_ffn_shared_up_w"].T]),
                        np.concatenate([f["L2_ffn_w2"].reshape(E * I, D), f["L2_ffn_shared_down_w"]]),
                        np.concatenate([np.repeat(np.arange(E), I), np.full(I, E)]))
    a["L3_router"] = chan(f["L3_ffn_router_w"])
    a["L3_router_bias"] = f["L3_ffn_router_bias"].reshape(1, -1)
    E, I = f["L3_ffn_gate_w"].shape[:2]
    S, SF = f["L3_ffn_sh_gate_w"].shape[:2]
    a["L3_bank"] = bank(np.concatenate([f["L3_ffn_gate_w"].reshape(E * I, D), f["L3_ffn_sh_gate_w"].reshape(S * SF, D)]),
                        np.concatenate([f["L3_ffn_up_w"].reshape(E * I, D), f["L3_ffn_sh_up_w"].reshape(S * SF, D)]),
                        np.concatenate([f["L3_ffn_down_w"].transpose(0, 2, 1).reshape(E * I, D),
                                        f["L3_ffn_sh_down_w"].transpose(0, 2, 1).reshape(S * SF, D)]),
                        np.concatenate([np.repeat(np.arange(E), I), np.full(S * SF, E)]))

    a["heads"] = np.kron(np.eye(HC, dtype=np.float32), np.ones((DH, 1), np.float32))
    a["order"] = np.tile(np.arange(64, 0, -1, dtype=np.float32), (P, 1))
    a["ident"] = np.eye(P, dtype=np.float32)
    tri = np.tril(np.ones((P, P), np.float32))
    ones = np.ones((P, P), np.float32)
    a["cmask01"] = np.concatenate([tri, ones, tri], 1)
    a["cmask"] = np.where(a["cmask01"] > 0, np.float32(0), np.float32(-BIG)).astype(np.float32)
    a["cmask01T"] = np.concatenate([tri.T, ones, tri.T], 1)
    freq = (1.0 / np.float32(10000.0) ** (np.arange(0, EH, 2, dtype=np.float32) / np.float32(EH))).astype(np.float32)
    angle = (np.arange(SEQ, dtype=np.float32)[:, None] * freq[None, :]).reshape(QT, P, EH // 2).transpose(1, 0, 2)
    c, s = np.cos(angle).astype(np.float32), np.sin(angle).astype(np.float32)
    a["L1_cos"] = np.concatenate([c, c], 2)
    a["L1_sin"] = np.concatenate([-s, s], 2)
    a["L1_decay"] = np.stack([(ones - tri.T) / 16, -tri.T / 16], 1).astype(np.float32)
    a["before"] = ones - tri
    a["ones"] = ones
    return a


def kernel(**inputs):
    import concourse.bacc as _bacc
    from concourse.bass_utils import run_bass_kernel_spmd as _run

    nc = _bacc.Bacc("TRN2", target_bir_lowering=False, num_devices=1)
    a = host_layout(inputs)
    arrays = {f"in_{k}": np.ascontiguousarray(v) for k, v in a.items()}
    args = {k: nc.dram_tensor(f"in_{k}", arrays[f"in_{k}"].shape, F32, kind="ExternalInput").ap() for k in a}
    out = nc.dram_tensor("out_0", (NB, SEQ, D), F32, kind="ExternalOutput").ap()
    program(nc, args, out)
    r = _run(nc, [arrays], core_ids=[0])
    return r.results[0]["out_0"]
```

```python
from contextlib import ExitStack

import numpy as np

import concourse.bass as bass
from concourse import mybir

ALU = mybir.AluOpType
ACT = mybir.ActivationFunctionType
F32 = mybir.dt.float32
BF16 = mybir.dt.bfloat16
F32R = mybir.dt.float32r
AX_X = mybir.AxisListType.X

P = 128
D = 256
KD = D // P
SEQ = 256
NB = 8
TOK = NB * SEQ
NT = TOK // P
QT = SEQ // P
BIG = 1.0e30
PARTS = 3
NO_RANK = 255.0
SMALL = ("wq", "wk", "wv", "wo", "bq", "bk", "bv", "bo")
CONSTS = ("ident", "cmask", "cmask01", "before", "ones")


class Chain:

    def __init__(self, eng, sem, base=0):
        self.eng, self.sem, self.base, self.count = eng, sem, base, 0

    def link(self, ins):
        self.count += 1
        ins.then_inc(self.sem, 1)
        self.eng.wait_ge(self.sem, self.base + self.count)


class Space:

    def __init__(self, nc, ctx, name):
        self.nc, self.ctx, self.name = nc, ctx, name
        self.sems = []
        ctx.callback(self.close)

    def sb(self, name, shape, dtype=F32):
        return self.ctx.enter_context(self.nc.sbuf_tensor(f"{self.name}_{name}", shape, dtype))

    def ps(self, name, shape, dtype=F32):
        return self.ctx.enter_context(self.nc.psum_tensor(f"{self.name}_{name}", shape, dtype))

    def sem(self, name):
        self.sems.append(self.nc.alloc_semaphore(name=f"{self.name}_{name}"))
        return self.sems[-1]

    def close(self):
        if self.sems:
            self.nc.clear_and_free_semaphores(self.sems)
            self.nc.all_engine_barrier()


def setup(nc, x_dram, const):
    with ExitStack() as ctx:
        load_all(nc, Space(nc, ctx, "setup"), x_dram, const)


def load_all(nc, sp, x_dram, const):
    loaded = sp.sem("loaded")
    with nc.Block() as block:
        @block.sync
        def _(sync):
            sync.dma_start(const["x"][:, :, :], x_dram.rearrange("b (s p) d -> p (b s) d", p=P)).then_inc(loaded, 16)
            for name in CONSTS:
                sync.dma_start(const[name][:, :], const[name + "_dram"]).then_inc(loaded, 16)
            sync.wait_ge(loaded, 16 * (1 + len(CONSTS)))


def store(nc, out, const):
    with ExitStack() as ctx:
        store_all(nc, Space(nc, ctx, "store"), out, const)


def store_all(nc, sp, out, const):
    stored = sp.sem("stored")
    with nc.Block() as block:
        @block.sync
        def _(sync):
            sync.dma_start(out.rearrange("b (s p) d -> p (b s) d", p=P), const["x"][:, :, :]).then_inc(stored, 16)
            sync.wait_ge(stored, 16)


def normalize(nc, name, src, const, xn, xT, eps, rms, w_dram=None, add_src=False):
    with ExitStack() as ctx:
        sp = Space(nc, ctx, name)
        stats = sp.sb("stats", [P, NT, 6])
        mv = sp.sb("mv", [P, NT, 2])
        std = sp.sb("std", [P, NT])
        rstd = sp.sb("rstd", [P, NT])
        tmp = sp.sb("tmp", [P, NT])
        epsb = sp.sb("epsb", [P, 1])
        wcol = sp.sb("wcol", [P, KD])
        pT = [sp.ps(f"pT{i}", [P, KD, P]) for i in range(2)]
        stat_done = sp.sem("stat_done")
        agg_done = sp.sem("agg_done")
        var_ready = sp.sem("var_ready")
        std_ready = sp.sem("std_ready")
        xn_ready = sp.sem("xn_ready")
        turned = sp.sem("turned")
        copied = sp.sem("copied")
        w_in = sp.sem("w_in")
        chain = sp.sem("chain")
        ident = const["ident"]
        with nc.Block() as block:
            if w_dram is not None:
                @block.sync
                def _(sync):
                    sync.dma_start(wcol[:, :], w_dram).then_inc(w_in, 16)

            @block.vector
            def _(dve):
                nc.vector.memset(epsb[:, :], eps).then_inc(chain, 1)
                if add_src:
                    nc.vector.tensor_tensor(const["x"][:, :, :], const["x"][:, :, :], src[:, :, :],
                                            ALU.add).then_inc(chain, 1)
                    dve.wait_ge(chain, 2)
                for t in range(NT):
                    nc.vector.bn_stats(stats[:, t, :], src[:, t, :]).then_inc(stat_done, 1)
                for t in range(NT):
                    dve.wait_ge(stat_done, t + 1)
                    nc.vector.bn_aggr(mv[:, t, :], stats[:, t, :]).then_inc(agg_done, 1)
                dve.wait_ge(agg_done, NT)
                if rms:
                    nc.vector.tensor_tensor(tmp[:, :], mv[:, :, 0], mv[:, :, 0], ALU.mult).then_inc(chain, 1)
                    dve.wait_ge(chain, 3 if add_src else 2)
                    nc.vector.tensor_tensor(tmp[:, :], tmp[:, :], mv[:, :, 1], ALU.add).then_inc(var_ready, 1)
                else:
                    nc.vector.tensor_copy(tmp[:, :], mv[:, :, 1]).then_inc(var_ready, 1)
                dve.wait_ge(std_ready, 1)
                nc.vector.reciprocal(rstd[:, :], std[:, :]).then_inc(std_ready, 1)
                dve.wait_ge(std_ready, 2)
                for t in range(NT):
                    if rms:
                        nc.vector.tensor_scalar(xn[:, t, :], src[:, t, :], rstd[:, t:t + 1], None,
                                                ALU.mult).then_inc(xn_ready, 1)
                    else:
                        nc.vector.tensor_scalar(xn[:, t, :], src[:, t, :], mv[:, t, 0:1], rstd[:, t:t + 1],
                                                ALU.subtract, ALU.mult).then_inc(xn_ready, 1)

            @block.tensor
            def _(pe):
                for t in range(NT):
                    pe.wait_ge(xn_ready, t + 1)
                    if t >= 2:
                        pe.wait_ge(copied, t - 1)
                    for k in range(KD):
                        last = nc.tensor.transpose(pT[t % 2][:, k, :], xn[:, t, k * P:(k + 1) * P], ident[:, :])
                    last.then_inc(turned, 1)

            @block.scalar
            def _(act):
                act.wait_ge(chain, 1)
                act.wait_ge(var_ready, 1)
                nc.scalar.activation(std[:, :], tmp[:, :], ACT.Sqrt, bias=epsb[:, 0:1]).then_inc(std_ready, 1)
                if w_dram is not None:
                    act.wait_ge(w_in, 16)
                for t in range(NT):
                    act.wait_ge(turned, t + 1)
                    if w_dram is None:
                        nc.scalar.activation(xT[:, :, t * P:(t + 1) * P], pT[t % 2][:, :, :],
                                             ACT.Copy).then_inc(copied, 1)
                    else:
                        for k in range(KD):
                            last = nc.scalar.activation(xT[:, k, t * P:(t + 1) * P], pT[t % 2][:, k, :],
                                                        ACT.Copy, scale=wcol[:, k:k + 1])
                        last.then_inc(copied, 1)


def route(nc, name, const, xT, w_dram, E, K, cT, groups=None, bias_dram=None, renorm=True, cap=None, extra=None,
          slots=None):
    H = 2 if slots else 1
    C = E // 2 if slots else E + 1
    R = PARTS * C
    per = min(NT, 512 // E)
    banks = NT // per
    with ExitStack() as ctx:
        sp = Space(nc, ctx, name)
        w = sp.sb("w", [P, KD, E])
        bias = sp.sb("bias", [P, E])
        order = sp.sb("order", [P, E])
        lg = sp.sb("lg", [P, NT, E])
        ex = sp.sb("ex", [P, NT, E])
        key = sp.sb("key", [P, NT, E])
        sel = sp.sb("sel", [P, NT, E])
        eq = sp.sb("eq", [P, NT, E])
        c = sp.sb("c", [P, NT, H * C])
        parts = sp.sb("parts", [P, NT, H, PARTS, C], BF16)
        identb = sp.sb("identb", [P, P], BF16)
        m1 = sp.sb("m1", [P, NT, 1])
        m2 = sp.sb("m2", [P, NT, 1])
        plog = [sp.ps(f"plog{i}", [P, per, E]) for i in range(banks)]
        if extra or slots:
            pT = [sp.ps(f"pT{i}", [P, P]) for i in range(2)]
        pTb = [sp.ps(f"pTb{i}", [P, H, P], BF16) for i in range(2)]
        w_in = sp.sem("w_in")
        logits = sp.sem("logits")
        chain = sp.sem("chain")
        shifted = sp.sem("shifted")
        exped = sp.sem("exped")
        chosen = sp.sem("chosen")
        ranked = sp.sem("ranked")
        c_ready = sp.sem("c_ready")
        turned = sp.sem("turned")
        copied = sp.sem("copied")
        if groups:
            GR, GK = groups
            gs = sp.sb("gs", [P, NT, GR])
            gsel = sp.sb("gsel", [P, NT, GR])
            geq = sp.sb("geq", [P, NT, GR])
        if cap:
            tot = sp.sb("tot", [P, NT, E])
            rank = sp.sb("rank", [P, NT, E])
            base = sp.sb("base", [P, NT, E])
            prank = [sp.ps(f"prank{i}", [P, per, E]) for i in range(banks)]
            ptot = [sp.ps(f"ptot{i}", [P, per, E]) for i in range(banks)] if banks == 1 else plog
        if extra:
            over = sp.sb("over", [P, NT, E])
            wcol = sp.sb("wcol", [P, KD])
            px = sp.ps("px", [P, KD, E])
        ident = const["ident"]
        n_in = 2 + (bias_dram is not None) + (extra is not None)
        with nc.Block() as block:
            @block.sync
            def _(sync):
                sync.dma_start(w[:, :, :], w_dram).then_inc(w_in, 16)
                sync.dma_start(order[:, :], const["order_dram"][:, 0:E]).then_inc(w_in, 16)
                if bias_dram is not None:
                    sync.dma_start(bias[:, :], bias_dram[0, :].partition_broadcast(P)).then_inc(w_in, 16)
                if extra:
                    sync.dma_start(wcol[:, :], extra[3]).then_inc(w_in, 16)

            @block.tensor
            def _(pe):
                pe.wait_ge(w_in, 16 * n_in)
                for t in range(NT):
                    for k in range(KD):
                        last = nc.tensor.matmul(plog[t // per][:, t % per, :], xT[:, k, t * P:(t + 1) * P], w[:, k, :],
                                                start=(k == 0), stop=(k == KD - 1))
                last.then_inc(logits, 1)
                if cap:
                    pe.wait_ge(chosen, 1)
                    for i in range(banks):
                        nc.tensor.matmul(prank[i][:, :, :], const["before"][:, :], sel[:, i * per:(i + 1) * per, :],
                                         start=True, stop=True)
                        last = nc.tensor.matmul(ptot[i][:, :, :], const["ones"][:, :], sel[:, i * per:(i + 1) * per, :],
                                                start=True, stop=True)
                    last.then_inc(ranked, 1)
                pe.wait_ge(c_ready, 1)
                for t in range(NT):
                    if t >= 2:
                        pe.wait_ge(copied, t - 1)
                    for h in range(H):
                        last = nc.tensor.transpose(pTb[t % 2][0:R, h, :],
                                                   parts[:, t, h, :, :].rearrange("p a c -> p (a c)"), identb[:, :])
                    if extra:
                        last = nc.tensor.transpose(pT[t % 2][0:E, :], over[:, t, :], ident[:, :])
                    if slots:
                        last = nc.tensor.transpose(pT[t % 2][0:E, :], slots[0][:, t, :], ident[:, :])
                    last.then_inc(turned, 1)
                if extra:
                    for k in range(KD):
                        for t in range(NT):
                            last = nc.tensor.matmul(px[:, k, :], extra[0][:, t, k * P:(k + 1) * P], eq[:, t, :],
                                                    start=(t == 0), stop=(t == NT - 1))
                    last.then_inc(turned, 1)

            @block.scalar
            def _(act):
                act.wait_ge(shifted, 1)
                nc.scalar.activation(ex[:, :, :], ex[:, :, :], ACT.Exp).then_inc(exped, 1)
                for t in range(NT):
                    act.wait_ge(turned, t + 1)
                    if slots:
                        last = nc.scalar.activation(cT[0:R, :, t * P:(t + 1) * P], pTb[t % 2][0:R, :, :], ACT.Copy)
                        last = nc.scalar.activation(slots[1][0:E, t * P:(t + 1) * P], pT[t % 2][0:E, :], ACT.Copy)
                    else:
                        last = nc.scalar.activation(cT[0:R, t * P:(t + 1) * P], pTb[t % 2][0:R, 0, :], ACT.Copy)
                    if extra:
                        last = nc.scalar.activation(extra[2][0:E, t * P:(t + 1) * P], pT[t % 2][0:E, :], ACT.Copy)
                    last.then_inc(copied, 1)
                if extra:
                    act.wait_ge(turned, NT + 1)
                    for k in range(KD):
                        nc.scalar.activation(extra[1][:, k, :], px[:, k, :], ACT.Copy, scale=wcol[:, k:k + 1])

            @block.vector
            def _(dve):
                ch = Chain(dve, chain)

                def wide(small, n):
                    return small[:, :, 0:1].broadcast_to([P, NT, n])

                def take_best(key, eq, sel, n, times):
                    for _ in range(times):
                        ch.link(nc.vector.tensor_reduce(m1[:, :, 0], key[:, :, :], AX_X, ALU.max))
                        ch.link(nc.vector.tensor_tensor(eq[:, :, :], key[:, :, :], wide(m1, n), ALU.is_equal))
                        ch.link(nc.vector.tensor_tensor(eq[:, :, :], eq[:, :, :],
                                                        order[:, 0:n].unsqueeze(1).broadcast_to([P, NT, n]), ALU.mult))
                        ch.link(nc.vector.tensor_reduce(m1[:, :, 0], eq[:, :, :], AX_X, ALU.max))
                        ch.link(nc.vector.tensor_tensor(eq[:, :, :], eq[:, :, :], wide(m1, n), ALU.is_equal))
                        ch.link(nc.vector.scalar_tensor_tensor(out=key[:, :, :], in0=eq[:, :, :], scalar=-4 * BIG,
                                                               in1=key[:, :, :], op0=ALU.mult, op1=ALU.add))
                    ch.link(nc.vector.tensor_scalar(sel[:, :, :], key[:, :, :], -2 * BIG, None, ALU.is_lt))

                dve.wait_ge(w_in, 16 * n_in)
                dve.wait_ge(logits, 1)
                for i in range(banks):
                    ch.link(nc.vector.tensor_copy(lg[:, i * per:(i + 1) * per, :], plog[i][:, :, :]))
                ch.link(nc.vector.tensor_reduce(m2[:, :, 0], lg[:, :, :], AX_X, ALU.max))
                nc.vector.tensor_tensor(ex[:, :, :], lg[:, :, :], wide(m2, E), ALU.subtract).then_inc(shifted, 1)
                if bias_dram is not None:
                    ch.link(nc.vector.tensor_tensor(key[:, :, :], lg[:, :, :],
                                                    bias[:, :].unsqueeze(1).broadcast_to([P, NT, E]), ALU.add))
                else:
                    ch.link(nc.vector.tensor_copy(key[:, :, :], lg[:, :, :]))
                if groups:
                    ch.link(nc.vector.tensor_reduce(gs[:, :, :], key[:, :, :].rearrange("p t (g e) -> p (t g) e", g=GR),
                                                    AX_X, ALU.max))
                    take_best(gs, geq, gsel, GR, GK)
                    ch.link(nc.vector.tensor_scalar(gsel[:, :, :], gsel[:, :, :], -1.0, BIG, ALU.add, ALU.mult))
                    kg = key[:, :, :].rearrange("p t (g e) -> p (t g) e", g=GR)
                    gg = gsel[:, :, :].rearrange("p t g -> p (t g)").unsqueeze(2).broadcast_to([P, NT * GR, E // GR])
                    ch.link(nc.vector.tensor_tensor(kg, kg, gg, ALU.add))
                take_best(key, eq, sel, E, K)
                if cap:
                    dve.sem_inc(chosen, 1)
                dve.wait_ge(exped, 1)
                if not renorm:
                    ch.link(nc.vector.tensor_reduce(m1[:, :, 0], ex[:, :, :], AX_X, ALU.add))
                ch.link(nc.vector.tensor_tensor(c[:, :, 0:E], ex[:, :, :], sel[:, :, :], ALU.mult))
                if renorm:
                    ch.link(nc.vector.tensor_reduce(m1[:, :, 0], c[:, :, 0:E], AX_X, ALU.add))
                ch.link(nc.vector.reciprocal(m2[:, :, 0], m1[:, :, 0]))
                ch.link(nc.vector.tensor_tensor(c[:, :, 0:E], c[:, :, 0:E], wide(m2, E), ALU.mult))
                if not slots:
                    ch.link(nc.vector.memset(c[:, :, E:C], 1.0))
                if cap:
                    dve.wait_ge(ranked, 1)
                    for i in range(banks):
                        ch.link(nc.vector.tensor_copy(rank[:, i * per:(i + 1) * per, :], prank[i][:, :, :]))
                        ch.link(nc.vector.tensor_copy(tot[:, i * per:(i + 1) * per, :], ptot[i][:, :, :]))
                    ch.link(nc.vector.memset(base[:, 0, :], 0.0))
                    for t in range(1, NT):
                        ch.link(nc.vector.tensor_tensor(base[:, t, :], base[:, t - 1, :], tot[:, t - 1, :], ALU.add))
                    ch.link(nc.vector.tensor_tensor(rank[:, :, :], rank[:, :, :], base[:, :, :], ALU.add))
                    if extra:
                        ch.link(nc.vector.tensor_scalar(eq[:, :, :], rank[:, :, :], float(cap - 1), None, ALU.is_equal))
                        ch.link(nc.vector.tensor_tensor(eq[:, :, :], eq[:, :, :], sel[:, :, :], ALU.mult))
                        ch.link(nc.vector.tensor_scalar(over[:, :, :], rank[:, :, :], float(cap), None, ALU.is_ge))
                        ch.link(nc.vector.tensor_tensor(over[:, :, :], over[:, :, :], c[:, :, 0:E], ALU.mult))
                        ch.link(nc.vector.memset(cT[0:R, TOK:TOK + E], 0.0))
                        ch.link(nc.vector.tensor_copy(cT[0:E, TOK:TOK + E], ident[0:E, 0:E]))
                    if slots:
                        ch.link(nc.vector.scalar_tensor_tensor(out=eq[:, :, :], in0=rank[:, :, :], scalar=float(cap),
                                                               in1=sel[:, :, :], op0=ALU.is_lt, op1=ALU.mult))
                        ch.link(nc.vector.scalar_tensor_tensor(out=slots[0][:, :, :], in0=rank[:, :, :],
                                                               scalar=-NO_RANK, in1=eq[:, :, :], op0=ALU.add,
                                                               op1=ALU.mult))
                        ch.link(nc.vector.tensor_scalar(slots[0][:, :, :], slots[0][:, :, :], NO_RANK, None, ALU.add))
                    ch.link(nc.vector.tensor_scalar(rank[:, :, :], rank[:, :, :], float(cap), None, ALU.is_lt))
                    ch.link(nc.vector.tensor_tensor(c[:, :, 0:E], c[:, :, 0:E], rank[:, :, :], ALU.mult))
                ch.link(nc.vector.tensor_copy(identb[:, :], ident[:, :]))
                cv = c[:, :, :].rearrange("p t (h c) -> p t h c", h=H)
                for i in range(PARTS):
                    ch.link(nc.vector.tensor_copy(parts[:, :, :, i, :], cv))
                    if i < PARTS - 1:
                        ch.link(nc.vector.tensor_tensor(cv, cv, parts[:, :, :, i, :], ALU.subtract))
                dve.sem_inc(c_ready, 1)


HALF = TOK // 2
GRP = 512


def gated_ffn(nc, name, const, xT, bank, n_pieces, cT=None, extra=None):
    R = cT.shape[0] if cT is not None else 0
    WB = bank.shape[2]
    W13 = KD * 2 * P
    NX = extra[0].shape[2] if extra else 0
    G = 3 if extra else 2
    TH = HALF // P
    with ExitStack() as ctx:
        sp = Space(nc, ctx, name)
        w = [sp.sb(f"w{i}", [P, WB]) for i in range(2)]
        gate = [sp.sb(f"gate{g}", [P, GRP]) for g in range(2)]
        prod = sp.sb("prod", [P, GRP])
        hid = [sp.sb(f"hid{g}", [P, GRP]) for g in range(3)]
        zero = sp.sb("zero", [1, 512])
        xh = sp.sb("xh", [P, KD, TOK + NX], F32R)
        xl = sp.sb("xl", [P, KD, TOK + NX], F32R)
        wh = [sp.sb(f"wh{i}", [P, W13], F32R) for i in range(2)]
        wl = [sp.sb(f"wl{i}", [P, W13], F32R) for i in range(2)]
        xh_ready = sp.sem("xh_ready")
        xl_ready = sp.sem("xl_ready")
        wh_ready = sp.sem("wh_ready")
        wl_ready = sp.sem("wl_ready")
        if cT is not None:
            spread = [sp.sb(f"spread{i}", [P, P], BF16) for i in range(2)]
            spread_ready = sp.sem("spread_ready")
        pg = sp.ps("pg", [P, GRP])
        pu = sp.ps("pu", [P, GRP])
        pc = sp.ps("pc", [P, GRP])
        pout = [sp.ps(f"pout{i}", [P, 2, D]) for i in range(TH // 2)]
        if extra:
            pex = sp.ps("pex", [P, D])
            fex = sp.sb("fex", [P, D])
        w_in = [sp.sem(f"w_in{i}") for i in range(2)]
        w_used = sp.sem("w_used")
        zeroed = sp.sem("zeroed")
        g_done = sp.sem("g_done")
        u_done = sp.sem("u_done")
        c_done = sp.sem("c_done")
        silu_done = sp.sem("silu_done")
        prod_done = sp.sem("prod_done")
        hid_done = sp.sem("hid_done")
        ex_done = sp.sem("ex_done")
        fex_done = sp.sem("fex_done")
        out_done = sp.sem("out_done")
        added = sp.sem("added")

        hidden_ready = hid_done if cT is not None else prod_done
        odd = n_pieces % 2
        per_buf = [(n_pieces + 1) // 2, n_pieces // 2]

        def groups(half):
            at = [(half * HALF + g * GRP, GRP) for g in range(2)]
            return at + ([(TOK, NX)] if extra else [])

        x_pieces = [(xT, 0, GRP), (xT, GRP, GRP)] + ([(extra[0], TOK, NX)] if extra else []) + \
            [(xT, HALF, GRP), (xT, HALF + GRP, GRP)]

        def pieces(eng, body):
            whole = n_pieces // 2 - (0 if odd else 1)
            with eng.Fori(0, whole) as i:
                body(2 * i, 0, i, True)
                body(2 * i + 1, 1, i, True)
            if odd:
                body(n_pieces - 1, 0, n_pieces // 2, False)
            else:
                body(n_pieces - 2, 0, whole, True)
                body(n_pieces - 1, 1, whole, False)

        with nc.Block() as block:
            @block.sync
            def _(sync):
                def load(p, buf):
                    sync.dma_start(w[buf][:, :], bank[bass.ds(p, 1), :, :].rearrange("a p w -> p (a w)")
                                   ).then_inc(w_in[buf], 16)

                for half in range(2):
                    done = half * n_pieces
                    for buf in range(2):
                        if half:
                            sync.wait_ge(w_used, done - 1 + buf + (odd if buf == 0 else 0))
                        load(buf, buf)
                    with sync.Fori(1, n_pieces // 2) as i:
                        for buf in range(2):
                            sync.wait_ge(w_used, 2 * i + (done + buf - 1))
                            load(2 * i + buf, buf)
                    if odd:
                        sync.wait_ge(w_used, done + n_pieces - 2)
                        load(n_pieces - 1, 0)

            @block.tensor
            def _(pe):
                def piece(half, p, buf, turn):
                    n = p + half * n_pieces
                    pe.wait_ge(w_in[buf], turn * 16 + 16 * (half * per_buf[buf] + 1))
                    pe.wait_ge(wl_ready, n + 1)
                    wb = w[buf]
                    w2 = wb[:, KD * 2 * P:KD * 2 * P + D]

                    def product(to, col, at, width):
                        parts = [(wp, xp, k) for k in range(KD) for wp, xp in ((wh, xh), (wh, xl), (wl, xh))]
                        for i, (wp, xp, k) in enumerate(parts):
                            c = k * 2 * P + col
                            last = nc.tensor.matmul(to[:, 0:width], wp[buf][:, c:c + P], xp[:, k, at:at + width],
                                                    start=(i == 0), stop=(i == len(parts) - 1))
                        return last

                    def hidden(g, at, width):
                        m = n * G + g
                        pe.wait_ge(silu_done, m + 1)
                        product(pg, 0, at, width).then_inc(g_done, 1)
                        pe.wait_ge(prod_done, m + 1)
                        product(pu, P, at, width).then_inc(u_done, 1)
                        if cT is not None:
                            pe.wait_ge(hid_done, m + 1)
                            pe.wait_ge(spread_ready, n + 1)
                            nc.tensor.matmul(pc[:, 0:width], spread[buf][0:R, :],
                                             cT[:, at:at + width], start=True, stop=True).then_inc(c_done, 1)

                    def outputs(g):
                        pe.wait_ge(hidden_ready, n * G + (g + 2))
                        if g == 2:
                            return nc.tensor.matmul(pex[0:NX, :], hid[2][:, 0:NX], w2,
                                                    start=False, stop=False, skip_group_check=True)
                        for j in range(GRP // P):
                            t = g * (GRP // P) + j
                            last = nc.tensor.matmul(pout[t // 2][:, t % 2, :], hid[g][:, j * P:(j + 1) * P], w2,
                                                    start=False, stop=False, skip_group_check=True)
                        return last

                    at = groups(half)
                    hidden(0, *at[0])
                    hidden(1, *at[1])
                    outputs(0)
                    if extra:
                        hidden(2, *at[2])
                    last = outputs(1)
                    if extra:
                        last = outputs(2)
                    last.then_inc(w_used, 1)

                pe.wait_ge(zeroed, 1)
                if cT is not None:
                    pe.sem_inc(c_done, 2 * G)
                for half in range(2):
                    pe.wait_ge(added, half * (TH // 2))
                    pe.wait_ge(xl_ready, len(x_pieces) if half else len(x_pieces) - 2)
                    for i in range(TH // 2):
                        nc.tensor.matmul(pout[i][:, :, :], zero[:, 0:P], zero[:, :], start=True, stop=False,
                                         skip_group_check=True)
                    if extra:
                        nc.tensor.matmul(pex[:, :], zero[:, 0:P], zero[:, 0:D], start=True, stop=False,
                                         skip_group_check=True)
                    with pe.Fori(0, n_pieces // 2) as i:
                        for buf in range(2):
                            piece(half, 2 * i + buf, buf, i)
                    if odd:
                        piece(half, n_pieces - 1, 0, n_pieces // 2)
                    if extra:
                        pe.wait_ge(w_used, (half + 1) * n_pieces)
                        nc.tensor.matmul(pex[:, :], zero[:, 0:P], zero[:, 0:D], start=False, stop=True,
                                         skip_group_check=True).then_inc(ex_done, 1)
                        pe.wait_ge(fex_done, half + 1)
                        for t in range(TH):
                            at = half * HALF + t * P
                            nc.tensor.matmul(pout[t // 2][:, t % 2, :], extra[1][:, at:at + P], fex[0:NX, :],
                                             start=False, stop=False, skip_group_check=True)
                    for i in range(TH // 2):
                        last = nc.tensor.matmul(pout[i][:, :, :], zero[:, 0:P], zero[:, :], start=False, stop=True,
                                                skip_group_check=True)
                    last.then_inc(out_done, 1)

            if cT is not None:
                @block.gpsimd
                def _(pool):
                    def piece(half, p, buf, turn):
                        pool.wait_ge(w_in[buf], turn * 16 + 16 * (half * per_buf[buf] + 1))
                        pool.wait_ge(c_done, p * G + G * (half * n_pieces + 1 + (half and buf == 0 and odd)))
                        nc.gpsimd.tensor_tensor(spread[buf][0:R, :], w[buf][0:R, KD * 2 * P + D:KD * 2 * P + D + P],
                                                const["ones"][0:R, :], ALU.mult).then_inc(spread_ready, 1)

                    for half in range(2):
                        with pool.Fori(0, n_pieces // 2) as i:
                            for buf in range(2):
                                piece(half, 2 * i + buf, buf, i)
                        if odd:
                            piece(half, n_pieces - 1, 0, n_pieces // 2)

            @block.scalar
            def _(act):
                def split_weights(half, buf, turn):
                    act.wait_ge(w_in[buf], turn * 16 + 16 * (half * per_buf[buf] + 1))
                    nc.scalar.activation(wh[buf][:, :], w[buf][:, 0:W13], ACT.Copy).then_inc(wh_ready, 1)

                act.sem_inc(silu_done, 1)
                for xs, at, width in x_pieces:
                    src = xs[:, :, at:at + width] if xs is xT else xs[:, :, :]
                    nc.scalar.activation(xh[:, :, at:at + width], src, ACT.Copy).then_inc(xh_ready, 1)
                for half in range(2):
                    def piece(p, buf, turn, more):
                        n = p + half * n_pieces
                        for g, (at, width) in enumerate(groups(half)):
                            act.wait_ge(g_done, n * G + (g + 1))
                            nc.scalar.activation(gate[g % 2][:, 0:width], pg[:, 0:width],
                                                 ACT.Silu).then_inc(silu_done, 1)
                        if more:
                            split_weights(half, 1 - buf, turn + buf)

                    if half:
                        act.wait_ge(w_used, n_pieces)
                    split_weights(half, 0, 0)
                    pieces(act, piece)
                    if extra:
                        act.wait_ge(ex_done, half + 1)
                        nc.scalar.activation(fex[:, :], pex[:, :], ACT.Copy).then_inc(fex_done, 1)

            @block.vector
            def _(dve):
                def split_weights(n, buf):
                    dve.wait_ge(wh_ready, n + 1)
                    nc.vector.tensor_tensor(wl[buf][:, :], w[buf][:, 0:W13], wh[buf][:, :],
                                            ALU.subtract).then_inc(wl_ready, 1)

                nc.vector.memset(zero[:, :], 0.0).then_inc(zeroed, 1)
                dve.sem_inc(prod_done, 1)
                if cT is not None:
                    dve.sem_inc(hid_done, 1)
                for i, (xs, at, width) in enumerate(x_pieces):
                    dve.wait_ge(xh_ready, i + 1)
                    src = xs[:, :, at:at + width] if xs is xT else xs[:, :, :]
                    nc.vector.tensor_tensor(xl[:, :, at:at + width], src, xh[:, :, at:at + width],
                                            ALU.subtract).then_inc(xl_ready, 1)
                for half in range(2):
                    def piece(p, buf, turn, more):
                        n = p + half * n_pieces
                        for g, (at, width) in enumerate(groups(half)):
                            m = n * G + g
                            dve.wait_ge(silu_done, m + 2)
                            dve.wait_ge(u_done, m + 1)
                            dve.wait_ge(hidden_ready, m + 1)
                            to = prod if cT is not None else hid[g]
                            last = nc.vector.tensor_tensor(to[:, 0:width], gate[g % 2][:, 0:width], pu[:, 0:width],
                                                           ALU.mult)
                            last.then_inc(prod_done, 1)
                            if cT is not None:
                                dve.wait_ge(prod_done, m + 2)
                                dve.wait_ge(c_done, m + (2 * G + 1))
                                nc.vector.tensor_tensor(hid[g][:, 0:width], prod[:, 0:width], pc[:, 0:width],
                                                        ALU.mult).then_inc(hid_done, 1)
                        if more:
                            split_weights(n + 1, 1 - buf)

                    split_weights(half * n_pieces, 0)
                    pieces(dve, piece)
                    dve.wait_ge(out_done, half + 1)
                    for i in range(TH // 2):
                        t = half * TH + 2 * i
                        nc.vector.tensor_tensor(const["x"][:, t:t + 2, :], const["x"][:, t:t + 2, :],
                                                pout[i][:, :, :], ALU.add).then_inc(added, 1)




CAP = 32
SEX = 64
SE = P // CAP
SCH = SEX // SE
NSLOT = SEX * CAP


def slot_ffn(nc, name, const, xn, a, bank, key, keyT, cT):
    WB = KD * 2 * P + D
    S2 = 2 * CAP
    NP = SEX // 2
    SB = NSLOT // 512
    with ExitStack() as ctx:
        sp = Space(nc, ctx, name)
        xg = sp.sb("xg", [P, KD, NSLOT])
        y = sp.sb("y", [P, SCH, D])
        with ExitStack() as inner:
            gather_slots(nc, Space(nc, inner, name + "g"), const, xn, a, key, xg, SB)
        with ExitStack() as inner:
            slot_experts(nc, Space(nc, inner, name + "e"), a, bank, xg, y, WB, S2)
        with ExitStack() as inner:
            scatter_slots(nc, Space(nc, inner, name + "s"), const, a, keyT, cT, y)


def gather_slots(nc, sp, const, xn, a, key, xg, SB):
    ranks = sp.sb("ranks", [P, CAP])
    hot = [sp.sb(f"hot{i}", [P, SEX, CAP], F32R) for i in range(2)]
    high = [sp.sb(f"high{i}", [P, D], F32R) for i in range(2)]
    low = [sp.sb(f"low{i}", [P, D], F32R) for i in range(2)]
    px = [[sp.ps(f"px{k}_{b}", [P, 512]) for b in range(SB)] for k in range(KD)]
    w_in = sp.sem("w_in")
    hot_ready = sp.sem("hot_ready")
    high_ready = sp.sem("high_ready")
    low_ready = sp.sem("low_ready")
    used = sp.sem("used")
    with nc.Block() as block:
        @block.sync
        def _(sync):
            sync.dma_start(ranks[:, :], a["slot_ranks"]).then_inc(w_in, 16)

        @block.vector
        def _(dve):
            def tile(t, i):
                dve.wait_ge(used, t + 1)
                nc.vector.tensor_tensor(hot[i][:, :, :], key[:, bass.ds(t, 1), :].rearrange("p a e -> p (a e)")
                                        .unsqueeze(2).broadcast_to([P, SEX, CAP]),
                                        ranks[:, :].unsqueeze(1).broadcast_to([P, SEX, CAP]),
                                        ALU.is_equal).then_inc(hot_ready, 1)
                dve.wait_ge(high_ready, t + 1)
                nc.vector.tensor_tensor(low[i][:, :], xn[:, bass.ds(t, 1), :].rearrange("p a d -> p (a d)"),
                                        high[i][:, :], ALU.subtract).then_inc(low_ready, 1)

            dve.wait_ge(w_in, 16)
            with dve.Fori(0, NT // 2) as t:
                for i in range(2):
                    tile(2 * t + i, i)
            dve.wait_ge(used, NT + 2)
            for b in range(SB):
                nc.vector.tensor_copy(xg[:, 1, b * 512:(b + 1) * 512], px[1][b][:, :])

        @block.scalar
        def _(act):
            def tile(t, i):
                act.wait_ge(used, t + 1)
                nc.scalar.activation(high[i][:, :], xn[:, bass.ds(t, 1), :].rearrange("p a d -> p (a d)"),
                                     ACT.Copy).then_inc(high_ready, 1)

            with act.Fori(0, NT // 2) as t:
                for i in range(2):
                    tile(2 * t + i, i)
            act.wait_ge(used, NT + 2)
            for b in range(SB):
                nc.scalar.activation(xg[:, 0, b * 512:(b + 1) * 512], px[0][b][:, :], ACT.Copy)

        @block.tensor
        def _(pe):
            def tile(t, i, first=False, final=False):
                pe.wait_ge(hot_ready, t + 1)
                pe.wait_ge(low_ready, t + 1)
                flat = hot[i][:, :, :].rearrange("p e r -> p (e r)")
                for k in range(KD):
                    for part in (high, low):
                        for b in range(SB):
                            last = nc.tensor.matmul(px[k][b][:, :], part[i][:, k * P:(k + 1) * P],
                                                    flat[:, b * 512:(b + 1) * 512],
                                                    start=(first and part is high), stop=(final and part is low))
                last.then_inc(used, 1)

            pe.sem_inc(used, 2)
            tile(0, 0, first=True)
            tile(1, 1)
            with pe.Fori(1, NT // 2 - 1) as t:
                for i in range(2):
                    tile(2 * t + i, i)
            tile(NT - 2, 0)
            tile(NT - 1, 1, final=True)



def slot_experts(nc, sp, a, bank, xg, y, WB, S2):
    NW = 4
    w = [[sp.sb(f"w{i}_{j}", [P, WB]) for j in range(2)] for i in range(NW)]
    pair = sp.sb("pair", [P, S2])
    gate = sp.sb("gate", [P, 2, S2])
    prod = sp.sb("prod", [P, 2, S2])
    hid = [sp.sb(f"hid{i}", [P, 3 * P]) for i in range(2)]
    pg = [sp.ps(f"pg{i}", [P, 512]) for i in range(2)]
    pu = [sp.ps(f"pu{i}", [P, 512]) for i in range(2)]
    py = [sp.ps(f"py{i}", [P, 512]) for i in range(2)]
    pair_in = sp.sem("pair_in")
    w_in = [sp.sem(f"w_in{i}") for i in range(NW)]
    w_used = sp.sem("w_used")
    zeroed = sp.sem("zeroed")
    g_done = sp.sem("g_done")
    u_done = sp.sem("u_done")
    masked = sp.sem("masked")
    hid_ready = sp.sem("hid_ready")
    silu_ready = sp.sem("silu_ready")
    y_read = sp.sem("y_read")

    def cols(buf):
        return buf[:, 0:2 * S2].rearrange("p (j s) -> p j s", j=2)

    with nc.Block() as block:
        @block.sync
        def _(sync):
            sync.dma_start(pair[:, :], a["slot_pair"]).then_inc(pair_in, 16)

            def load(q, i):
                for j in range(2):
                    sync.dma_start(w[i][j][:, :], bank[bass.ds(2 * q + j, 1), :, 0:WB].rearrange("a p w -> p (a w)")
                                   ).then_inc(w_in[i], 16)

            for i in range(NW):
                load(i, i)
            with sync.Fori(1, SCH // NW) as q:
                for i in range(NW):
                    sync.wait_ge(w_used, NW * q + (i + 3 - NW))
                    load(NW * q + i, i)

        @block.tensor
        def _(pe):
            def hidden(q, i, turn):
                pe.wait_ge(w_in[i], 32 * turn + 32)
                pe.wait_ge(hid_ready, q + 1)
                for bank_of, at, done in ((pg, 0, g_done), (pu, P, u_done)):
                    for j in range(2):
                        for k in range(KD):
                            last = nc.tensor.matmul(bank_of[i % 2][:, j * S2:(j + 1) * S2],
                                                    w[i][j][:, k * 2 * P + at:k * 2 * P + at + P],
                                                    xg[:, k, bass.ds(q * P + j * S2, S2)], start=(k == 0), stop=(k == KD - 1))
                    last.then_inc(done, 1)

            def outputs(q, i):
                pe.wait_ge(hid_ready, q + 3)
                pe.wait_ge(y_read, q + 1)
                for j in range(2):
                    last = nc.tensor.matmul(py[i % 2][:, 0:D], hid[i % 2][:, j * P:(j + 1) * P],
                                            w[i][j][:, KD * 2 * P:WB], start=(j == 0), stop=(j == 1))
                last.then_inc(w_used, 1)

            pe.sem_inc(w_used, 2)
            hidden(0, 0, 0)
            with pe.Fori(0, SCH // NW - 1) as q:
                for i in range(NW):
                    hidden(NW * q + (i + 1), (i + 1) % NW, q + (i + 1) // NW)
                    outputs(NW * q + i, i)
            for i in range(NW):
                if i + 1 < NW:
                    hidden(SCH - NW + i + 1, i + 1, SCH // NW - 1)
                outputs(SCH - NW + i, i)

        @block.scalar
        def _(act):
            def silu(q, i):
                act.wait_ge(masked, q + 1)
                act.wait_ge(g_done, q + 1)
                nc.scalar.activation(gate[:, :, :], cols(pg[i]), ACT.Silu).then_inc(silu_ready, 1)

            def copy_out(q, i):
                act.wait_ge(w_used, q + 3)
                nc.scalar.activation(y[:, bass.ds(q, 1), :].rearrange("p a d -> p (a d)"), py[i][:, 0:D],
                                     ACT.Copy).then_inc(y_read, 1)

            act.sem_inc(y_read, 2)
            silu(0, 0)
            silu(1, 1)
            with act.Fori(0, SCH // 2 - 1) as q:
                for i in range(2):
                    copy_out(2 * q + i, i)
                    silu(2 * q + i + 2, i)
            copy_out(SCH - 2, 0)
            copy_out(SCH - 1, 1)

        @block.vector
        def _(dve):
            def chunk(q, i):
                dve.wait_ge(silu_ready, q + 1)
                dve.wait_ge(hid_ready, q + 2)
                nc.vector.tensor_tensor(prod[:, :, :], gate[:, :, :], pair[:, :].unsqueeze(1).broadcast_to([P, 2, S2]),
                                        ALU.mult).then_inc(masked, 1)
                dve.wait_ge(masked, q + 2)
                dve.wait_ge(u_done, q + 1)
                dve.wait_ge(w_used, q + 1)
                nc.vector.tensor_tensor(hid[i][:, :].rearrange("p (j c) -> p j c", j=2)[:, :, 0:S2], prod[:, :, :],
                                        cols(pu[i]), ALU.mult).then_inc(hid_ready, 1)

            for i in range(2):
                nc.vector.memset(hid[i][:, :], 0.0).then_inc(zeroed, 1)
            dve.wait_ge(zeroed, 2)
            dve.wait_ge(pair_in, 16)
            dve.sem_inc(masked, 1)
            dve.sem_inc(hid_ready, 2)
            with dve.Fori(0, SCH // 2) as q:
                for i in range(2):
                    chunk(2 * q + i, i)


def scatter_slots(nc, sp, const, a, keyT, cT, y):
    TH = HALF // P
    RC = cT.shape[0]
    rank = sp.sb("rank", [P, 1])
    sel = [sp.sb(f"sel{i}", [P, 2, P]) for i in range(2)]
    selb = [sp.sb(f"selb{i}", [P, 2, P], BF16) for i in range(2)]
    wt = [[sp.sb(f"wt{i}_{g}", [P, GRP]) for g in range(2)] for i in range(2)]
    rk = [sp.sb(f"rk{g}", [P, GRP]) for g in range(2)]
    prank = [sp.ps(f"prank{g}", [P, GRP]) for g in range(2)]
    pc = [sp.ps(f"pc{g}", [P, GRP]) for g in range(2)]
    pout = [sp.ps(f"pout{i}", [P, 2, D]) for i in range(TH // 2)]
    rank_in = sp.sem("rank_in")
    sel_in = [sp.sem(f"sel_in{i}") for i in range(2)]
    selb_ready = sp.sem("selb_ready")
    spread_done = sp.sem("spread_done")
    rk_ready = sp.sem("rk_ready")
    wt_ready = sp.sem("wt_ready")
    wt_used = sp.sem("wt_used")
    zeroed = sp.sem("zeroed")
    out_done = sp.sem("out_done")
    added = sp.sem("added")
    zero = sp.sb("zero", [1, GRP])

    def pairs(eng, body):
        for half in range(2):
            for side in range(2):
                with eng.Fori(0, SCH // 4) as i:
                    at = side * (SCH // 2)
                    body(half, side, 2 * i + at, 2 * i + (at + half * SCH), i + (at // 2 + half * (SCH // 2)))
            yield half

    with nc.Block() as block:
        @block.sync
        def _(sync):
            sync.dma_start(rank[:, :], a["slot_rank"]).then_inc(rank_in, 16)

            def body(half, side, q, n, m):
                for i in range(2):
                    sync.wait_ge(selb_ready, n + (i + 1))
                    sync.dma_start(sel[i][:, :, :], a["slot_spread"][bass.ds(q + i, 1), :, :, :]
                                   .rearrange("a p j s -> p (a j) s")).then_inc(sel_in[i], 16)

            for _ in pairs(sync, body):
                pass

        @block.gpsimd
        def _(pool):
            def body(half, side, q, n, m):
                for i in range(2):
                    pool.wait_ge(sel_in[i], 16 * m + 16)
                    pool.wait_ge(spread_done, 2 * n + (2 * i + 2))
                    nc.gpsimd.tensor_tensor(selb[i][:, :, :], sel[i][:, :, :],
                                            const["ones"][:, :].unsqueeze(1).broadcast_to([P, 2, P]),
                                            ALU.mult).then_inc(selb_ready, 1)

            pool.sem_inc(selb_ready, 2)
            for _ in pairs(pool, body):
                pass

        @block.tensor
        def _(pe):
            def spread(half, side, n, i, g):
                at = half * HALF + g * GRP
                pe.wait_ge(selb_ready, n + (i + 3))
                pe.wait_ge(wt_ready, 2 * n + (2 * i + g + 1))
                nc.tensor.matmul(prank[g][:, :], selb[i][0:SEX, 0, :], keyT[:, at:at + GRP], start=True, stop=True)
                nc.tensor.matmul(pc[g][:, :], selb[i][0:RC, 1, :], cT[:, side, at:at + GRP], start=True,
                                 stop=True).then_inc(spread_done, 1)

            def outputs(q, n, i, g):
                pe.wait_ge(wt_ready, 2 * n + (2 * i + g + 3))
                for j in range(GRP // P):
                    t = g * (GRP // P) + j
                    last = nc.tensor.matmul(pout[t // 2][:, t % 2, :], wt[i][g][:, j * P:(j + 1) * P],
                                            y[:, bass.ds(q + i, 1), :].rearrange("p a d -> p (a d)"),
                                            start=False, stop=False, skip_group_check=True)
                last.then_inc(wt_used, 1)

            def body(half, side, q, n, nxt):
                outputs(q, n, 0, 0)
                spread(half, side, n, 1, 0)
                outputs(q, n, 0, 1)
                spread(half, side, n, 1, 1)
                outputs(q, n, 1, 0)
                if nxt is not None:
                    spread(half, nxt, n + 2, 0, 0)
                outputs(q, n, 1, 1)
                if nxt is not None:
                    spread(half, nxt, n + 2, 0, 1)

            def clear():
                for i in range(TH // 2):
                    nc.tensor.matmul(pout[i][:, :, :], zero[:, 0:P], zero[:, :], start=True, stop=False,
                                     skip_group_check=True)

            pe.sem_inc(spread_done, 4)
            pe.sem_inc(wt_used, 4)
            pe.wait_ge(zeroed, 1)
            clear()
            for half in range(2):
                spread(half, 0, half * SCH, 0, 0)
                spread(half, 0, half * SCH, 0, 1)
                for side in range(2):
                    at = side * (SCH // 2)
                    with pe.Fori(0, SCH // 4 - 1) as i:
                        body(half, side, 2 * i + at, 2 * i + (at + half * SCH), side)
                    end = at + SCH // 2 - 2
                    body(half, side, end, end + half * SCH, None if side else 1)
                for i in range(TH // 2):
                    last = nc.tensor.matmul(pout[i][:, :, :], zero[:, 0:P], zero[:, :], start=False, stop=True,
                                            skip_group_check=True)
                last.then_inc(out_done, 1)
                if half == 0:
                    pe.wait_ge(added, TH // 2)
                    clear()

        @block.scalar
        def _(act):
            def body(half, side, q, n, m):
                for i in range(2):
                    for g in range(2):
                        act.wait_ge(spread_done, 2 * n + (2 * i + g + 5))
                        act.wait_ge(wt_ready, 2 * n + (2 * i + g + 1))
                        nc.scalar.activation(rk[g][:, :], prank[g][:, :], ACT.Copy).then_inc(rk_ready, 1)

            for _ in pairs(act, body):
                pass

        @block.vector
        def _(dve):
            def body(half, side, q, n, m):
                for i in range(2):
                    for g in range(2):
                        dve.wait_ge(rk_ready, 2 * n + (2 * i + g + 1))
                        dve.wait_ge(wt_used, 2 * n + (2 * i + g + 1))
                        nc.vector.scalar_tensor_tensor(out=wt[i][g][:, :], in0=rk[g][:, :], scalar=rank[:, 0:1],
                                                       in1=pc[g][:, :], op0=ALU.is_equal,
                                                       op1=ALU.mult).then_inc(wt_ready, 1)

            nc.vector.memset(zero[:, :], 0.0).then_inc(zeroed, 1)
            dve.wait_ge(rank_in, 16)
            dve.sem_inc(wt_ready, 2)
            for half in pairs(dve, body):
                dve.wait_ge(out_done, half + 1)
                for i in range(TH // 2):
                    t = half * TH + 2 * i
                    nc.vector.tensor_tensor(const["x"][:, t:t + 2, :], const["x"][:, t:t + 2, :],
                                            pout[i][:, :, :], ALU.add).then_inc(added, 1)


HS = 16
DH = D // HS
HC = P // DH
SC = P + SEQ
AHEAD = 4
SUMS_AHEAD = 3
SLOTS = 2 * AHEAD
VS = P + DH


def attention_small(nc, name, const, xT, w, scale):
    with ExitStack() as ctx:
        sp = Space(nc, ctx, name)
        wts = {n: sp.sb(n, [P, KD, D]) for n in ("wq", "wk", "wv", "wo")}
        bq = sp.sb("bq", [P, KD])
        bk = sp.sb("bk", [P, KD])
        bv = sp.sb("bv", [1, D])
        bo = sp.sb("bo", [1, D])
        heads = sp.sb("heads", [P, HC])
        bkh = sp.sb("bkh", [P, HS])
        xb = sp.sb("xb", [P, KD, SEQ])
        qT = sp.sb("qT", [P, KD, SEQ])
        kT = sp.sb("kT", [P, HS, SEQ])
        v = sp.sb("v", [P, QT * KD, HC * VS])
        s = sp.sb("s", [P, SLOTS, SC])
        nmax = sp.sb("nmax", [P, SLOTS, QT])
        rsum = sp.sb("rsum", [P, HS, QT])
        rinv = sp.sb("rinv", [P, HS, QT])
        pT = [sp.sb(f"pT{i}", [P, SC]) for i in range(2)]
        oT = sp.sb("oT", [P, KD, SEQ])
        ring = [sp.ps(f"ring{i}", [P, 512]) for i in range(4)]
        pv = sp.ps("pv", [P, KD, SEQ])
        ppT = [sp.ps(f"ppT{i}", [P, 512]) for i in range(2)]
        pend = sp.ps("pend", [P, 512])
        w_in = sp.sem("w_in")
        bkh_ready = sp.sem("bkh_ready")
        xb_ready = sp.sem("xb_ready")
        q_done = sp.sem("q_done")
        k_done = sp.sem("k_done")
        v_done = sp.sem("v_done")
        q_ready = sp.sem("q_ready")
        k0_ready = sp.sem("k0_ready")
        k1_ready = sp.sem("k1_ready")
        v_ready = sp.sem("v_ready")
        s_done = sp.sem("s_done")
        s_read = sp.sem("s_read")
        max_ready = sp.sem("max_ready")
        exp_ready = sp.sem("exp_ready")
        turned = sp.sem("turned")
        even_copied = sp.sem("even_copied")
        odd_copied = sp.sem("odd_copied")
        pv_done = sp.sem("pv_done")
        inv_ready = sp.sem("inv_ready")
        o_ready = sp.sem("o_ready")
        scaled = sp.sem("scaled")
        v_zeroed = sp.sem("v_zeroed")
        out_done = sp.sem("out_done")
        added = sp.sem("added")
        ident, ones, cmask = const["ident"], const["ones"], const["cmask"]
        spans = ((0, P), (P, SC))

        def batches(eng, run):
            with eng.Fori(0, NB - 1) as b:
                run(b, True)
            run(NB - 1, False)

        with nc.Block() as block:
            @block.sync
            def _(sync):
                for n in ("wq", "wk", "wv", "wo"):
                    sync.dma_start(wts[n][:, :, :], w[n]).then_inc(w_in, 16)
                for to, n in ((bq, "bq"), (bk, "bk"), (bv, "bv"), (bo, "bo"), (heads, "heads")):
                    sync.dma_start(to[:, :], w[n]).then_inc(w_in, 16)

            @block.gpsimd
            def _(pool):
                def scale_rows(b, h):
                    pool.wait_ge(inv_ready, b * HS + (h + 1))
                    for t, (lo, hi) in enumerate(spans):
                        rows = s[:, h % SLOTS, lo:hi]
                        last = nc.gpsimd.tensor_tensor(rows, rows, rinv[:, h, t:t + 1].broadcast_to([P, hi - lo]),
                                                       ALU.mult)
                    last.then_inc(scaled, 1)

                def run(b, more):
                    for h in range(HS):
                        scale_rows(b, h)
                        if more and h == HC:
                            pool.wait_ge(v_done, b + 1)
                            nc.gpsimd.tensor_copy(xb[:, :, :], xT[:, :, bass.ds(b * SEQ + SEQ, SEQ)]
                                                  ).then_inc(xb_ready, 1)

                nc.gpsimd.tensor_copy(xb[:, :, :], xT[:, :, 0:SEQ]).then_inc(xb_ready, 1)
                batches(pool, run)

            @block.tensor
            def _(pe):
                def project(b):
                    pe.wait_ge(xb_ready, b + 1)
                    for n, bank, done in (("wk", 1, k_done), ("wq", 0, q_done)):
                        for c in range(KD):
                            to = ring[bank + c] if n == "wk" else ring[bank]
                            at = 0 if n == "wk" else c * SEQ
                            for k in range(KD):
                                last = nc.tensor.matmul(to[:, at:at + SEQ], wts[n][:, k, c * P:(c + 1) * P], xb[:, k, :],
                                                        start=(k == 0), stop=(k == KD - 1))
                        last.then_inc(done, 1)
                    for t in range(QT):
                        for k in range(KD):
                            nc.tensor.matmul(ring[3][:, t * D:(t + 1) * D], xb[:, k, t * P:(t + 1) * P],
                                             wts["wv"][:, k, :], start=(k == 0), stop=False)
                        last = nc.tensor.matmul(ring[3][:, t * D:(t + 1) * D], ones[0:1, :], bv[:, :],
                                                start=False, stop=True)
                    last.then_inc(v_done, 1)

                def scores(b, h):
                    if h >= 4:
                        pe.wait_ge(s_read, b * HS + (h - 3))
                    c = h // HC
                    nc.tensor.matmul(ring[h % 4][:, 0:P], qT[:, c, 0:P], kT[:, h, 0:P], start=True, stop=True)
                    nc.tensor.matmul(ring[h % 4][:, P:SC], qT[:, c, P:SEQ], kT[:, h, :],
                                     start=True, stop=True).then_inc(s_done, 1)

                def turn(b, h):
                    pe.wait_ge(scaled, b * HS + (h + 1))
                    pe.wait_ge(odd_copied if h % 2 else even_copied, b * (HS // 2) + (h // 2 + 1))
                    for i in range(3):
                        last = nc.tensor.transpose(ppT[h % 2][:, i * P:(i + 1) * P],
                                                   s[:, h % SLOTS, i * P:(i + 1) * P], ident[:, :])
                    last.then_inc(turned, 1)

                def values(b, h):
                    pe.wait_ge(odd_copied if h % 2 else even_copied, b * (HS // 2) + (h // 2 + 2))
                    if h == 0:
                        pe.wait_ge(o_ready, b + 1)
                    c, j = h // HC, h % HC
                    first, final = j == 0, j == HC - 1
                    nc.tensor.matmul(pv[:, c, :], v[:, c, j * P:(j + 1) * P], pT[h % 2][:, 0:SEQ],
                                     start=first, stop=final, skip_group_check=True)
                    last = nc.tensor.matmul(pv[:, c, P:SEQ], v[:, KD + c, j * P:(j + 1) * P], pT[h % 2][:, SEQ:SC],
                                            start=False, stop=final, skip_group_check=True)
                    if h == HS - 1:
                        last.then_inc(pv_done, 1)

                def first_scores(b):
                    pe.wait_ge(q_ready, b + 1)
                    pe.wait_ge(k0_ready, b + 1)
                    pe.wait_ge(k1_ready, b + 1)
                    pe.wait_ge(v_ready, b + 1)
                    for h in range(AHEAD):
                        scores(b, h)

                def run(b, more):
                    for h in range(HS):
                        if h + AHEAD < HS:
                            scores(b, h + AHEAD)
                        turn(b, h)
                        if h:
                            values(b, h - 1)
                    values(b, HS - 1)
                    if more:
                        pe.wait_ge(s_read, (b + 1) * HS)
                        project(b + 1)
                        first_scores(b + 1)
                    pe.wait_ge(o_ready, b + 2)
                    pe.wait_ge(added, b + 1)
                    for t in range(QT):
                        for k in range(KD):
                            nc.tensor.matmul(pend[:, t * D:(t + 1) * D], oT[:, k, t * P:(t + 1) * P], wts["wo"][:, k, :],
                                             start=(k == 0), stop=False)
                        last = nc.tensor.matmul(pend[:, t * D:(t + 1) * D], ones[0:1, :], bo[:, :],
                                                start=False, stop=True)
                    last.then_inc(out_done, 1)

                pe.wait_ge(w_in, 16 * 9)
                project(0)
                first_scores(0)
                batches(pe, run)

            @block.scalar
            def _(act):
                def load_qk(b):
                    act.wait_ge(k_done, b + 1)
                    for h in range(HC):
                        last = nc.scalar.activation(kT[:, h, :], ring[1][:, 0:SEQ], ACT.Identity,
                                                    bias=bkh[:, h:h + 1], scale=heads[:, h:h + 1])
                    last.then_inc(k0_ready, 1)
                    act.wait_ge(q_done, b + 1)
                    for c in range(KD):
                        last = nc.scalar.activation(qT[:, c, :], ring[0][:, c * SEQ:(c + 1) * SEQ],
                                                    ACT.Identity, bias=bq[:, c:c + 1])
                    last.then_inc(q_ready, 1)

                def exps(b, h):
                    act.wait_ge(max_ready, b * HS + (h + 1))
                    for t, (lo, hi) in enumerate(spans):
                        last = nc.scalar.activation(s[:, h % SLOTS, lo:hi], s[:, h % SLOTS, lo:hi], ACT.Exp,
                                                    bias=nmax[:, h % SLOTS, t:t + 1], accum_out=rsum[:, h, t:t + 1])
                    last.then_inc(exp_ready, 1)

                def run(b, more):
                    for h in range(AHEAD):
                        exps(b, h)
                    for h in range(HS):
                        if h % 2 == 0:
                            act.wait_ge(turned, b * HS + (h + 1 + SLOTS))
                            nc.scalar.activation(pT[0][:, :], ppT[0][:, 0:SC], ACT.Copy).then_inc(even_copied, 1)
                        if h + AHEAD < HS:
                            exps(b, h + AHEAD)
                    if more:
                        load_qk(b + 1)

                act.sem_inc(even_copied, 1)
                act.wait_ge(bkh_ready, KD)
                load_qk(0)
                batches(act, run)

            @block.vector
            def _(dve):
                def load_kv(b):
                    dve.wait_ge(k_done, b + 1)
                    for h in range(HC, HS):
                        last = nc.vector.tensor_scalar(kT[:, h, :], ring[2][:, 0:SEQ], heads[:, h - HC:h - HC + 1],
                                                       bkh[:, h:h + 1], ALU.mult, ALU.add)
                    last.then_inc(k1_ready, 1)
                    dve.wait_ge(v_done, b + 1)
                    nc.vector.tensor_copy(v[:, :, :].rearrange("p a (j s) -> p a j s", j=HC)[:, :, :, 0:DH],
                                          ring[3][:, :].rearrange("p (a j d) -> p a j d", j=HC, d=DH)
                                          ).then_inc(v_ready, 1)

                def maxima(b, h):
                    dve.wait_ge(turned, b * HS + (h + 1))
                    dve.wait_ge(s_done, b * HS + (h + 1))
                    nc.vector.scalar_tensor_tensor(out=s[:, h % SLOTS, :], in0=ring[h % 4][:, 0:SC], scalar=scale,
                                                   in1=cmask[:, :], op0=ALU.mult, op1=ALU.add).then_inc(s_read, 1)
                    dve.wait_ge(s_read, b * HS + (h + 1))
                    for t, (lo, hi) in enumerate(spans):
                        last = nc.vector.tensor_reduce(nmax[:, h % SLOTS, t:t + 1], s[:, h % SLOTS, lo:hi], AX_X,
                                                       ALU.max, negate=True)
                    last.then_inc(max_ready, 1)

                def inverse(b, h):
                    dve.wait_ge(exp_ready, b * HS + (h + 1))
                    nc.vector.reciprocal(rinv[:, h, :], rsum[:, h, :]).then_inc(inv_ready, 1)

                def run(b, more):
                    for h in range(HS):
                        if h % 2:
                            dve.wait_ge(turned, b * HS + (h + 1 + SLOTS))
                            nc.vector.tensor_copy(pT[1][:, :], ppT[1][:, 0:SC]).then_inc(odd_copied, 1)
                        if h + AHEAD < HS:
                            maxima(b, h + AHEAD)
                        if h + SUMS_AHEAD < HS:
                            inverse(b, h + SUMS_AHEAD)
                    dve.wait_ge(pv_done, b + 1)
                    nc.vector.tensor_copy(oT[:, :, :], pv[:, :, :]).then_inc(o_ready, 1)
                    if more:
                        load_kv(b + 1)
                        for h in range(AHEAD):
                            maxima(b + 1, h)
                        for h in range(SUMS_AHEAD):
                            inverse(b + 1, h)
                    dve.wait_ge(out_done, b + 1)
                    nc.vector.tensor_tensor(const["x"][:, bass.ds(2 * b, QT), :], const["x"][:, bass.ds(2 * b, QT), :],
                                            pend[:, :].rearrange("p (t d) -> p t d", t=QT), ALU.add).then_inc(added, 1)

                dve.sem_inc(odd_copied, 1)
                dve.sem_inc(o_ready, 1)
                dve.sem_inc(added, 1)
                dve.sem_inc(turned, SLOTS)
                nc.vector.memset(v[:, :, :], 0.0).then_inc(v_zeroed, 1)
                dve.wait_ge(w_in, 16 * 9)
                for c in range(KD):
                    nc.vector.tensor_scalar(bkh[:, c * HC:(c + 1) * HC], heads[:, :], bk[:, c:c + 1], None,
                                            ALU.mult).then_inc(bkh_ready, 1)
                dve.wait_ge(bkh_ready, KD)
                dve.wait_ge(v_zeroed, 1)
                load_kv(0)
                for h in range(AHEAD):
                    maxima(0, h)
                for h in range(SUMS_AHEAD):
                    inverse(0, h)
                batches(dve, run)


HL = 2
EL = D // HL


def linear_attention(nc, name, const, xT, w, o):
    with ExitStack() as ctx:
        sp = Space(nc, ctx, name)
        wts = {n: sp.sb(n, [P, KD, D]) for n in ("wq", "wk", "wv")}
        cm = sp.sb("cm", [P, SC])
        xb = sp.sb("xb", [P, KD, SEQ])
        v = sp.sb("v", [P, QT, D])
        q = sp.sb("q", [P, HL, SEQ])
        k = sp.sb("k", [P, HL, SEQ])
        f = sp.sb("f", [P, HL, SEQ])
        a = sp.sb("a", [P, HL, SEQ])
        up = sp.sb("up", [P, HL, SEQ])
        down = sp.sb("down", [P, HL, SEQ])
        nmid = sp.sb("nmid", [P, HL, QT])
        edge = sp.sb("edge", [P, HL, 2])
        qx = sp.sb("qx", [P, HL, P])
        kx = sp.sb("kx", [P, HL, P])
        sT = sp.sb("sT", [P, HL, SC])
        pq = sp.ps("pq", [P, HL, SEQ])
        pk = sp.ps("pk", [P, HL, SEQ])
        pv = sp.ps("pv", [P, QT, D])
        psT = [sp.ps(f"psT{h}", [P, 512]) for h in range(HL)]
        po = sp.ps("po", [P, QT, D])
        w_in = sp.sem("w_in")
        xb_ready = sp.sem("xb_ready")
        q_done = sp.sem("q_done")
        k_done = sp.sem("k_done")
        v_done = sp.sem("v_done")
        v_ready = sp.sem("v_ready")
        act_done = sp.sem("act_done")
        gate_ready = sp.sem("gate_ready")
        chain = sp.sem("chain")
        dve_done = sp.sem("dve_done")
        scores_done = sp.sem("scores_done")
        scores_ready = sp.sem("scores_ready")
        o_done = sp.sem("o_done")
        o_ready = sp.sem("o_ready")
        NCHAIN = 11
        ones = const["ones"]
        tiles = [(h, t) for h in range(HL) for t in range(QT)]

        with nc.Block() as block:
            @block.sync
            def _(sync):
                for n in ("wq", "wk", "wv"):
                    sync.dma_start(wts[n][:, :, :], w[n]).then_inc(w_in, 16)
                sync.dma_start(cm[:, :], const["cmask01T_dram"]).then_inc(w_in, 16)

            @block.gpsimd
            def _(pool):
                with pool.Fori(0, NB) as b:
                    pool.wait_ge(v_done, b + 1)
                    nc.gpsimd.tensor_copy(xb[:, :, :], xT[:, :, bass.ds(b * SEQ, SEQ)]).then_inc(xb_ready, 1)

            @block.tensor
            def _(pe):
                def project_batch(b, first=False):
                    pe.wait_ge(xb_ready, b + 1)
                    if not first:
                        pe.wait_ge(gate_ready, 3 * b - 2)
                    for to, n, done in ((pk, "wk", k_done), (pq, "wq", q_done)):
                        if n == "wq" and not first:
                            pe.wait_ge(chain, NCHAIN * b + (1 - NCHAIN))
                        for h in range(HL):
                            for c in range(KD):
                                last = nc.tensor.matmul(to[:, h, :], wts[n][:, c, h * EL:(h + 1) * EL], xb[:, c, :],
                                                        start=(c == 0), stop=(c == KD - 1))
                        last.then_inc(done, 1)
                    if not first:
                        pe.wait_ge(v_ready, b)
                    for t in range(QT):
                        for c in range(KD):
                            last = nc.tensor.matmul(pv[:, t, :], xb[:, c, t * P:(t + 1) * P], wts["wv"][:, c, :],
                                                    start=(c == 0), stop=(c == KD - 1))
                    last.then_inc(v_done, 1)

                def attend(b):
                    pe.wait_ge(dve_done, b + 1)
                    pe.wait_ge(scores_ready, 2 * b + 1)
                    for h in range(HL):
                        nc.tensor.matmul(psT[h][:, 0:P], k[:, h, 0:P], q[:, h, 0:P], start=True, stop=True)
                        nc.tensor.matmul(psT[h][:, P:2 * P], kx[:, h, :], qx[:, h, :], start=True, stop=True)
                        nc.tensor.matmul(psT[h][:, 2 * P:SC], k[:, h, P:SEQ], q[:, h, P:SEQ],
                                         start=True, stop=True).then_inc(scores_done, 1)
                    pe.wait_ge(v_ready, b + 1)
                    pe.wait_ge(o_ready, b + 1)
                    for h in range(HL):
                        pe.wait_ge(scores_ready, 2 * b + (h + 2))
                        for qt, kt, at in ((0, 0, 0), (1, 0, P), (1, 1, 2 * P)):
                            last = nc.tensor.matmul(po[:, qt, h * EL:(h + 1) * EL], sT[:, h, at:at + P],
                                                    v[:, kt, h * EL:(h + 1) * EL], start=(kt == 0), stop=(kt == qt))
                    last.then_inc(o_done, 1)

                pe.sem_inc(v_done, 1)
                pe.sem_inc(scores_done, 1)
                pe.sem_inc(o_done, 1)
                pe.wait_ge(w_in, 16 * 4)
                project_batch(0, first=True)
                with pe.Fori(1, NB) as b:
                    project_batch(b)
                    attend(b - 1)
                attend(NB - 1)

            @block.scalar
            def _(act):
                with act.Fori(0, NB) as b:
                    act.wait_ge(k_done, b + 1)
                    nc.scalar.activation(f[:, :, :], pk[:, :, :], ACT.Sigmoid).then_inc(gate_ready, 1)
                    act.wait_ge(q_done, b + 1)
                    act.wait_ge(scores_done, 2 * b + 1)
                    nc.scalar.activation(q[:, :, :], pq[:, :, :], ACT.Sigmoid).then_inc(act_done, 1)
                    act.wait_ge(gate_ready, 3 * b + 1)
                    nc.scalar.activation(k[:, :, :], f[:, :, :], ACT.Sigmoid).then_inc(gate_ready, 1)
                    act.wait_ge(gate_ready, 3 * b + 2)
                    nc.scalar.activation(f[:, :, :], k[:, :, :], ACT.Ln).then_inc(gate_ready, 1)
                    act.wait_ge(v_done, b + 2)
                    act.wait_ge(o_done, b + 1)
                    nc.scalar.activation(v[:, :, :], pv[:, :, :], ACT.Copy).then_inc(v_ready, 1)
                    act.wait_ge(chain, b * NCHAIN + 6)
                    for h, t in tiles:
                        nc.scalar.activation(up[:, h, t * P:(t + 1) * P], a[:, h, t * P:(t + 1) * P], ACT.Exp,
                                             bias=nmid[:, h, t:t + 1])
                        last = nc.scalar.activation(down[:, h, t * P:(t + 1) * P], a[:, h, t * P:(t + 1) * P], ACT.Exp,
                                                    bias=a[:, h, t * P + P // 2 - 1:t * P + P // 2], scale=-1.0)
                    last.then_inc(act_done, 1)
                    for h in range(HL):
                        nc.scalar.activation(edge[:, h, 0:1], a[:, h, P + P // 2 - 1:P + P // 2], ACT.Exp)
                        last = nc.scalar.activation(edge[:, h, 1:2], a[:, h, P - 1:P], ACT.Exp, bias=nmid[:, h, 0:1])
                    last.then_inc(act_done, 1)

            @block.vector
            def _(dve):
                NA = 3
                dve.sem_inc(scores_ready, 1)
                dve.sem_inc(o_ready, 1)
                with dve.Fori(0, NB) as b:
                    ch = Chain(dve, chain, b * NCHAIN)
                    dve.wait_ge(act_done, b * NA + 1)
                    ch.link(nc.vector.tensor_tensor(q[:, :, :], q[:, :, :], pq[:, :, :], ALU.mult))
                    dve.wait_ge(gate_ready, 3 * b + 3)
                    for h, t in tiles:
                        sl = slice(t * P, (t + 1) * P)
                        ch.link(nc.vector.tensor_tensor_scan(a[:, h, sl], ones[:, :], f[:, h, sl], 0.0, ALU.mult, ALU.add))
                    ch.link(nc.vector.tensor_scalar(nmid[:, :, :], a[:, :, :].rearrange("p h (t c) -> p h t c", t=QT)
                                                    [:, :, :, P // 2 - 1], -1.0, None, ALU.mult))
                    ch.link(nc.vector.tensor_scalar(k[:, :, :], k[:, :, :], -1.0, 1.0, ALU.mult, ALU.add))
                    dve.wait_ge(act_done, b * NA + 2)
                    ch.link(nc.vector.tensor_tensor(q[:, :, :], q[:, :, :], up[:, :, :], ALU.mult))
                    ch.link(nc.vector.tensor_tensor(k[:, :, :], k[:, :, :], down[:, :, :], ALU.mult))
                    dve.wait_ge(act_done, b * NA + 3)
                    for h in range(HL):
                        nc.vector.tensor_scalar(qx[:, h, :], q[:, h, P:SEQ], edge[:, h, 0:1], None, ALU.mult)
                        last = nc.vector.tensor_scalar(kx[:, h, :], k[:, h, 0:P], edge[:, h, 1:2], None, ALU.mult)
                        if h == 0:
                            ch.link(last)
                    ch.link(last)
                    dve.sem_inc(dve_done, 1)
                    assert ch.count == NCHAIN, ch.count
                    for h in range(HL):
                        dve.wait_ge(scores_done, 2 * b + (h + 2))
                        nc.vector.tensor_tensor(sT[:, h, :], psT[h][:, 0:SC], cm[:, :], ALU.mult).then_inc(scores_ready, 1)
                    dve.wait_ge(o_done, b + 2)
                    nc.vector.tensor_copy(o[:, bass.ds(2 * b, QT), :], po[:, :, :]).then_inc(o_ready, 1)


def project(nc, name, const, xT, w_dram):
    with ExitStack() as ctx:
        sp = Space(nc, ctx, name)
        w = sp.sb("w", [P, KD, D])
        po = [sp.ps(f"po{i}", [P, 2, D]) for i in range(4)]
        w_in = sp.sem("w_in")
        done = sp.sem("done")
        added = sp.sem("added")
        with nc.Block() as block:
            @block.sync
            def _(sync):
                sync.dma_start(w[:, :, :], w_dram).then_inc(w_in, 16)

            @block.tensor
            def _(pe):
                pe.wait_ge(w_in, 16)
                for i in range(NT // 2):
                    if i >= 4:
                        pe.wait_ge(added, i - 3)
                    for t in (2 * i, 2 * i + 1):
                        for k in range(KD):
                            last = nc.tensor.matmul(po[i % 4][:, t % 2, :], xT[:, k, t * P:(t + 1) * P], w[:, k, :],
                                                    start=(k == 0), stop=(k == KD - 1))
                    last.then_inc(done, 1)

            @block.vector
            def _(dve):
                for i in range(NT // 2):
                    dve.wait_ge(done, i + 1)
                    nc.vector.tensor_tensor(const["x"][:, 2 * i:2 * i + 2, :], const["x"][:, 2 * i:2 * i + 2, :],
                                            po[i % 4][:, :, :], ALU.add).then_inc(added, 1)


HQ = 16
HKV = 4
GQ = HQ // HKV
HB = GQ + 1
EH = 128
NBLK = 2 * HB * QT
NTT = NBLK // 4


def attention_mixed(nc, name, const, xT, w):
    scale = float(EH) ** -0.5
    with ExitStack() as ctx:
        sp = Space(nc, ctx, name)
        wq = sp.sb("wq", [P, KD, HKV, GQ * EH])
        wk = sp.sb("wk", [P, KD, HKV * EH])
        wv = sp.sb("wv", [P, KD, HKV * EH])
        wo = sp.sb("wo", [P, HQ, D])
        cos = sp.sb("cos", [P, QT, EH])
        sin = sp.sb("sin", [P, QT, EH])
        decay = sp.sb("decay", [P, QT, P])
        xb = sp.sb("xb", [P, KD, SEQ])
        qk = sp.sb("qk", [P, QT, HB, EH])
        e = sp.sb("e", [P, QT, HB, EH])
        rcos = sp.sb("rcos", [P, QT, HB, EH])
        rsin = sp.sb("rsin", [P, QT, HB, EH])
        src = sp.sb("src", [P, 2, QT, HB, EH])
        tt = sp.sb("tt", [P, 2, HB, QT, P])
        keys = sp.sb("keys", [P, QT, HKV, EH])
        gate = sp.sb("gate", [P, QT, HKV, EH])
        up = sp.sb("up", [P, QT, HKV, EH])
        down = sp.sb("down", [P, QT, HKV, EH])
        v = sp.sb("v", [P, QT, EH])
        top = sp.sb("top", [P, QT * HB])
        total = sp.sb("total", [P, QT * HB])
        inv_next = sp.sb("inv_next", [P, QT * HB])
        inv = sp.sb("inv", [P, QT * HB])
        s = [sp.sb(f"s{i}", [P, SC]) for i in range(GQ)]
        g = [sp.sb(f"g{i}", [P, SC]) for i in range(GQ)]
        nmax = [sp.sb(f"nmax{i}", [P, QT]) for i in range(GQ)]
        rsum = [sp.sb(f"rsum{i}", [P, QT]) for i in range(GQ)]
        rinv = [sp.sb(f"rinv{i}", [P, QT]) for i in range(GQ)]
        pT = [sp.sb(f"pT{i}", [P, SC]) for i in range(2)]
        oT = [sp.sb(f"oT{i}", [P, SEQ]) for i in range(2)]
        pq = [sp.ps(f"pq{i}", [P, 512]) for i in range(2)]
        pv = sp.ps("pv", [P, QT, EH])
        po = sp.ps("po", [P, SEQ])
        pS = sp.ps("pS", [P, 512])
        pG = sp.ps("pG", [P, 512])
        ppT = sp.ps("ppT", [P, 512])
        pout = sp.ps("pout", [P, QT, D])
        turn_banks = (pq[0], pq[1], pS, pG)
        w_in = sp.sem("w_in")
        xb_ready = sp.sem("xb_ready")
        k_done = sp.sem("k_done")
        v_done = sp.sem("v_done")
        q_done = sp.sem("q_done")
        gate_exp = sp.sem("gate_exp")
        gate_ready = sp.sem("gate_ready")
        decay_done = sp.sem("decay_done")
        decay_ready = sp.sem("decay_ready")
        qk_ready = sp.sem("qk_ready")
        rotated = sp.sem("rotated")
        pool_chain = sp.sem("pool_chain")
        top_ready = sp.sem("top_ready")
        sub_ready = sp.sem("sub_ready")
        e_ready = sp.sem("e_ready")
        total_ready = sp.sem("total_ready")
        inv_ready = sp.sem("inv_ready")
        prepared = sp.sem("prepared")
        tt_done = sp.sem("tt_done")
        tt_even_read = sp.sem("tt_even_read")
        tt_odd_read = sp.sem("tt_odd_read")
        v_ready = sp.sem("v_ready")
        s_done = sp.sem("s_done")
        s_read = sp.sem("s_read")
        g_done = sp.sem("g_done")
        g_read = sp.sem("g_read")
        max_ready = sp.sem("max_ready")
        exp_ready = sp.sem("exp_ready")
        rinv_ready = sp.sem("rinv_ready")
        p_ready = sp.sem("p_ready")
        pT_done = sp.sem("pT_done")
        pT_read = sp.sem("pT_read")
        oT_done = sp.sem("oT_done")
        oT_read = sp.sem("oT_read")
        out_done = sp.sem("out_done")
        added = sp.sem("added")
        inv_moved = sp.sem("inv_moved")
        ident = const["ident"]
        flat = tt[:, :, :, :, :].rearrange("p a h t c -> p (a h t) c")
        spans = ((0, P), (P, SC))

        def steps(eng, run):
            with eng.Fori(0, NB - 1) as b:
                for gr in range(HKV):
                    i = b * HKV + gr
                    nxt = (i + 1, b, gr + 1) if gr + 1 < HKV else (b * HKV + HKV, b + 1, 0)
                    run(i, b, gr, nxt)
            for gr in range(HKV):
                i = (NB - 1) * HKV + gr
                run(i, NB - 1, gr, (i + 1, NB - 1, gr + 1) if gr + 1 < HKV else None)

        with nc.Block() as block:
            @block.sync
            def _(sync):
                sync.dma_start(wk[:, :, :], w["wk"]).then_inc(w_in, 16)
                sync.dma_start(wv[:, :, :], w["wv"]).then_inc(w_in, 16)
                sync.dma_start(wq[:, :, :, :], w["wq"]).then_inc(w_in, 16)
                for to, n in ((cos, "cos"), (sin, "sin"), (decay, "decay"), (wo, "wo")):
                    sync.dma_start(to[:, :, :], w[n]).then_inc(w_in, 16)

            @block.gpsimd
            def _(pool):
                def load(b):
                    nc.gpsimd.tensor_copy(xb[:, :, :], xT[:, :, bass.ds(b * SEQ, SEQ)]).then_inc(xb_ready, 1)

                def rotate(n):
                    pool.wait_ge(qk_ready, n + 1)
                    wide = [P, QT, HB, EH]
                    half = [P, QT, HB, EH // 2]
                    nc.gpsimd.tensor_tensor(rcos[:, :, :, :], qk[:, :, :, :],
                                            cos[:, :, :].unsqueeze(2).broadcast_to(wide), ALU.mult).then_inc(pool_chain, 1)
                    nc.gpsimd.tensor_tensor(rsin[:, :, :, 0:EH // 2], qk[:, :, :, EH // 2:EH],
                                            sin[:, :, 0:EH // 2].unsqueeze(2).broadcast_to(half),
                                            ALU.mult).then_inc(pool_chain, 1)
                    nc.gpsimd.tensor_tensor(rsin[:, :, :, EH // 2:EH], qk[:, :, :, 0:EH // 2],
                                            sin[:, :, EH // 2:EH].unsqueeze(2).broadcast_to(half),
                                            ALU.mult).then_inc(pool_chain, 1)
                    pool.wait_ge(pool_chain, 3 * n + 3)
                    nc.gpsimd.tensor_tensor(src[:, 0, :, :, :], rcos[:, :, :, :], rsin[:, :, :, :],
                                            ALU.add).then_inc(rotated, 1)

                pool.wait_ge(w_in, 16 * 7)
                nc.gpsimd.tensor_copy(xb[:, :, :], xT[:, :, 0:SEQ]).then_inc(xb_ready, 1)
                rotate(0)

                def run(i, b, gr, nxt):
                    if nxt:
                        if gr == HKV - 1:
                            pool.wait_ge(v_done, i + 1)
                            load(nxt[1])
                        rotate(nxt[0])

                steps(pool, run)

            @block.tensor
            def _(pe):
                def project_keys(n, b):
                    pe.wait_ge(xb_ready, b + 1)
                    pe.wait_ge(tt_even_read, n * 3 + 1)
                    pe.wait_ge(tt_odd_read, n * 2 + 1)
                    for t in range(QT):
                        for k in range(KD):
                            last = nc.tensor.matmul(pq[t][:, :], xb[:, k, t * P:(t + 1) * P], wk[:, k, :],
                                                    start=(k == 0), stop=(k == KD - 1))
                    last.then_inc(k_done, 1)

                def decays(b):
                    pe.wait_ge(gate_ready, b + 1)
                    for t in range(QT):
                        last = nc.tensor.matmul(pq[t][:, :], decay[:, t, :], gate[:, t, :, :], start=True, stop=True)
                    last.then_inc(decay_done, 1)

                def project(n, b, gr):
                    pe.wait_ge(tt_even_read, n * 3 + 1)
                    pe.wait_ge(tt_odd_read, n * 2 + 1)
                    if gr == 0:
                        pe.wait_ge(decay_ready, b + 1)
                    project_tile(gr, 0)

                def project_tile(gr, t):
                    for k in range(KD):
                        last = nc.tensor.matmul(pq[t][:, :], xb[:, k, t * P:(t + 1) * P], wq[:, k, gr, :],
                                                start=(k == 0), stop=(k == KD - 1))
                    last.then_inc(q_done, 1)

                def project_rest(n, gr):
                    project_tile(gr, 1)
                    pe.wait_ge(v_ready, n + 1)
                    for t in range(QT):
                        for k in range(KD):
                            last = nc.tensor.matmul(pv[:, t, :], xb[:, k, t * P:(t + 1) * P], wv[:, k, gr * EH:(gr + 1) * EH],
                                                    start=(k == 0), stop=(k == KD - 1))
                    last.then_inc(v_done, 1)

                def turn(n):
                    pe.wait_ge(prepared, n + 1)
                    for m in range(NTT):
                        if m == 4:
                            pe.wait_ge(tt_even_read, n * 3 + 2)
                        for c in range(4):
                            blk = 4 * m + c
                            kind, h, t = blk // (HB * QT), blk // QT % HB, blk % QT
                            last = nc.tensor.transpose(turn_banks[m % 4][:, c * P:(c + 1) * P], src[:, kind, t, h, :],
                                                       ident[:, :])
                        last.then_inc(tt_done, 1)

                def scores(i, h):
                    for kind, bank, read, done in ((0, pS, s_read, s_done), (1, pG, g_read, g_done)):
                        pe.wait_ge(read, i * GQ + (h + 1))
                        nc.tensor.matmul(bank[:, 0:P], tt[:, kind, h, 0, :], tt[:, kind, GQ, 0, :], start=True, stop=True)
                        nc.tensor.matmul(bank[:, P:SC], tt[:, kind, h, 1, :], tt[:, kind, GQ, :, :],
                                         start=True, stop=True).then_inc(done, 1)

                def turn_p(i, h):
                    pe.wait_ge(p_ready, i * GQ + (h + 1))
                    pe.wait_ge(pT_read, i * GQ + (h + 1))
                    for c in range(3):
                        last = nc.tensor.transpose(ppT[:, c * P:(c + 1) * P], s[h][:, c * P:(c + 1) * P], ident[:, :])
                    last.then_inc(pT_done, 1)

                def values(i, h):
                    pe.wait_ge(pT_read, i * GQ + (h + 2))
                    pe.wait_ge(oT_read, i * GQ + (h + 1))
                    nc.tensor.matmul(po[:, :], v[:, 0, :], pT[h % 2][:, 0:SEQ], start=True, stop=False,
                                     skip_group_check=True)
                    nc.tensor.matmul(po[:, P:SEQ], v[:, 1, :], pT[h % 2][:, SEQ:SC], start=False, stop=True,
                                     skip_group_check=True).then_inc(oT_done, 1)

                def output(i, gr, h):
                    pe.wait_ge(oT_read, i * GQ + (h + 2))
                    if h == 0:
                        pe.wait_ge(added, i + 1)
                    for t in range(QT):
                        last = nc.tensor.matmul(pout[:, t, :], oT[h % 2][:, t * P:(t + 1) * P], wo[:, gr * GQ + h, :],
                                                start=(h == 0 and t == 0), stop=(h == GQ - 1), skip_group_check=True)
                    if h == GQ - 1:
                        last.then_inc(out_done, 1)

                def run(i, b, gr, nxt):
                    new_batch = nxt and nxt[2] == 0
                    if new_batch:
                        project_keys(nxt[0], nxt[1])
                    pe.wait_ge(tt_even_read, i * 3 + 4)
                    pe.wait_ge(tt_odd_read, i * 2 + 3)
                    pe.wait_ge(v_ready, i + 2)
                    scores(i, 0)
                    if nxt and not new_batch:
                        project(*nxt)
                    scores(i, 1)
                    if nxt and not new_batch:
                        project_rest(nxt[0], nxt[2])
                    scores(i, 2)
                    turn_p(i, 0)
                    if new_batch:
                        decays(nxt[1])
                    scores(i, 3)
                    values(i, 0)
                    turn_p(i, 1)
                    output(i, gr, 0)
                    values(i, 1)
                    if new_batch:
                        project(*nxt)
                        project_rest(nxt[0], nxt[2])
                    turn_p(i, 2)
                    output(i, gr, 1)
                    values(i, 2)
                    turn_p(i, 3)
                    output(i, gr, 2)
                    values(i, 3)
                    output(i, gr, 3)
                    if nxt:
                        turn(nxt[0])

                pe.wait_ge(w_in, 16 * 7)
                project_keys(0, 0)
                decays(0)
                project(0, 0, 0)
                project_rest(0, 0)
                turn(0)
                steps(pe, run)

            @block.scalar
            def _(act):
                act.sem_inc(tt_even_read, 1)
                act.sem_inc(v_ready, 1)
                act.sem_inc(pT_read, 1)
                act.sem_inc(oT_read, 1)

                def gates(b):
                    act.wait_ge(k_done, b + 1)
                    for t in range(QT):
                        nc.scalar.activation(gate[:, t, :, :], pq[t][:, :].rearrange("p (h e) -> p h e", h=HKV), ACT.Exp,
                                             scale=-1.0)
                        last = nc.scalar.activation(keys[:, t, :, :], pq[t][:, :].rearrange("p (h e) -> p h e", h=HKV),
                                                    ACT.Copy)
                    last.then_inc(gate_exp, 1)
                    act.wait_ge(gate_exp, b + 1)
                    nc.scalar.activation(gate[:, :, :, :], gate[:, :, :, :], ACT.Ln, bias=1.0).then_inc(gate_ready, 1)

                def decay_exps(b):
                    act.wait_ge(decay_done, b + 1)
                    for t in range(QT):
                        pd = pq[t][:, :].rearrange("p (h e) -> p h e", h=HKV)
                        nc.scalar.activation(up[:, t, :, :], pd, ACT.Exp)
                        last = nc.scalar.activation(down[:, t, :, :], pd, ACT.Exp, scale=-1.0)
                    last.then_inc(decay_ready, 1)

                def gather_qk(n, gr):
                    nc.scalar.activation(qk[:, :, GQ, :], keys[:, :, gr, :], ACT.Copy)
                    for t in range(QT):
                        act.wait_ge(q_done, n * QT + (t + 1))
                        last = nc.scalar.activation(qk[:, t, 0:GQ, :], pq[t][:, :].rearrange("p (h e) -> p h e", h=GQ),
                                                    ACT.Copy)
                    last.then_inc(qk_ready, 1)

                def softmax_exps(n):
                    act.wait_ge(sub_ready, n + 1)
                    nc.scalar.activation(e[:, :, :, :], e[:, :, :, :], ACT.Exp).then_inc(e_ready, 1)

                def copies(n):
                    for m in range(0, NTT, 2):
                        act.wait_ge(tt_done, n * NTT + (m + 1))
                        nc.scalar.activation(flat[:, 4 * m:4 * m + 4, :],
                                             turn_banks[m % 4][:, :].rearrange("p (a c) -> p a c", a=4),
                                             ACT.Copy).then_inc(tt_even_read, 1)
                    act.wait_ge(v_done, n + 1)
                    nc.scalar.activation(v[:, :, :], pv[:, :, :], ACT.Copy).then_inc(v_ready, 1)

                def exps(i, h):
                    act.wait_ge(max_ready, i * GQ + (h + 1))
                    for t, (lo, hi) in enumerate(spans):
                        last = nc.scalar.activation(s[h][:, lo:hi], s[h][:, lo:hi], ACT.Exp,
                                                    bias=nmax[h][:, t:t + 1], accum_out=rsum[h][:, t:t + 1])
                    last.then_inc(exp_ready, 1)

                def outs(i, h):
                    act.wait_ge(pT_done, i * GQ + (h + 1))
                    nc.scalar.activation(pT[h % 2][:, :], ppT[:, 0:SC], ACT.Copy).then_inc(pT_read, 1)
                    act.wait_ge(oT_done, i * GQ + (h + 1))
                    nc.scalar.activation(oT[h % 2][:, :], po[:, :], ACT.Copy, scale=0.5).then_inc(oT_read, 1)

                def run(i, b, gr, nxt):
                    new_batch = nxt and nxt[2] == 0
                    exps(i, 0)
                    if new_batch:
                        gates(nxt[1])
                    exps(i, 1)
                    if nxt and not new_batch:
                        gather_qk(nxt[0], nxt[2])
                    exps(i, 2)
                    outs(i, 0)
                    if new_batch:
                        decay_exps(nxt[1])
                    exps(i, 3)
                    outs(i, 1)
                    if new_batch:
                        gather_qk(nxt[0], nxt[2])
                    outs(i, 2)
                    if nxt:
                        softmax_exps(nxt[0])
                    outs(i, 3)
                    if nxt:
                        copies(nxt[0])

                gates(0)
                decay_exps(0)
                gather_qk(0, 0)
                softmax_exps(0)
                copies(0)
                steps(act, run)

            @block.vector
            def _(dve):
                dve.sem_inc(s_read, 1)
                dve.sem_inc(g_read, 1)
                dve.sem_inc(tt_odd_read, 1)
                dve.sem_inc(added, 1)
                nf = "p t h e -> p (t h) e"

                def shift(n):
                    dve.wait_ge(qk_ready, n + 1)
                    nc.vector.tensor_reduce(top[:, :], qk[:, :, :, :].rearrange(nf), AX_X, ALU.max).then_inc(top_ready, 1)
                    dve.wait_ge(top_ready, n + 1)
                    nc.vector.tensor_tensor(e[:, :, :, :].rearrange(nf), qk[:, :, :, :].rearrange(nf),
                                            top[:, :].unsqueeze(2).broadcast_to([P, QT * HB, EH]),
                                            ALU.subtract).then_inc(sub_ready, 1)

                def sums(n):
                    dve.wait_ge(e_ready, n + 1)
                    nc.vector.tensor_reduce(total[:, :], e[:, :, :, :].rearrange(nf), AX_X, ALU.add).then_inc(total_ready, 1)
                    dve.wait_ge(total_ready, n + 1)
                    nc.vector.reciprocal(inv_next[:, :], total[:, :]).then_inc(inv_ready, 1)

                def decay(n, b, gr):
                    dve.wait_ge(inv_ready, n + 1)
                    dve.wait_ge(decay_ready, b + 1)
                    for t in range(QT):
                        nc.vector.scalar_tensor_tensor(out=src[:, 1, t, GQ, :], in0=e[:, t, GQ, :],
                                                       scalar=inv_next[:, t * HB + GQ:t * HB + GQ + 1],
                                                       in1=down[:, t, gr, :], op0=ALU.mult, op1=ALU.mult)
                    nc.vector.tensor_tensor(src[:, 1, :, 0:GQ, :], e[:, :, 0:GQ, :],
                                            up[:, :, gr, :].unsqueeze(2).broadcast_to([P, QT, GQ, EH]), ALU.mult)
                    dve.wait_ge(rotated, n + 1)

                def maxima(i, h):
                    dve.wait_ge(s_done, i * GQ + (h + 1))
                    nc.vector.scalar_tensor_tensor(out=s[h][:, :], in0=pS[:, 0:SC], scalar=scale,
                                                   in1=const["cmask"][:, :], op0=ALU.mult, op1=ALU.add).then_inc(s_read, 1)
                    dve.wait_ge(s_read, i * GQ + (h + 2))
                    for t, (lo, hi) in enumerate(spans):
                        last = nc.vector.tensor_reduce(nmax[h][:, t:t + 1], s[h][:, lo:hi], AX_X, ALU.max,
                                                       negate=True)
                    last.then_inc(max_ready, 1)
                    dve.wait_ge(g_done, i * GQ + (h + 1))
                    for t, (lo, hi) in enumerate(spans):
                        last = nc.vector.scalar_tensor_tensor(out=g[h][:, lo:hi], in0=pG[:, lo:hi],
                                                              scalar=inv[:, t * HB + h:t * HB + h + 1],
                                                              in1=const["cmask01"][:, lo:hi], op0=ALU.mult, op1=ALU.mult)
                    last.then_inc(g_read, 1)

                def join(i, h):
                    dve.wait_ge(exp_ready, i * GQ + (h + 1))
                    nc.vector.reciprocal(rinv[h][:, :], rsum[h][:, :]).then_inc(rinv_ready, 1)
                    dve.wait_ge(rinv_ready, i * GQ + (h + 1))
                    dve.wait_ge(g_read, i * GQ + (h + 2))
                    for t, (lo, hi) in enumerate(spans):
                        last = nc.vector.scalar_tensor_tensor(out=s[h][:, lo:hi], in0=s[h][:, lo:hi],
                                                              scalar=rinv[h][:, t:t + 1], in1=g[h][:, lo:hi],
                                                              op0=ALU.mult, op1=ALU.add)
                    last.then_inc(p_ready, 1)

                def finish_prepare(n):
                    nc.vector.tensor_copy(inv[:, :], inv_next[:, :]).then_inc(prepared, 1)
                    for m in range(1, NTT, 2):
                        dve.wait_ge(tt_done, n * NTT + (m + 1))
                        nc.vector.tensor_copy(flat[:, 4 * m:4 * m + 4, :],
                                              turn_banks[m % 4][:, :].rearrange("p (a c) -> p a c", a=4)
                                              ).then_inc(tt_odd_read, 1)

                def run(i, b, gr, nxt):
                    new_batch = nxt and nxt[2] == 0
                    dve.wait_ge(prepared, i + 1)
                    maxima(i, 0)
                    maxima(i, 1)
                    join(i, 0)
                    maxima(i, 2)
                    join(i, 1)
                    maxima(i, 3)
                    join(i, 2)
                    if nxt and not new_batch:
                        shift(nxt[0])
                    join(i, 3)
                    if new_batch:
                        shift(nxt[0])
                    if nxt:
                        sums(nxt[0])
                    if nxt:
                        decay(*nxt)
                        finish_prepare(nxt[0])
                    dve.wait_ge(out_done, i + 1)
                    nc.vector.tensor_tensor(const["x"][:, bass.ds(2 * b, QT), :], const["x"][:, bass.ds(2 * b, QT), :],
                                            pout[:, :, :], ALU.add).then_inc(added, 1)

                shift(0)
                sums(0)
                decay(0, 0, 0)
                finish_prepare(0)
                steps(dve, run)


def program(nc, a, out):
    with ExitStack() as ctx:
        sp = Space(nc, ctx, "all")
        const = {"x": sp.sb("x", [P, NT, D])}
        for c in CONSTS:
            const[c] = sp.sb(c, list(a[c].shape))
            const[c + "_dram"] = a[c]
        const["cmask01T_dram"] = a["cmask01T"]
        const["order_dram"] = a["order"]
        xn = sp.sb("xn", [P, NT, D])
        xT = sp.sb("xT", [P, KD, TOK])
        setup(nc, a["X"], const)
        normalize(nc, "n0", const["x"], const, xn, xT, 1e-5, False)
        attention_small(nc, "a0", const, xT, {**{k: a["L0_" + k] for k in SMALL}, "heads": a["heads"]}, 0.25)
        with nc.sbuf_tensor("cT0", [PARTS * 17, TOK], BF16) as cT:
            route(nc, "r0", const, xT, a["L0_Wg"], 16, 4, cT, groups=(4, 2), renorm=False)
            gated_ffn(nc, "f0", const, xT, a["L0_bank"], 25, cT=cT)
        normalize(nc, "n1", const["x"], const, xn, xT, 1e-5, False)
        attention_mixed(nc, "a1", const, xT, {k: a["L1_" + k] for k in ("wq", "wk", "wv", "wo", "cos", "sin", "decay")})
        gated_ffn(nc, "f1", const, xT, a["L1_bank"], 8)
        normalize(nc, "n2", const["x"], const, xn, xT, 1e-5, False)
        with nc.sbuf_tensor("o2", [P, NT, D], F32) as o:
            linear_attention(nc, "a2", const, xT, {k: a["L2_" + k] for k in ("wq", "wk", "wv")}, o)
            normalize(nc, "n2o", o, const, o, xT, 1e-6, True, a["L2_attn_norm"])
        project(nc, "p2", const, xT, a["L2_wo"])
        E = 32
        normalize(nc, "n2f", xn, const, xn, xT, 1e-6, True, a["L2_ffn_norm"], add_src=True)
        with (nc.sbuf_tensor("cT2", [PARTS * (E + 1), TOK + E], BF16) as cT, nc.sbuf_tensor("cover2", [E, TOK], F32) as coverT,
              nc.sbuf_tensor("xs2", [P, KD, E], F32) as xsT):
            route(nc, "r2", const, xT, a["L2_gate"], E, 4, cT, cap=2 * TOK * 4 // E,
                  extra=(xn, xsT, coverT, a["L2_ffn_norm"]))
            gated_ffn(nc, "f2", const, xT, a["L2_bank"], 33, cT=cT, extra=(xsT, coverT))
        normalize(nc, "n3", const["x"], const, xn, xT, 1e-5, False)
        attention_small(nc, "a3", const, xT, {**{k: a["L3_" + k] for k in SMALL}, "heads": a["heads"]}, 0.25)
        with (nc.sbuf_tensor("cT3", [PARTS * SEX // 2, 2, TOK], BF16) as cT,
              nc.sbuf_tensor("key3", [P, NT, SEX], F32) as key, nc.sbuf_tensor("keyT3", [SEX, TOK], BF16) as keyT):
            route(nc, "r3", const, xT, a["L3_router"], SEX, 4, cT, bias_dram=a["L3_router_bias"], cap=CAP,
                  slots=(key, keyT))
            slot_ffn(nc, "s3", const, xn, a, a["L3_bank"], key, keyT, cT)
        gated_ffn(nc, "f3", const, xT, a["L3_shared"], 4)
        store(nc, out, const)


def host_layout(inp):
    f = {k: np.asarray(v) for k, v in inp.items()}
    a = {"X": f["L0_attn_X"]}

    def bank(w1, w3, w2, expert_of):
        rows = w1.shape[0]
        n = -(-rows // P)
        E = int(expert_of.max()) + 1
        b = np.zeros((n, P, KD * 2 * P + D + P), np.float32)
        for p in range(n):
            r = slice(p * P, min((p + 1) * P, rows))
            m = r.stop - r.start
            for k in range(KD):
                b[p, :, k * 2 * P:k * 2 * P + m] = w1[r, k * P:(k + 1) * P].T
                b[p, :, k * 2 * P + P:k * 2 * P + P + m] = w3[r, k * P:(k + 1) * P].T
            b[p, :m, KD * 2 * P:KD * 2 * P + D] = w2[r]
            for part in range(PARTS if E > 1 else 0):
                b[p, :, KD * 2 * P + D:][part * E + expert_of[r], np.arange(m)] = 1.0
        return b

    gu = f["L1_ffn_w_gate_up"]
    n = gu.shape[0] // 2
    a["L1_bank"] = bank(gu[:n], gu[n:], f["L1_ffn_w_down"].T, np.zeros(n, np.int64))

    def col(w):
        return w.reshape(KD, P).T

    def chan(w):
        return w.T.reshape(KD, P, -1).transpose(1, 0, 2)

    for l in ("L0_", "L3_"):
        g = l + "attn_"
        for n in "qk":
            a[l + "w" + n] = chan(f[g + "W" + n])
            a[l + "b" + n] = col(f[g + "b" + n])
        for n in "vo":
            a[l + "w" + n] = chan(f[g + "W" + n])
            a[l + "b" + n] = f[g + "b" + n].reshape(1, D)
    a["L0_Wg"] = chan(f["L0_ffn_Wg"])
    E, I = f["L0_ffn_W1"].shape[:2]
    sh = f["L0_ffn_Ws1"].shape[0]
    a["L0_bank"] = bank(np.concatenate([f["L0_ffn_W1"].reshape(E * I, D), f["L0_ffn_Ws1"]]),
                        np.concatenate([f["L0_ffn_W3"].reshape(E * I, D), f["L0_ffn_Ws3"]]),
                        np.concatenate([f["L0_ffn_W2"].transpose(0, 2, 1).reshape(E * I, D), f["L0_ffn_Ws2"].T]),
                        np.concatenate([np.repeat(np.arange(E), I), np.full(sh, E)]))
    def rows(w):
        return w.reshape(KD, P, -1).transpose(1, 0, 2)

    a["L1_wq"] = rows(f["L1_attn_Wq"]).reshape(P, KD, HKV, GQ * EH)
    a["L1_wk"] = rows(f["L1_attn_Wk"])
    a["L1_wv"] = rows(f["L1_attn_Wv"])
    a["L1_wo"] = f["L1_attn_Wo"].reshape(HQ, P, D).transpose(1, 0, 2)
    for n in "qkvo":
        a["L2_w" + n] = chan(f["L2_attn_W" + n])
    a["L2_attn_norm"] = col(f["L2_attn_norm_w"])
    a["L2_gate"] = chan(f["L2_ffn_gate_w"])
    a["L2_ffn_norm"] = col(f["L2_ffn_norm_w"])
    E, I = f["L2_ffn_w2"].shape[:2]
    w13 = f["L2_ffn_w13"].transpose(0, 2, 1)
    a["L2_bank"] = bank(np.concatenate([w13[:, :I].reshape(E * I, D), f["L2_ffn_shared_gate_w"].T]),
                        np.concatenate([w13[:, I:].reshape(E * I, D), f["L2_ffn_shared_up_w"].T]),
                        np.concatenate([f["L2_ffn_w2"].reshape(E * I, D), f["L2_ffn_shared_down_w"]]),
                        np.concatenate([np.repeat(np.arange(E), I), np.full(I, E)]))
    a["L3_router"] = chan(f["L3_ffn_router_w"])
    a["L3_router_bias"] = f["L3_ffn_router_bias"].reshape(1, -1)
    E, I = f["L3_ffn_gate_w"].shape[:2]
    S, SF = f["L3_ffn_sh_gate_w"].shape[:2]
    a["L3_bank"] = bank(f["L3_ffn_gate_w"].reshape(E * I, D), f["L3_ffn_up_w"].reshape(E * I, D),
                        f["L3_ffn_down_w"].transpose(0, 2, 1).reshape(E * I, D), np.zeros(E * I, np.int64))
    a["L3_shared"] = bank(f["L3_ffn_sh_gate_w"].reshape(S * SF, D), f["L3_ffn_sh_up_w"].reshape(S * SF, D),
                          f["L3_ffn_sh_down_w"].transpose(0, 2, 1).reshape(S * SF, D), np.zeros(S * SF, np.int64))

    a["heads"] = np.kron(np.eye(HC, dtype=np.float32), np.ones((DH, 1), np.float32))
    a["order"] = np.tile(np.arange(64, 0, -1, dtype=np.float32), (P, 1))
    a["ident"] = np.eye(P, dtype=np.float32)
    tri = np.tril(np.ones((P, P), np.float32))
    ones = np.ones((P, P), np.float32)
    a["cmask01"] = np.concatenate([tri, ones, tri], 1)
    a["cmask"] = np.where(a["cmask01"] > 0, np.float32(0), np.float32(-BIG)).astype(np.float32)
    a["cmask01T"] = np.concatenate([tri.T, ones, tri.T], 1)
    freq = (1.0 / np.float32(10000.0) ** (np.arange(0, EH, 2, dtype=np.float32) / np.float32(EH))).astype(np.float32)
    angle = (np.arange(SEQ, dtype=np.float32)[:, None] * freq[None, :]).reshape(QT, P, EH // 2).transpose(1, 0, 2)
    c, s = np.cos(angle).astype(np.float32), np.sin(angle).astype(np.float32)
    a["L1_cos"] = np.concatenate([c, c], 2)
    a["L1_sin"] = np.concatenate([-s, s], 2)
    a["L1_decay"] = np.stack([(ones - tri.T) / 16, -tri.T / 16], 1).astype(np.float32)
    a["before"] = ones - tri
    a["slot_ranks"] = np.tile(np.arange(CAP, dtype=np.float32), (P, 1))
    a["slot_rank"] = np.tile(np.arange(CAP, dtype=np.float32), SE).reshape(P, 1)
    sel = np.zeros((SCH, P, 2, P), np.float32)
    expert = np.arange(SCH)[:, None] * SE + np.arange(P)[None, :] // CAP
    q, col = np.arange(SCH)[:, None], np.arange(P)[None, :]
    sel[q, expert, 0, col] = 1.0
    for part in range(PARTS):
        sel[q, part * (SEX // 2) + expert % (SEX // 2), 1, col] = 1.0
    a["slot_spread"] = sel
    a["slot_pair"] = np.kron(np.eye(2, dtype=np.float32), np.ones((P // 2, CAP), np.float32))
    a["ones"] = ones
    return a


def kernel(**inputs):
    import concourse.bacc as _bacc
    from concourse.bass_utils import run_bass_kernel_spmd as _run

    nc = _bacc.Bacc("TRN2", target_bir_lowering=False, num_devices=1)
    a = host_layout(inputs)
    arrays = {f"in_{k}": np.ascontiguousarray(v) for k, v in a.items()}
    args = {k: nc.dram_tensor(f"in_{k}", arrays[f"in_{k}"].shape, F32, kind="ExternalInput").ap() for k in a}
    out = nc.dram_tensor("out_0", (NB, SEQ, D), F32, kind="ExternalOutput").ap()
    program(nc, args, out)
    r = _run(nc, [arrays], core_ids=[0])
    return r.results[0]["out_0"]
```
